# Optimizing a Trainium2 kernel written in Bass

```python
import numpy as np
import jax
import jax.numpy as jnp

def _softmax(x, axis=-1):
    return jax.nn.softmax(x, axis=axis)

def _gelu(x):
    return jax.nn.gelu(x, approximate=True)

def _silu(x):
    return jax.nn.silu(x)

def _sigmoid(x):
    return jax.nn.sigmoid(x)

def _layernorm(x, axis=-1, eps=1e-05):
    m = jnp.mean(x, axis=axis, keepdims=True)
    v = jnp.var(x, axis=axis, keepdims=True)
    return (x - m) / jnp.sqrt(v + eps)

def _scatter_add(tgt, idx, src, axis=0):
    return tgt.at[idx].add(src)

def _segment_sum(src, seg, n):
    return jax.ops.segment_sum(src, seg, n)
kernel_name = 'mk_decoder_postln_d2_seqx_r8_577a51'

def setup_inputs(seed: int=0):
    np.random.seed(seed)
    _w = jnp.asarray

    def _rec_inputs():
        import jax
        import jax.numpy as jnp
        _rk = jax.random.key(seed)
        x = 7.22e-05 + 1 * jax.random.normal(jax.random.fold_in(_rk, 1), (8, 256, 128), jnp.float32)
        _lenS = 256 - jax.random.randint(jax.random.fold_in(_rk, 7), (8,), 0, max(1, 256 // 4) + 1, jnp.int32)
        _lenS2 = 512 - jax.random.randint(jax.random.fold_in(_rk, 8), (8,), 0, max(1, 512 // 4) + 1, jnp.int32)
        _ctx_1024P = jax.random.normal(jax.random.fold_in(_rk, 11), (8, 16, 128), jnp.float32)
        _ctx_1024c = jax.random.dirichlet(jax.random.fold_in(_rk, 511), 0.3 * jnp.ones((16,), jnp.float32), (8, 512))
        _ctx_1024t = jnp.einsum('bsk,bkd->bsd', _ctx_1024c, _ctx_1024P)
        _ctx_1024t = _ctx_1024t * jax.lax.rsqrt(jnp.mean(jnp.square(_ctx_1024t)) + 1e-12) * 0.953939
        ctx_1024 = 0.00191187 + 0.999416 * (_ctx_1024t + 0.3 * jax.random.normal(jax.random.fold_in(_rk, 611), (8, 512, 128), jnp.float32))
        return (x, ctx_1024)
    x, ctx_1024 = _rec_inputs()

    def _L0_attn_setup():
        import jax, jax.numpy as jnp
        import numpy as np
        B, L, SIZE, ATT, LIN = (8, 256, 128, 128, 512)
        EPS = 1e-05

        def layer_norm(x, g, b):
            m = x.mean(-1, keepdims=True)
            v = ((x - m) ** 2).mean(-1, keepdims=True)
            return (x - m) * jax.lax.rsqrt(v + EPS) * g + b

        def time_shift(x):
            return jnp.pad(x, ((0, 0), (1, 0), (0, 0)))[:, :-1]

        def wkv(time_decay, time_first, k, v):
            w = -jnp.exp(time_decay)
            u = time_first

            def step(carry, kv):
                p, q, o = carry
                kt, vt = kv
                no = jnp.maximum(o, u + kt)
                A = jnp.exp(o - no)
                Bc = jnp.exp(u + kt - no)
                out = (A * p + Bc * vt) / (A * q + Bc)
                no2 = jnp.maximum(o + w, kt)
                A2 = jnp.exp(o + w - no2)
                B2 = jnp.exp(kt - no2)
                return ((A2 * p + B2 * vt, A2 * q + B2, no2), out)
            Bn, Ln, D = k.shape
            init = (jnp.zeros((Bn, D), k.dtype), jnp.zeros((Bn, D), k.dtype), jnp.full((Bn, D), -1e+38, k.dtype))
            _, out = jax.lax.scan(step, init, (jnp.moveaxis(k, 1, 0), jnp.moveaxis(v, 1, 0)))
            return jnp.moveaxis(out, 0, 1)
        key = jax.random.key(seed)
        ks = jax.random.split(key, 20)
        n = lambda i, shape, s=1.0: jax.random.normal(ks[i], shape, jnp.float32) * s
        u = lambda i, shape: jax.random.uniform(ks[i], shape, jnp.float32)
        return {'x': n(0, (B, L, SIZE)), 'ln_att_g': jnp.ones((SIZE,), jnp.float32), 'ln_att_b': jnp.zeros((SIZE,), jnp.float32), 'ln_ffn_g': jnp.ones((SIZE,), jnp.float32), 'ln_ffn_b': jnp.zeros((SIZE,), jnp.float32), 'att_time_decay': n(1, (ATT,), 0.5), 'att_time_first': n(2, (ATT,), 0.5), 'att_mix_k': u(3, (SIZE,)), 'att_mix_v': u(4, (SIZE,)), 'att_mix_r': u(5, (SIZE,)), 'att_wk': n(6, (SIZE, ATT), 0.02), 'att_wv': n(7, (SIZE, ATT), 0.02), 'att_wr': n(8, (SIZE, ATT), 0.02), 'att_wo': n(9, (ATT, SIZE), 0.02), 'ffn_mix_k': u(10, (SIZE,)), 'ffn_mix_r': u(11, (SIZE,)), 'ffn_wk': n(12, (SIZE, LIN), 0.02), 'ffn_wv': n(13, (LIN, SIZE), 0.02), 'ffn_wr': n(14, (SIZE, SIZE), 0.02)}
    _L0_attn_all = _L0_attn_setup()
    _L0_attn_in = {k: v for k, v in _L0_attn_all.items() if k in ('ln_att_g', 'ln_att_b', 'ln_ffn_g', 'ln_ffn_b', 'att_time_decay', 'att_time_first', 'att_mix_k', 'att_mix_v', 'att_mix_r', 'att_wk', 'att_wv', 'att_wr', 'att_wo', 'ffn_mix_k', 'ffn_mix_r', 'ffn_wk', 'ffn_wv', 'ffn_wr')}
    del _L0_attn_all

    def _L0_xattn_setup():
        import jax, jax.numpy as jnp
        import numpy as np
        EPS = 1e-06

        def _rmsnorm(x, w, eps=EPS):
            x32 = x.astype(jnp.float32)
            var = jnp.mean(x32 * x32, axis=-1, keepdims=True)
            return (x32 * jax.lax.rsqrt(var + eps)).astype(x.dtype) * w
        key = jax.random.key(seed)
        ks = jax.random.split(key, 6)
        B, S, K, H = (4, 256, 64, 128)
        return {'hidden_states': jax.random.normal(ks[0], (B, S, H), jnp.float32), 'memory_state': jax.random.normal(ks[1], (B, K, H), jnp.float32), 'q_w': jax.random.normal(ks[2], (H, H), jnp.float32) * (1.0 / np.sqrt(H)), 'k_w': jax.random.normal(ks[3], (H, H), jnp.float32) * (1.0 / np.sqrt(H)), 'norm_w': jnp.ones((H,), jnp.float32), 'gate_w': jax.random.normal(ks[4], (H, H), jnp.float32) * 0.02, 'gate_b': jnp.zeros((H,), jnp.float32)}
    _L0_xattn_all = _L0_xattn_setup()
    _L0_xattn_in = {k: v for k, v in _L0_xattn_all.items() if k in ('q_w', 'k_w', 'norm_w', 'gate_w', 'gate_b')}
    del _L0_xattn_all

    def _L0_ffn_setup():
        import jax, jax.numpy as jnp
        import numpy as np
        LN_EPS = 1e-12
        key = jax.random.key(seed)
        ks = jax.random.split(key, 8)
        B, S, H, I, E = (4, 256, 128, 512, 8)
        sH = 1.0 / np.sqrt(H)
        sI = 1.0 / np.sqrt(I)
        return {'hidden_states': jax.random.normal(ks[0], (B, S, H), dtype=jnp.float32), 'Wr': jax.random.uniform(ks[1], (E, H), jnp.float32, -sH, sH), 'W1': jax.random.uniform(ks[2], (E, H, I), jnp.float32, -sH, sH), 'b1': jax.random.uniform(ks[3], (E, I), jnp.float32, -sH, sH), 'Wo': jax.random.uniform(ks[4], (I, H), jnp.float32, -sI, sI), 'bo': jax.random.uniform(ks[5], (H,), jnp.float32, -sI, sI), 'gamma': jnp.ones((H,), jnp.float32), 'beta': jnp.zeros((H,), jnp.float32)}
    _L0_ffn_all = _L0_ffn_setup()
    _L0_ffn_in = {k: v for k, v in _L0_ffn_all.items() if k in ('Wr', 'W1', 'b1', 'Wo', 'bo', 'gamma', 'beta')}
    del _L0_ffn_all

    def _L1_attn_setup():
        import jax, jax.numpy as jnp
        import numpy as np
        import math
        N_HEAD = 16
        STRIDE = 128
        C = 8

        def _sparse_causal_mask(q_len, k_len):
            cols = np.arange(k_len)
            rows = np.arange(k_len)[:, None]
            strided = cols % STRIDE >= STRIDE - C
            local = cols[None, :] // STRIDE == rows // STRIDE
            causal = cols[None, :] <= rows
            layout = (strided[None, :] | local) & causal
            return jnp.asarray(layout[k_len - q_len:])
        key = jax.random.key(seed)
        k1, k2, k3 = jax.random.split(key, 3)
        B, S, E = (2, 256, 128)
        return {'hidden_states': jax.random.normal(k1, (B, S, E), dtype=jnp.float32), 'W_attn': jax.random.normal(k2, (E, 3 * E), dtype=jnp.float32) * 0.02, 'b_attn': jnp.zeros((3 * E,), dtype=jnp.float32), 'W_proj': jax.random.normal(k3, (E, E), dtype=jnp.float32) * 0.02, 'b_proj': jnp.zeros((E,), dtype=jnp.float32)}
    _L1_attn_all = _L1_attn_setup()
    _L1_attn_in = {k: v for k, v in _L1_attn_all.items() if k in ('W_attn', 'b_attn', 'W_proj', 'b_proj')}
    del _L1_attn_all

    def _L1_xattn_setup():
        import jax, jax.numpy as jnp
        import numpy as np
        B, S, D, H, DK = (4, 256, 128, 16, 64)

        def _proj(x, W, b):
            y = jnp.einsum('bsd,ed->bse', x, W) + b
            return y.reshape(x.shape[0], x.shape[1], H, DK).transpose(0, 2, 1, 3)
        key = jax.random.key(seed)
        ks = jax.random.split(key, 10)
        scale = 1.0 / np.sqrt(D)
        return {'input_Q': jax.random.normal(ks[0], (B, S, D), jnp.float32), 'input_K': jax.random.normal(ks[1], (B, S, D), jnp.float32), 'input_V': jax.random.normal(ks[2], (B, S, D), jnp.float32), 'Wq': jax.random.normal(ks[3], (H * DK, D), jnp.float32) * scale, 'bq': jax.random.normal(ks[4], (H * DK,), jnp.float32) * scale, 'Wk': jax.random.normal(ks[5], (H * DK, D), jnp.float32) * scale, 'bk': jax.random.normal(ks[6], (H * DK,), jnp.float32) * scale, 'Wv': jax.random.normal(ks[7], (H * DK, D), jnp.float32) * scale, 'bv': jax.random.normal(ks[8], (H * DK,), jnp.float32) * scale, 'Wo': jax.random.normal(ks[9], (D, H * DK), jnp.float32) * scale}
    _L1_xattn_all = _L1_xattn_setup()
    _L1_xattn_in = {k: v for k, v in _L1_xattn_all.items() if k in ('Wq', 'bq', 'Wk', 'bk', 'Wv', 'bv', 'Wo')}
    del _L1_xattn_all

    def _L1_ffn_setup():
        import jax, jax.numpy as jnp
        import numpy as np
        E = 8
        K = 2
        CAPACITY_FACTOR = 1.25
        key = jax.random.key(seed)
        ks = jax.random.split(key, 4)
        B, T, C, H = (8, 256, 128, 512)
        x = jax.random.normal(ks[0], (B, T, C), jnp.float32)
        Wr = jax.random.normal(ks[1], (C, E), jnp.float32) * 0.02
        br = jnp.zeros((E,), jnp.float32)
        W1 = jax.random.normal(ks[2], (E, C, H), jnp.float32) * 0.02
        b1 = jnp.zeros((E, H), jnp.float32)
        W2 = jax.random.normal(ks[3], (E, H, C), jnp.float32) * 0.02
        b2 = jnp.zeros((E, C), jnp.float32)
        return {'x': x, 'Wr': Wr, 'br': br, 'W1': W1, 'b1': b1, 'W2': W2, 'b2': b2}
    _L1_ffn_all = _L1_ffn_setup()
    _L1_ffn_in = {k: v for k, v in _L1_ffn_all.items() if k in ('Wr', 'br', 'W1', 'b1', 'W2', 'b2')}
    del _L1_ffn_all
    return {'x': x, 'ctx_1024': ctx_1024, 'L0_attn_ln_att_g': _L0_attn_in['ln_att_g'], 'L0_attn_ln_att_b': _L0_attn_in['ln_att_b'], 'L0_attn_ln_ffn_g': _L0_attn_in['ln_ffn_g'], 'L0_attn_ln_ffn_b': _L0_attn_in['ln_ffn_b'], 'L0_attn_att_time_decay': _L0_attn_in['att_time_decay'], 'L0_attn_att_time_first': _L0_attn_in['att_time_first'], 'L0_attn_att_mix_k': _L0_attn_in['att_mix_k'], 'L0_attn_att_mix_v': _L0_attn_in['att_mix_v'], 'L0_attn_att_mix_r': _L0_attn_in['att_mix_r'], 'L0_attn_att_wk': _L0_attn_in['att_wk'], 'L0_attn_att_wv': _L0_attn_in['att_wv'], 'L0_attn_att_wr': _L0_attn_in['att_wr'], 'L0_attn_att_wo': _L0_attn_in['att_wo'], 'L0_attn_ffn_mix_k': _L0_attn_in['ffn_mix_k'], 'L0_attn_ffn_mix_r': _L0_attn_in['ffn_mix_r'], 'L0_attn_ffn_wk': _L0_attn_in['ffn_wk'], 'L0_attn_ffn_wv': _L0_attn_in['ffn_wv'], 'L0_attn_ffn_wr': _L0_attn_in['ffn_wr'], 'L0_xattn_q_w': _L0_xattn_in['q_w'], 'L0_xattn_k_w': _L0_xattn_in['k_w'], 'L0_xattn_norm_w': _L0_xattn_in['norm_w'], 'L0_xattn_gate_w': _L0_xattn_in['gate_w'], 'L0_xattn_gate_b': _L0_xattn_in['gate_b'], 'L0_ffn_Wr': _L0_ffn_in['Wr'], 'L0_ffn_W1': _L0_ffn_in['W1'], 'L0_ffn_b1': _L0_ffn_in['b1'], 'L0_ffn_Wo': _L0_ffn_in['Wo'], 'L0_ffn_bo': _L0_ffn_in['bo'], 'L0_ffn_gamma': _L0_ffn_in['gamma'], 'L0_ffn_beta': _L0_ffn_in['beta'], 'L1_attn_W_attn': _L1_attn_in['W_attn'], 'L1_attn_b_attn': _L1_attn_in['b_attn'], 'L1_attn_W_proj': _L1_attn_in['W_proj'], 'L1_attn_b_proj': _L1_attn_in['b_proj'], 'L1_xattn_Wq': _L1_xattn_in['Wq'], 'L1_xattn_bq': _L1_xattn_in['bq'], 'L1_xattn_Wk': _L1_xattn_in['Wk'], 'L1_xattn_bk': _L1_xattn_in['bk'], 'L1_xattn_Wv': _L1_xattn_in['Wv'], 'L1_xattn_bv': _L1_xattn_in['bv'], 'L1_xattn_Wo': _L1_xattn_in['Wo'], 'L1_ffn_Wr': _L1_ffn_in['Wr'], 'L1_ffn_br': _L1_ffn_in['br'], 'L1_ffn_W1': _L1_ffn_in['W1'], 'L1_ffn_b1': _L1_ffn_in['b1'], 'L1_ffn_W2': _L1_ffn_in['W2'], 'L1_ffn_b2': _L1_ffn_in['b2']}

def reference(x, ctx_1024, L0_attn_ln_att_g, L0_attn_ln_att_b, L0_attn_ln_ffn_g, L0_attn_ln_ffn_b, L0_attn_att_time_decay, L0_attn_att_time_first, L0_attn_att_mix_k, L0_attn_att_mix_v, L0_attn_att_mix_r, L0_attn_att_wk, L0_attn_att_wv, L0_attn_att_wr, L0_attn_att_wo, L0_attn_ffn_mix_k, L0_attn_ffn_mix_r, L0_attn_ffn_wk, L0_attn_ffn_wv, L0_attn_ffn_wr, L0_xattn_q_w, L0_xattn_k_w, L0_xattn_norm_w, L0_xattn_gate_w, L0_xattn_gate_b, L0_ffn_Wr, L0_ffn_W1, L0_ffn_b1, L0_ffn_Wo, L0_ffn_bo, L0_ffn_gamma, L0_ffn_beta, L1_attn_W_attn, L1_attn_b_attn, L1_attn_W_proj, L1_attn_b_proj, L1_xattn_Wq, L1_xattn_bq, L1_xattn_Wk, L1_xattn_bk, L1_xattn_Wv, L1_xattn_bv, L1_xattn_Wo, L1_ffn_Wr, L1_ffn_br, L1_ffn_W1, L1_ffn_b1, L1_ffn_W2, L1_ffn_b2):
    import jax
    import jax.numpy as jnp

    def _L0_attn_ref(x, ln_att_g, ln_att_b, ln_ffn_g, ln_ffn_b, att_time_decay, att_time_first, att_mix_k, att_mix_v, att_mix_r, att_wk, att_wv, att_wr, att_wo, ffn_mix_k, ffn_mix_r, ffn_wk, ffn_wv, ffn_wr):
        import jax, jax.numpy as jnp
        import numpy as np
        B, L, SIZE, ATT, LIN = (8, 256, 128, 128, 512)
        EPS = 1e-05

        def layer_norm(x, g, b):
            m = x.mean(-1, keepdims=True)
            v = ((x - m) ** 2).mean(-1, keepdims=True)
            return (x - m) * jax.lax.rsqrt(v + EPS) * g + b

        def time_shift(x):
            return jnp.pad(x, ((0, 0), (1, 0), (0, 0)))[:, :-1]

        def wkv(time_decay, time_first, k, v):
            w = -jnp.exp(time_decay)
            u = time_first

            def step(carry, kv):
                p, q, o = carry
                kt, vt = kv
                no = jnp.maximum(o, u + kt)
                A = jnp.exp(o - no)
                Bc = jnp.exp(u + kt - no)
                out = (A * p + Bc * vt) / (A * q + Bc)
                no2 = jnp.maximum(o + w, kt)
                A2 = jnp.exp(o + w - no2)
                B2 = jnp.exp(kt - no2)
                return ((A2 * p + B2 * vt, A2 * q + B2, no2), out)
            Bn, Ln, D = k.shape
            init = (jnp.zeros((Bn, D), k.dtype), jnp.zeros((Bn, D), k.dtype), jnp.full((Bn, D), -1e+38, k.dtype))
            _, out = jax.lax.scan(step, init, (jnp.moveaxis(k, 1, 0), jnp.moveaxis(v, 1, 0)))
            return jnp.moveaxis(out, 0, 1)
        h = layer_norm(x, ln_att_g, ln_att_b)
        sx = time_shift(h)
        k = (h * att_mix_k + sx * (1.0 - att_mix_k)) @ att_wk
        v = (h * att_mix_v + sx * (1.0 - att_mix_v)) @ att_wv
        r = jax.nn.sigmoid((h * att_mix_r + sx * (1.0 - att_mix_r)) @ att_wr)
        att = r * wkv(att_time_decay, att_time_first, k, v) @ att_wo
        x = x + att
        h = layer_norm(x, ln_ffn_g, ln_ffn_b)
        sx = time_shift(h)
        kf = jnp.square(jax.nn.relu((h * ffn_mix_k + sx * (1.0 - ffn_mix_k)) @ ffn_wk))
        rf = jax.nn.sigmoid((h * ffn_mix_r + sx * (1.0 - ffn_mix_r)) @ ffn_wr)
        return x + rf * (kf @ ffn_wv)

    def _L0_xattn_ref(hidden_states, memory_state, q_w, k_w, norm_w, gate_w, gate_b):
        import jax, jax.numpy as jnp
        import numpy as np
        EPS = 1e-06

        def _rmsnorm(x, w, eps=EPS):
            x32 = x.astype(jnp.float32)
            var = jnp.mean(x32 * x32, axis=-1, keepdims=True)
            return (x32 * jax.lax.rsqrt(var + eps)).astype(x.dtype) * w
        B, S, H = hidden_states.shape
        K = memory_state.shape[1]
        scale = 1.0 / np.sqrt(H)
        normed = _rmsnorm(hidden_states, norm_w)
        v_pool = jnp.concatenate([normed, memory_state], axis=1)
        q = jnp.einsum('bsh,oh->bso', normed, q_w)
        k = jnp.einsum('bth,oh->bto', v_pool, k_w)
        logits = jnp.einsum('bsd,btd->bst', q, k) * scale
        local = jnp.tril(jnp.ones((S, S), bool))
        mask = jnp.concatenate([local, jnp.ones((S, K), bool)], axis=1)
        logits = jnp.where(mask[None], logits, -jnp.inf)
        attn = jax.nn.softmax(logits, axis=-1)
        h_tilde = jnp.einsum('bst,bth->bsh', attn, v_pool)
        alpha = jax.nn.sigmoid(jnp.einsum('bsh,oh->bso', hidden_states, gate_w) + gate_b)
        return (1.0 - alpha) * hidden_states + alpha * h_tilde

    def _L0_ffn_ref(hidden_states, Wr, W1, b1, Wo, bo, gamma, beta):
        import jax, jax.numpy as jnp
        import numpy as np
        LN_EPS = 1e-12
        B, S, H = hidden_states.shape
        E = Wr.shape[0]
        x = hidden_states.reshape(-1, H)
        router_logits = x @ Wr.T
        expert_idx = jnp.argmax(jax.nn.softmax(router_logits, axis=-1), axis=-1)
        inter = jnp.zeros((x.shape[0], W1.shape[2]), dtype=x.dtype)
        for e in range(E):
            mask = (expert_idx == e)[:, None].astype(x.dtype)
            inter = inter + mask * jax.nn.gelu(x @ W1[e] + b1[e], approximate=False)
        y = inter @ Wo + bo + x
        mu = jnp.mean(y, axis=-1, keepdims=True)
        var = jnp.mean(jnp.square(y - mu), axis=-1, keepdims=True)
        out = (y - mu) * jax.lax.rsqrt(var + LN_EPS) * gamma + beta
        return out.reshape(B, S, H)

    def _L1_attn_ref(hidden_states, W_attn, b_attn, W_proj, b_proj):
        import jax, jax.numpy as jnp
        import numpy as np
        import math
        N_HEAD = 16
        STRIDE = 128
        C = 8

        def _sparse_causal_mask(q_len, k_len):
            cols = np.arange(k_len)
            rows = np.arange(k_len)[:, None]
            strided = cols % STRIDE >= STRIDE - C
            local = cols[None, :] // STRIDE == rows // STRIDE
            causal = cols[None, :] <= rows
            layout = (strided[None, :] | local) & causal
            return jnp.asarray(layout[k_len - q_len:])
        B, S, E = hidden_states.shape
        H = N_HEAD
        D = E // H
        qkv = hidden_states @ W_attn + b_attn
        q, k, v = jnp.split(qkv, 3, axis=-1)
        split = lambda t: t.reshape(B, S, H, D).transpose(0, 2, 1, 3)
        q, k, v = (split(q), split(k), split(v))
        scale = jnp.asarray(1.0 / math.sqrt(D), dtype=q.dtype)
        scores = jnp.einsum('bhqd,bhkd->bhqk', q, k) * scale
        mask = _sparse_causal_mask(S, S)[None, None]
        mask_value = jnp.asarray(jnp.finfo(scores.dtype).min, dtype=scores.dtype)
        scores = jnp.where(mask, scores, mask_value)
        attn = jax.nn.softmax(scores, axis=-1)
        out = jnp.einsum('bhqk,bhkd->bhqd', attn, v)
        out = out.transpose(0, 2, 1, 3).reshape(B, S, E)
        return out @ W_proj + b_proj

    def _L1_xattn_ref(input_Q, input_K, input_V, Wq, bq, Wk, bk, Wv, bv, Wo):
        import jax, jax.numpy as jnp
        import numpy as np
        B, S, D, H, DK = (4, 256, 128, 16, 64)

        def _proj(x, W, b):
            y = jnp.einsum('bsd,ed->bse', x, W) + b
            return y.reshape(x.shape[0], x.shape[1], H, DK).transpose(0, 2, 1, 3)
        Q = _proj(input_Q, Wq, bq)
        K = _proj(input_K, Wk, bk)
        V = _proj(input_V, Wv, bv)
        scores = jnp.einsum('bhqd,bhkd->bhqk', Q, K) / np.sqrt(DK).astype(np.float32)
        attn = jax.nn.softmax(scores, axis=-1)
        context = jnp.einsum('bhqk,bhkd->bhqd', attn, V)
        context = context.transpose(0, 2, 1, 3).reshape(input_Q.shape[0], -1, H * DK)
        return jnp.einsum('bse,de->bsd', context, Wo)

    def _L1_ffn_ref(x, Wr, br, W1, b1, W2, b2):
        import jax, jax.numpy as jnp
        import numpy as np
        E = 8
        K = 2
        CAPACITY_FACTOR = 1.25
        B, T, C = x.shape
        cap = max(1, int(T / E * CAPACITY_FACTOR))
        probs = jax.nn.softmax(x @ Wr + br, axis=-1)
        topk_p, topk_e = jax.lax.top_k(probs, K)
        e_flat = topk_e.reshape(B, T * K)
        p_flat = topk_p.reshape(B, T * K)
        oh = jax.nn.one_hot(e_flat, E, dtype=jnp.int32)
        pos_all = jnp.cumsum(oh, axis=1) - oh
        pos = jnp.take_along_axis(pos_all, e_flat[:, :, None], axis=2)[:, :, 0]
        keep = pos < cap
        b_idx = jnp.arange(B)[:, None]
        flat_idx = (e_flat * B + b_idx) * cap + jnp.minimum(pos, cap - 1)
        x_rep = jnp.broadcast_to(x[:, :, None, :], (B, T, K, C)).reshape(B, T * K, C)
        buf = jnp.zeros((E * B * cap, C), x.dtype).at[flat_idx.reshape(-1)].add((x_rep * keep[:, :, None].astype(x.dtype)).reshape(-1, C))
        buf = buf.reshape(E, B * cap, C)
        h = jax.nn.relu(jnp.einsum('enc,ech->enh', buf, W1) + b1[:, None, :])
        y = jnp.einsum('enh,ehc->enc', h, W2) + b2[:, None, :]
        y_tok = y.reshape(E * B * cap, C)[flat_idx.reshape(-1)].reshape(B, T * K, C)
        y_tok = y_tok * (p_flat * keep.astype(x.dtype))[:, :, None]
        return y_tok.reshape(B, T, K, C).sum(axis=2)
    x = _layernorm(x + _L0_attn_ref(x, L0_attn_ln_att_g, L0_attn_ln_att_b, L0_attn_ln_ffn_g, L0_attn_ln_ffn_b, L0_attn_att_time_decay, L0_attn_att_time_first, L0_attn_att_mix_k, L0_attn_att_mix_v, L0_attn_att_mix_r, L0_attn_att_wk, L0_attn_att_wv, L0_attn_att_wr, L0_attn_att_wo, L0_attn_ffn_mix_k, L0_attn_ffn_mix_r, L0_attn_ffn_wk, L0_attn_ffn_wv, L0_attn_ffn_wr), axis=-1)
    x = _layernorm(x + _L0_xattn_ref(x, ctx_1024, L0_xattn_q_w, L0_xattn_k_w, L0_xattn_norm_w, L0_xattn_gate_w, L0_xattn_gate_b), axis=-1)
    x = _layernorm(x + _L0_ffn_ref(x, L0_ffn_Wr, L0_ffn_W1, L0_ffn_b1, L0_ffn_Wo, L0_ffn_bo, L0_ffn_gamma, L0_ffn_beta), axis=-1)
    x = _layernorm(x + _L1_attn_ref(x, L1_attn_W_attn, L1_attn_b_attn, L1_attn_W_proj, L1_attn_b_proj), axis=-1)
    x = _layernorm(x + _L1_xattn_ref(x, ctx_1024, ctx_1024, L1_xattn_Wq, L1_xattn_bq, L1_xattn_Wk, L1_xattn_bk, L1_xattn_Wv, L1_xattn_bv, L1_xattn_Wo), axis=-1)
    x = _layernorm(x + _L1_ffn_ref(x, L1_ffn_Wr, L1_ffn_br, L1_ffn_W1, L1_ffn_b1, L1_ffn_W2, L1_ffn_b2), axis=-1)
    return x

_drawn_inputs = setup_inputs


def setup_inputs(seed=0):
    import zlib

    import numpy as np

    out = dict(_drawn_inputs(seed))
    spreads = {'L0_attn_ln_att_g': (1.0, 0.6),
     'L0_attn_ln_att_b': (0.0, 0.8),
     'L0_attn_ln_ffn_g': (1.0, 0.6),
     'L0_attn_ln_ffn_b': (0.0, 0.8),
     'L0_xattn_norm_w': (1.0, 0.6),
     'L0_xattn_gate_b': (0.0, 0.543),
     'L0_ffn_gamma': (1.0, 0.2),
     'L0_ffn_beta': (0.0, 0.1),
     'L1_attn_b_attn': (0.0, 0.548),
     'L1_attn_b_proj': (0.0, 0.1),
     'L1_ffn_br': (0.0, 0.621),
     'L1_ffn_b1': (0.0, 0.8),
     'L1_ffn_b2': (0.0, 0.574)}
    factors = {'L0_attn_att_time_decay': 8.0,
     'L0_attn_att_time_first': 8.0,
     'L0_attn_att_mix_k': 8.0,
     'L0_attn_att_mix_v': 8.0,
     'L0_attn_att_mix_r': 8.0,
     'L0_attn_att_wk': 8.0,
     'L0_attn_att_wv': 7.159,
     'L0_attn_att_wr': 8.0,
     'L0_attn_att_wo': 7.502,
     'L0_attn_ffn_mix_k': 8.0,
     'L0_attn_ffn_mix_r': 8.0,
     'L0_attn_ffn_wk': 8.0,
     'L0_attn_ffn_wv': 8.0,
     'L0_attn_ffn_wr': 8.0,
     'L0_ffn_b1': 8.0,
     'L0_ffn_bo': 6.037,
     'L1_attn_W_attn': 7.591,
     'L1_attn_W_proj': 3.707,
     'L1_xattn_bk': 8.0,
     'L1_ffn_Wr': 3.525,
     'L1_ffn_W1': 6.816,
     'L1_ffn_W2': 5.366}
    for name, (base, spread) in spreads.items():
        noise = np.random.default_rng([zlib.crc32(name.encode()), seed]).standard_normal(out[name].shape)
        drawn = base * np.exp(spread * noise) if base else spread * noise
        out[name] = jnp.asarray(drawn.astype(out[name].dtype))
    for name, factor in factors.items():
        out[name] = (out[name] * factor).astype(out[name].dtype)
    return out
```

```python
from contextlib import ExitStack

import concourse.bass as bass
from concourse import mybir

F32 = mybir.dt.float32
BF16 = mybir.dt.bfloat16
U32 = mybir.dt.uint32
ALU = mybir.AluOpType
ACT = mybir.ActivationFunctionType
AX = mybir.AxisListType

P = 128
D = 128
BATCH, SEQ, CTX = 8, 256, 512
GROUP = 2
ITERS = BATCH // GROUP
TOK = GROUP * SEQ
TT = TOK // P
QT = SEQ // P
KT = CTX // P
CT = GROUP * KT
LIN = 512
HT = LIN // P
E = 8
NH, HD = 16, 8
CB = 8
KW = CB + P
XH, DK = 16, 64
PAIRS = XH // 2
CAP = max(1, int(SEQ / E * 1.25))
SLOTS = E * CAP
SB = (SLOTS + P - 1) // P
MASKED = -1.0e30

R_LNG, R_LNB, R_FLNG, R_FLNB, R_DECAY, R_FIRST, R_MK, R_MV, R_MR, R_FMK, R_FMR, R_NORMW = range(12)
R_BATT = 12
R_BQ = 14
R_BK = R_BQ + PAIRS
R_BV = R_BK + PAIRS
R_B1 = R_BV + PAIRS
R_B2 = R_B1 + E * HT
N_COL = R_B2 + E

V_GATEB, V_BV, V_BO, V_BPROJ, V_GAMMA, V_BETA, V_NORMW = range(7)
V_BR = 7 * D
N_ROW = V_BR + E


def decoder_kernel(
    nc, x, ctx_in,
    ln_att_g, ln_att_b, ln_ffn_g, ln_ffn_b, time_decay, time_first, mix_k, mix_v, mix_r,
    att_wk, att_wv, att_wr, att_wo, ffn_mix_k, ffn_mix_r, ffn_wk, ffn_wv, ffn_wr,
    q_w, k_w, norm_w, gate_w, gate_b,
    m0_wr, m0_w1, m0_b1, m0_wo, m0_bo, m0_gamma, m0_beta,
    a1_w, a1_b, a1_wp, a1_bp,
    x1_wq, x1_bq, x1_wk, x1_bk, x1_wv, x1_bv, x1_wo,
    m1_wr, m1_br, m1_w1, m1_b1, m1_w2, m1_b2,
    out,
):
    with ExitStack() as stack:
        def sb(name, shape, dt=F32):
            return stack.enter_context(nc.sbuf_tensor(name, shape, dt))

        def semaphore(name):
            return stack.enter_context(nc.semaphore(name))

        wk, wv, wr, wo = (sb(n, [P, D]) for n in ("wk", "wv", "wr", "wo"))
        fwk = sb("fwk", [P, LIN])
        fwv = sb("fwv", [P, HT, D])
        fwr = sb("fwr", [P, D])
        qw, kw, gw_raw = (sb(n, [P, D]) for n in ("qw", "kw", "gw_raw"))
        qk_fold = sb("qk_fold", [P, D])
        gwT = sb("gwT", [P, D])
        wr0_raw = sb("wr0_raw", [E, D])
        wr0T = sb("wr0T", [P, E])
        w1a = sb("w1a", [P, E, LIN])
        b1a = sb("b1a", [E, LIN])
        wo0 = sb("wo0", [P, HT, D])
        wattn = sb("wattn", [P, 3 * D])
        wproj = sb("wproj", [P, D])
        xwT = sb("xwT", [P, 4, PAIRS, D])
        wr1 = sb("wr1", [P, E])
        w1b = sb("w1b", [P, E, LIN])
        w2b = sb("w2b", [P, E, HT, D])
        col_rows = sb("col_rows", [N_COL, D])
        cols = sb("cols", [P, N_COL])
        decay_w = sb("decay_w", [P, 1])
        decay_e = sb("decay_e", [P, 1])
        bq_scaled = sb("bq_scaled", [P, PAIRS])
        battq_scaled = sb("battq_scaled", [P, 1])
        rows = sb("rows", [1, N_ROW])
        gamma_bc, beta_bc, normw_bc = (sb(n, [P, D]) for n in ("gamma_bc", "beta_bc", "normw_bc"))

        ident = sb("ident", [P, P])
        ident_bf = sb("ident_bf", [P, P], BF16)
        causal = sb("causal", [P, P], BF16)
        sparse = sb("sparse", [P, QT * KW], BF16)
        before = sb("before", [P, P], BF16)
        ones_bf = sb("ones_bf", [P, P], BF16)
        ones = sb("ones", [1, P])
        pick = sb("pick", [E, E, P], BF16)
        head_mask = sb("head_mask", [P, NH])
        iota_e = sb("iota_e", [P, E])
        iota_ei = sb("iota_ei", [P, E], mybir.dt.int32)
        iota_c = sb("iota_c", [P, CAP])
        iota_ci = sb("iota_ci", [P, CAP], mybir.dt.int32)
        neg_half = sb("neg_half", [P, TT])
        eps_ln = sb("eps_ln", [P, TT])
        eps_rms = sb("eps_rms", [P, TT])
        eps_post = sb("eps_post", [P, TT])

        arena = sb("arena", [P, 17 * TOK])

        class Carve:

            def __init__(self):
                self.at = 0

            def __call__(self, *shape, parts=P):
                n = 1
                for k in shape:
                    n *= k
                view = arena[0:parts, self.at:self.at + n]
                self.at += n
                assert self.at <= 17 * TOK
                if len(shape) == 2:
                    return view.rearrange("p (a b) -> p a b", b=shape[1])
                if len(shape) == 3:
                    return view.rearrange("p (a b c) -> p a b c", b=shape[1], c=shape[2])
                return view

        setup, rec_c, att_c, sparse_c, cross_c, mix_c = (Carve() for _ in range(6))
        xw_raw = setup(4, PAIRS, D)
        causal_f, before_f = setup(P), setup(P)
        sparse_f = setup(QT, KW)
        pick_f = setup(E, P, parts=E)

        X0 = sb("X0", [P, TT, D])
        X1 = sb("X1", [P, TT, D])
        X = sb("X", [P, TT, D])
        Y = sb("Y", [P, TT, D])
        NHAT = sb("NHAT", [P, TT, D])
        XT = sb("XT", [P, TOK])
        ctx = sb("ctx", [P, CT, D])
        ctxT = sb("ctxT", [P, CT * P])
        bn = sb("bn", [P, TT, 6])
        mv = sb("mv", [P, TT, 2])
        vare = sb("vare", [P, TT])
        rstd = sb("rstd", [P, TT])
        hT = sb("hT", [P, GROUP, SEQ + 1])
        dT = rec_c(GROUP, SEQ)
        zk, zv, zr, kS, vS, rS = (rec_c(GROUP, SEQ) for _ in range(6))
        o_max, p_num, q_den = (sb(n, [P, GROUP, SEQ + 1]) for n in ("o_max", "p_num", "q_den"))
        o_new = rec_c(GROUP, SEQ)
        w_bc = sb("w_bc", [P, SEQ])
        ex = rec_c(4, GROUP, SEQ)
        b2v, bv_, t_num, t_den, rec = (rec_c(GROUP, SEQ) for _ in range(5))
        big = sb("big", [P, HT, TOK])
        big2 = sb("big2", [P, HT, TOK])
        rf = sb("rf", [P, TT, D])
        junk = sb("junk", [P, D])
        ssq = sb("ssq", [P, TT])
        nT = sb("nT", [P, TOK])
        nTok = sb("nTok", [P, TT, D])
        qpT = sb("qpT", [P, TOK])
        alpha = sb("alpha", [P, TT, D])
        prob = att_c(2, CTX + SEQ)
        probT = att_c(2, CTX + SEQ)
        nmax = sb("nmax", [P, 8])
        rsum = sb("rsum", [P, 2, 8])
        rinv = sb("rinv", [P, 8])
        lg = sb("lg", [P, TT, E])
        top = sb("top", [P, TT, E])
        topi = sb("topi", [P, TT, E], U32)
        topf = sb("topf", [P, TT, 2])
        onehot = sb("onehot", [P, TT, E])
        ohT = sb("ohT", [E, TOK])
        ohT_bf = sb("ohT_bf", [E, TOK], BF16)
        XE = big2[:, 0:2, :]
        qT, kT = sb("qT", [P, TOK]), sb("kT", [P, TOK])
        V = sb("V", [P, TT, D])
        Vs = sb("Vs", [CB, GROUP, D])
        qm = sparse_c(2, TOK)
        SP_ = sparse_c(2, TT, KW)
        spT = sparse_c(2, TOK)
        spTs = sparse_c(2, GROUP, P, parts=CB)
        snm = sb("snm", [P, 2, TT])
        srs = sb("srs", [P, 2, TT])
        sri = sb("sri", [P, 2, TT])
        O = sb("O", [P, TT, D])
        OT = sb("OT", [P, TOK])
        wq_s, wk_s = sb("wq_s", [P, D]), sb("wk_s", [P, D])
        cprob, cprobT = cross_c(2, CTX), cross_c(2, CTX)
        QTs = cross_c(2, TOK)
        KTs = cross_c(2, CT * P)
        Vx = [cross_c(CT, P) for _ in range(2)]
        Cx = cross_c(TT, P)
        CTs = cross_c(TOK)
        ex1 = sb("ex1", [P, TT, E])
        esum = sb("esum", [P, TT])
        einv = sb("einv", [P, TT])
        A = sb("A", [P, TT, E])
        A_bf = sb("A_bf", [P, TT, E], BF16)
        posA = sb("posA", [P, TT, E])
        disp = mix_c(TT, SLOTS)
        comb = mix_c(TT, SLOTS)
        combT = mix_c(SB, TOK)
        xb = mix_c(GROUP, SLOTS)
        hpre = mix_c(2, HT, GROUP * CAP)
        hid = mix_c(2, HT, GROUP * CAP)
        yT = mix_c(GROUP, SLOTS)
        ySl = mix_c(GROUP, SB, D)

        ps = stack.enter_context(nc.psum_tensor("ps", [P, 8, 512], F32))

        def bank(i):
            return ps[:, i, :]

        def tiles(i):
            return ps[:, i, :].rearrange("p (t d) -> p t d", t=TT)

        def seqs(i):
            return ps[:, i, :].rearrange("p (b s) -> p b s", b=GROUP)

        psf = ps[:, :, :].rearrange("p b n -> p (b n)")

        weights_loaded = semaphore("weights_loaded")
        consts_ready = semaphore("consts_ready")
        wT_ps = semaphore("wT_ps")
        wT_sb = semaphore("wT_sb")
        cols_ready = semaphore("cols_ready")
        x_loaded, ctx_loaded, out_stored = (semaphore(n) for n in ("x_loaded", "ctx_loaded", "out_stored"))
        LNS = 9
        var_ready, rstd_ready = semaphore("var_ready"), semaphore("rstd_ready")
        xhat_ready, hT_ps, hT_ready = semaphore("xhat_ready"), semaphore("hT_ps"), semaphore("hT_ready")
        mix_ready, kvr_ps, kvr_ready = semaphore("mix_ready"), semaphore("kvr_ps"), semaphore("kvr_ready")
        wkv_arg, wkv_exp = semaphore("wkv_arg"), semaphore("wkv_exp")
        b2v_ready, bv_ready, wkv_ready = semaphore("b2v_ready"), semaphore("bv_ready"), semaphore("wkv_ready")
        att_ps = semaphore("att_ps")
        kf_ps, kf_relu, kf_ready = semaphore("kf_ps"), semaphore("kf_relu"), semaphore("kf_ready")
        rf_ps, rf_ready, ffn_ps = semaphore("rf_ps"), semaphore("rf_ready"), semaphore("ffn_ps")
        LAYERS = 6
        layer_done = semaphore("layer_done")
        xT_ps, xT_ready = semaphore("xT_ps"), semaphore("xT_ready")
        ctxT_ps, ctxT_ready = semaphore("ctxT_ps"), semaphore("ctxT_ready")
        ssq_ready, rms_ready, nhat_ready = semaphore("ssq_ready"), semaphore("rms_ready"), semaphore("nhat_ready")
        ntok_ready, nT_ps, nT_ready = semaphore("ntok_ready"), semaphore("nT_ps"), semaphore("nT_ready")
        gate_ps, alpha_ready = semaphore("gate_ps"), semaphore("alpha_ready")
        qp_ps, qp_ready = semaphore("qp_ps"), semaphore("qp_ready")
        lg_ps, lg_max, lg_exp = semaphore("lg_ps"), semaphore("lg_max"), semaphore("lg_exp")
        pT_ps, pT_ready, av_ps = semaphore("pT_ps"), semaphore("pT_ready"), semaphore("av_ps")
        route_ps, onehot_ready = semaphore("route_ps"), semaphore("onehot_ready")
        ohT_ps, ohT_ready = semaphore("ohT_ps"), semaphore("ohT_ready")
        pick_ps, xe_ready = semaphore("pick_ps"), semaphore("xe_ready")
        pre_ps, inter_ready, moe_ps = semaphore("pre_ps"), semaphore("inter_ready"), semaphore("moe_ps")
        qkv_ps, qk_ready, v_ready = semaphore("qkv_ps"), semaphore("qk_ready"), semaphore("v_ready")
        qm_ready, s_ps, s_max, s_exp = (semaphore(n) for n in ("qm_ready", "s_ps", "s_max", "s_exp"))
        sT_ps, sT_ready, sTs_ready = (semaphore(n) for n in ("sT_ps", "sT_ready", "sTs_ready"))
        so_ps, so_ready = semaphore("so_ps"), semaphore("so_ready")
        oT_ps, oT_ready, proj_ps = semaphore("oT_ps"), semaphore("oT_ready"), semaphore("proj_ps")
        NS = 2 * TT
        staged = semaphore("staged")
        q_ps, k_ps, vx_ps = semaphore("q_ps"), semaphore("k_ps"), semaphore("vx_ps")
        q_ready, k_ready = semaphore("q_ready"), semaphore("k_ready")
        vx_ready = semaphore("vx_ready")
        c_ps, c_max, c_exp = (semaphore(n) for n in ("c_ps", "c_max", "c_exp"))
        cT_ps, cT_even, cT_odd = semaphore("cT_ps"), semaphore("cT_even"), semaphore("cT_odd")
        o_ps, o_ready, ctT_ps, ctT_ready = (semaphore(n) for n in ("o_ps", "o_ready", "ctT_ps", "ctT_ready"))
        wo_ps, wo_added = semaphore("wo_ps"), semaphore("wo_added")
        r1_ps, e1_arg, e1_exp = semaphore("r1_ps"), semaphore("e1_arg"), semaphore("e1_exp")
        two_hot, pos_ps, disp_ready = semaphore("two_hot"), semaphore("pos_ps"), semaphore("disp_ready")
        comb_ready, combT_ps, combT_ready = semaphore("comb_ready"), semaphore("combT_ps"), semaphore("combT_ready")
        xb_ps, xb_ready = semaphore("xb_ps"), semaphore("xb_ready")
        hid_ps, hid_biased, hid_ready = (semaphore(n) for n in ("hid_ps", "hid_biased", "hid_ready"))
        y_ps, y_ready = semaphore("y_ps"), semaphore("y_ready")
        ysl_ps, ysl_ready, comb_ps = semaphore("ysl_ps"), semaphore("ysl_ready"), semaphore("comb_ps")

        def one_row(v):
            return v.rearrange("(a n) -> a n", a=1)

        def half(w, n):
            return w.rearrange("(t p) n -> p t n", p=P)

        loads = [
            (wk[:, :], att_wk), (wv[:, :], att_wv), (wr[:, :], att_wr), (wo[:, :], att_wo),
            (fwk[:, :], ffn_wk), (fwv[:, :, :], half(ffn_wv, D)), (fwr[:, :], ffn_wr),
            (qw[:, :], q_w), (kw[:, :], k_w), (gw_raw[:, :], gate_w),
            (wr0_raw[:, :], m0_wr), (b1a[:, :], m0_b1), (wo0[:, :, :], half(m0_wo, D)),
            (wattn[:, :], a1_w), (wproj[:, :], a1_wp), (wr1[:, :], m1_wr),
            (xw_raw[:, 0, :, :], half(x1_wq, D)), (xw_raw[:, 1, :, :], half(x1_wk, D)),
            (xw_raw[:, 2, :, :], half(x1_wv, D)),
            (xw_raw[:, 3, :, :], x1_wo.rearrange("p (j f) -> p j f", f=P)),
            (w1a[:, :, :], m0_w1.rearrange("e c h -> c e h")),
            (w1b[:, :, :], m1_w1.rearrange("e c h -> c e h")),
        ] + [(w2b[:, e, :, :], half(m1_w2[e, :, :], D)) for e in range(E)]
        for row, v in ((R_LNG, ln_att_g), (R_LNB, ln_att_b), (R_FLNG, ln_ffn_g), (R_FLNB, ln_ffn_b),
                       (R_DECAY, time_decay), (R_FIRST, time_first), (R_MK, mix_k), (R_MV, mix_v),
                       (R_MR, mix_r), (R_FMK, ffn_mix_k), (R_FMR, ffn_mix_r), (R_NORMW, norm_w)):
            loads.append((col_rows[row:row + 1, :], one_row(v)))
        loads += [
            (col_rows[R_BATT:R_BATT + 2, :], a1_b[0:2 * D].rearrange("(j p) -> j p", p=P)),
            (col_rows[R_BQ:R_BQ + PAIRS, :], x1_bq.rearrange("(j p) -> j p", p=P)),
            (col_rows[R_BK:R_BK + PAIRS, :], x1_bk.rearrange("(j p) -> j p", p=P)),
            (col_rows[R_BV:R_BV + PAIRS, :], x1_bv.rearrange("(j p) -> j p", p=P)),
            (col_rows[R_B1:R_B1 + E * HT, :], m1_b1.rearrange("e (h p) -> (e h) p", p=P)),
            (col_rows[R_B2:R_B2 + E, :], m1_b2),
        ]
        for i, v in enumerate((gate_b, a1_b[2 * D:3 * D], m0_bo, a1_bp, m0_gamma, m0_beta, norm_w)):
            loads.append((rows[0:1, i * D:(i + 1) * D], one_row(v)))
        loads.append((rows[0:1, V_BR:V_BR + E], one_row(m1_br)))

        def row_of(i):
            return rows[0:1, i * D:(i + 1) * D]

        def col(i):
            return cols[:, i:i + 1]

        weight_turns = []
        for w in range(4):
            for g in range(0, PAIRS, 4):
                weight_turns.append(([xw_raw[:, w, g + i, :] for i in range(4)], xwT[:, w, g:g + 4, :]))
        weight_turns.append(([gw_raw[:, :]], gwT[:, :]))
        weight_turns.append(([wr0_raw[:, :]], wr0T[:, :]))
        weight_turns.append(([col_rows[:, :]], cols[:, :]))
        N_TURNS = len(weight_turns)
        N_SETUP = N_TURNS + 4

        x_v = x.rearrange("(i b) (t p) d -> i p (b t) d", b=GROUP, p=P)
        out_v = out.rearrange("(i b) (t p) d -> i p (b t) d", b=GROUP, p=P)
        ctx_v = ctx_in.rearrange("(i b) (t p) d -> i p (b t) d", b=GROUP, p=P)

        def at(view, it):
            if isinstance(it, int):
                return view[it, :, :, :]
            return view[bass.ds(it, 1), :, :, :].squeeze(0)

        block = stack.enter_context(nc.Block())

        @block.sync
        def _(sp):
            def load_x(it):
                sp.dma_start(X0[:, :, :], at(x_v, it)).then_inc(x_loaded, 16)

            def load_ctx(it):
                sp.dma_start(ctx[:, :, :], at(ctx_v, it)).then_inc(ctx_loaded, 16)

            def store(it):
                sp.wait_ge(layer_done, it * LAYERS + LAYERS)
                sp.dma_start(at(out_v, it), X[:, :, :]).then_inc(out_stored, 16)

            load_x(0)
            for dst, src in loads:
                sp.dma_start(dst, src).then_inc(weights_loaded, 16)
            load_ctx(0)
            with sp.Fori(0, ITERS - 1) as it:
                sp.wait_ge(layer_done, it * LAYERS + 1)
                load_x(it + 1)
                sp.wait_ge(av_ps, it + 1)
                load_ctx(it + 1)
                store(it)
            store(ITERS - 1)
            sp.wait_ge(out_stored, 16 * ITERS + 1)

        @block.tensor
        def _(pe):
            def turn(src, b):
                for t in range(TT):
                    last = pe.transpose(ps[:, b, t * P:(t + 1) * P], src[:, t, :], ident[:, :])
                return last

            def turn_x(it, n, layers):
                pe.wait_ge(layer_done, it * LAYERS + layers)
                turn(X, 0).then_inc(xT_ps, 1)
                pe.wait_ge(xT_ready, it * 5 + n)

            def token_major(b, lhs, w, row=None):
                for t in range(TT):
                    o = ps[:, b, t * D:(t + 1) * D]
                    if row is not None:
                        pe.matmul(o, ones[0:1, :], row, start=True, stop=False)
                    last = pe.matmul(o, lhs[:, t * P:(t + 1) * P], w, start=row is None, stop=True)
                return last

            pe.wait_ge(consts_ready, 1)
            pe.wait_ge(weights_loaded, 16 * len(loads))
            for n, (srcs, _) in enumerate(weight_turns):
                if n >= 8:
                    pe.wait_ge(wT_sb, n - 7)
                for i, s in enumerate(srcs):
                    k = s.shape[0]
                    last = pe.transpose(ps[:, n % 8, i * P:i * P + k], s, ident[0:k, 0:k])
                last.then_inc(wT_ps, 1)
            for i in range(4):
                n = N_TURNS + i
                pe.wait_ge(wT_sb, n - 7)
                o = ps[:, n % 8, 0:D]
                if i == 0:
                    last = pe.matmul(o, qw[:, :], kw[:, :], start=True, stop=True)
                else:
                    last = pe.matmul(o, ones[0:1, :], row_of((V_GAMMA, V_BETA, V_NORMW)[i - 1]),
                                     start=True, stop=True)
                last.then_inc(wT_ps, 1)
            pe.wait_ge(wT_sb, N_SETUP)

            def recurrent(it):
                pe.wait_ge(xhat_ready, it * 2 + 1)
                turn(NHAT, 0).then_inc(hT_ps, 1)
                for i, (z, w) in enumerate(((zk, wk), (zv, wv), (zr, wr))):
                    pe.wait_ge(mix_ready, it * 5 + i + 1)
                    pe.matmul(bank(1 + i), w[:, :], z[:, :, :], start=True, stop=True).then_inc(kvr_ps, 1)
                pe.wait_ge(wkv_ready, it + 1)
                y = rec[:, :, :].rearrange("p b s -> p (b s)")
                token_major(4, y, wo[:, :]).then_inc(att_ps, 1)
                pe.wait_ge(xhat_ready, it * 2 + 2)
                turn(NHAT, 0).then_inc(hT_ps, 1)
                pe.wait_ge(mix_ready, it * 5 + 4)
                for h, b in enumerate((1, 2, 3, 5)):
                    pe.matmul(bank(b), fwk[:, h * P:(h + 1) * P], zk[:, :, :], start=True, stop=True)\
                        .then_inc(kf_ps, 1)
                pe.wait_ge(mix_ready, it * 5 + 5)
                token_major(6, zr[:, :, :].rearrange("p b s -> p (b s)"), fwr[:, :]).then_inc(rf_ps, 1)
                pe.wait_ge(kf_ready, it * HT + HT)
                for t in range(TT):
                    for h in range(HT):
                        last = pe.matmul(ps[:, 7, t * D:(t + 1) * D], big2[:, h, t * P:(t + 1) * P],
                                         fwv[:, h, :], start=(h == 0), stop=(h == HT - 1))
                last.then_inc(ffn_ps, 1)

            def memory(it):
                pe.wait_ge(layer_done, it * LAYERS + 1)
                pe.wait_ge(ctx_loaded, it * 16 + 16)
                for g in range(2):
                    for i in range(4):
                        last = pe.transpose(ps[:, 6 + g, i * P:(i + 1) * P], ctx[:, 4 * g + i, :], ident[:, :])
                    last.then_inc(ctxT_ps, 1)
                turn_x(it, 1, 1)
                token_major(2, XT, gwT[:, :], row_of(V_GATEB)).then_inc(gate_ps, 1)
                pe.wait_ge(nhat_ready, it + 1)
                turn(NHAT, 1).then_inc(nT_ps, 1)
                pe.wait_ge(nT_ready, it + 1)
                pe.matmul(bank(3), qk_fold[:, :], nT[:, :], start=True, stop=True).then_inc(qp_ps, 1)
                pe.wait_ge(ctxT_ready, it * 2 + 2)
                pe.wait_ge(qp_ready, it + 1)
                pe.wait_ge(alpha_ready, it + 1)

                def logits(t):
                    b, tq, base = t // QT, t % QT, 2 * (t % 2)
                    nk = (tq + 1) * P
                    q = qpT[:, t * P:(t + 1) * P]
                    pe.matmul(bank(base), q, ctxT[:, b * CTX:(b + 1) * CTX], start=True, stop=True)
                    k0 = b * SEQ + nk - P
                    if tq:
                        pe.matmul(ps[:, base + 1, 0:nk - P], q, nT[:, b * SEQ:k0], start=True, stop=True)
                    pe.matmul(ps[:, base + 1, nk - P:nk], ident_bf[:, :], causal[:, :], start=True, stop=False)
                    pe.matmul(ps[:, base + 1, nk - P:nk], q, nT[:, k0:k0 + P], start=False, stop=True)\
                        .then_inc(lg_ps, 1)

                def turn_probs(t):
                    pe.wait_ge(lg_exp, it * TT + t + 1)
                    for k in range(KT + t % QT + 1):
                        last = pe.transpose(psf[:, 4 * 512 + k * P:4 * 512 + (k + 1) * P],
                                            prob[:, t % 2, k * P:(k + 1) * P], ident[:, :])
                    last.then_inc(pT_ps, 1)

                def values(t):
                    b, tq = t // QT, t % QT
                    if t == 0:
                        pe.wait_ge(ntok_ready, it + 1)
                    pe.wait_ge(pT_ready, it * TT + t + 1)
                    n = KT + tq + 1
                    for k in range(n):
                        v = ctx[:, b * KT + k, :] if k < KT else nTok[:, b * QT + k - KT, :]
                        last = pe.matmul(ps[:, 6, t * D:(t + 1) * D], probT[:, 0, k * P:(k + 1) * P], v,
                                         start=(k == 0), stop=(k == n - 1))
                    return last

                logits(0)
                logits(1)
                for t in range(TT):
                    turn_probs(t)
                    if t + 2 < TT:
                        logits(t + 2)
                    last = values(t)
                last.then_inc(av_ps, 1)

            def mixture_top1(it):
                turn_x(it, 2, 2)
                for t in range(TT):
                    last = pe.matmul(ps[:, 1, t * E:(t + 1) * E], XT[:, t * P:(t + 1) * P], wr0T[:, :],
                                     start=True, stop=True)
                last.then_inc(route_ps, 1)
                pe.wait_ge(onehot_ready, it + 1)
                for t in range(TT):
                    last = pe.transpose(ps[0:E, 2, t * P:(t + 1) * P], onehot[:, t, :], ident[:, :])
                last.then_inc(ohT_ps, 1)
                pe.wait_ge(ohT_ready, it * 2 + 2)

                def pick_rows(e):
                    pe.matmul(bank(3 + e % 2), pick[:, e, :], ohT_bf[:, :], start=True, stop=True)\
                        .then_inc(pick_ps, 1)

                acc = (5, 6, 7, 0)
                pick_rows(0)
                pick_rows(1)
                for e in range(E):
                    pe.wait_ge(xe_ready, it * E + e + 1)
                    for h in range(HT):
                        pe.matmul(bank(acc[h]), w1a[:, e, h * P:(h + 1) * P], XE[:, e % 2, :],
                                  start=(e == 0), stop=False)
                        if e == E - 1:
                            pe.matmul(bank(acc[h]), b1a[:, h * P:(h + 1) * P], ohT[:, :], start=False, stop=True)\
                                .then_inc(pre_ps, 1)
                    if e + 2 < E:
                        pick_rows(e + 2)
                pe.wait_ge(inter_ready, it * HT + HT)
                for t in range(TT):
                    o = ps[:, 1, t * D:(t + 1) * D]
                    pe.matmul(o, ones[0:1, :], row_of(V_BO), start=True, stop=False)
                    for h in range(HT):
                        last = pe.matmul(o, big[:, h, t * P:(t + 1) * P], wo0[:, h, :], start=False, stop=(h == HT - 1))
                last.then_inc(moe_ps, 1)

            def sparse_attention(it):
                turn_x(it, 3, 3)
                pe.matmul(bank(1), wattn[:, 0:D], XT[:, :], start=True, stop=True).then_inc(qkv_ps, 1)
                pe.matmul(bank(2), wattn[:, D:2 * D], XT[:, :], start=True, stop=True).then_inc(qkv_ps, 1)
                token_major(3, XT, wattn[:, 2 * D:3 * D], row_of(V_BV)).then_inc(qkv_ps, 1)
                for b in range(GROUP):
                    o = ps[0:CB, 4, b * D:(b + 1) * D]
                    pe.matmul(o, ones[0:1, 0:CB], row_of(V_BV), start=True, stop=False)
                    last = pe.matmul(o, XT[:, b * SEQ + P - CB:b * SEQ + P], wattn[:, 2 * D:3 * D],
                                     start=False, stop=True)
                last.then_inc(qkv_ps, 1)

                def scores(hh, u):
                    pe.wait_ge(qm_ready, it * NH + 2 * hh + u + 1)
                    for b in range(GROUP):
                        o = 2 * u + b
                        for tq in range(QT):
                            c = tq * KW
                            k0 = b * SEQ + tq * (SEQ - KW)
                            pe.matmul(ps[:, o, c:c + KW], ident_bf[:, :], sparse[:, c:c + KW], start=True, stop=False)
                            last = pe.matmul(ps[:, o, c:c + KW], qm[:, u, b * SEQ + tq * P:b * SEQ + (tq + 1) * P],
                                             kT[:, k0:k0 + KW], start=False, stop=True)
                    last.then_inc(s_ps, 1)

                def turn_probs(hh, u):
                    pe.wait_ge(s_exp, it * NH + 2 * hh + u + 1)
                    pe.wait_ge(so_ready, it * NH + 2 * hh + u + 1)
                    for t in range(TT):
                        lo = 0 if t % QT == 0 else CB
                        pe.transpose(ps[:, 4 + u, t * P:(t + 1) * P], SP_[:, u, t, lo:lo + P], ident[:, :])
                    for b in range(GROUP):
                        last = pe.transpose(ps[0:CB, 6 + u, b * P:(b + 1) * P], SP_[:, u, b * QT + 1, 0:CB], ident[:, :])
                    last.then_inc(sT_ps, 1)

                def values(hh, u):
                    h = 2 * hh + u
                    pe.wait_ge(sT_ready, it * NH + h + 1)
                    pe.wait_ge(sTs_ready, it * NH + h + 1)
                    for t in range(TT):
                        c = GROUP * P + t * HD
                        first = t % QT == 0
                        last = pe.matmul(ps[:, 6 + u, c:c + HD], spT[:, u, t * P:(t + 1) * P],
                                         V[:, t, bass.ds(h * HD, HD)], start=True, stop=first)
                        if not first:
                            last = pe.matmul(ps[:, 6 + u, c:c + HD], spTs[:, u, t // QT, :],
                                             Vs[:, t // QT, bass.ds(h * HD, HD)], start=False, stop=True)
                    last.then_inc(so_ps, 1)

                def two_heads(hh, more):
                    turn_probs(hh, 0)
                    if more:
                        scores(hh + 1, 0)
                    turn_probs(hh, 1)
                    values(hh, 0)
                    if more:
                        scores(hh + 1, 1)
                    values(hh, 1)

                pe.wait_ge(qk_ready, it * 2 + 2)
                pe.wait_ge(v_ready, it * 2 + 2)
                scores(0, 0)
                scores(0, 1)
                with pe.Fori(0, NH // 2 - 1) as hh:
                    two_heads(hh, True)
                two_heads(NH // 2 - 1, False)
                pe.wait_ge(so_ready, it * NH + NH + 2)
                turn(O, 0).then_inc(oT_ps, 1)
                pe.wait_ge(oT_ready, it + 1)
                token_major(1, OT, wproj[:, :], row_of(V_BPROJ)).then_inc(proj_ps, 1)

            def cross_attention(it):
                turn_x(it, 4, 4)

                def project_q(j, b):
                    pe.wait_ge(staged, it * PAIRS + j + 1)
                    pe.matmul(bank(b), wq_s[:, :], XT[:, :], start=True, stop=True).then_inc(q_ps, 1)

                def project_k(b, seq):
                    pe.matmul(bank(b), wk_s[:, :], ctxT[:, seq * CTX:(seq + 1) * CTX], start=True, stop=True)\
                        .then_inc(k_ps, 1)

                def project_v(j, b, seq):
                    for k in range(KT):
                        c = seq * KT + k
                        last = pe.matmul(ps[:, b, k * P:(k + 1) * P], ctxT[:, c * P:(c + 1) * P],
                                         xwT[:, 2, bass.ds(j, 1), :], start=True, stop=True)
                    last.then_inc(vx_ps, 1)

                def scores(j, u, s):
                    h, t = s // TT, s % TT
                    if s == 0:
                        pe.wait_ge(q_ready, it * PAIRS + j + 1)
                        pe.wait_ge(k_ready, it * (2 * PAIRS) + 2 * j + 1)
                    if s == QT:
                        pe.wait_ge(k_ready, it * (2 * PAIRS) + 2 * j + 2)
                    r = slice(h * DK, (h + 1) * DK)
                    pe.matmul(bank(s % 2), QTs[r, u, t * P:(t + 1) * P],
                              KTs[r, u, (t // QT) * CTX:(t // QT + 1) * CTX], start=True, stop=True).then_inc(c_ps, 1)

                def turn_probs(j, s):
                    pe.wait_ge(c_exp, it * (NS * PAIRS) + j * NS + s + 1)
                    for k in range(KT):
                        last = pe.transpose(ps[:, 2 + s % 2, k * P:(k + 1) * P], cprob[:, s % 2, k * P:(k + 1) * P],
                                            ident[:, :])
                    last.then_inc(cT_ps, 1)

                def values(j, u, s):
                    h, t = s // TT, s % TT
                    if s == 0:
                        pe.wait_ge(vx_ready, it * (2 * PAIRS) + 2 * j + 2)
                    pe.wait_ge((cT_even, cT_odd)[s % 2], it * (NS * PAIRS // 2) + j * (NS // 2) + s // 2 + 1)
                    o = ps[:, 4 + u, t * P + h * DK:t * P + (h + 1) * DK]
                    for k in range(KT):
                        last = pe.matmul(o, cprobT[:, s % 2, k * P:(k + 1) * P],
                                         Vx[u][:, (t // QT) * KT + k, h * DK:(h + 1) * DK],
                                         start=(k == 0), stop=(k == KT - 1))
                    return last

                def turn_context(j):
                    pe.wait_ge(o_ready, it * PAIRS + j + 1)
                    turn(Cx, 6).then_inc(ctT_ps, 1)

                def project_out(j, b):
                    pe.wait_ge(ctT_ready, it * PAIRS + j + 1)
                    for t in range(TT):
                        last = pe.matmul(ps[:, b, t * D:(t + 1) * D], CTs[:, t * P:(t + 1) * P],
                                         xwT[:, 3, bass.ds(j, 1), :], start=True, stop=True)
                    last.then_inc(wo_ps, 1)

                def between_steps(j, s, first, more):
                    if s == 0 and more:
                        pe.wait_ge(vx_ready, it * (2 * PAIRS) + 2 * j + 2)
                        project_q(j + 1, 7)
                    if s == 1 and not first:
                        turn_context(j - 1)
                    if s == 2 and more:
                        pe.wait_ge(q_ready, it * PAIRS + j + 2)
                        project_k(7, 0)
                    if s == 3 and not first:
                        project_out(j - 1, 6)
                    if s == 4 and more:
                        pe.wait_ge(k_ready, it * (2 * PAIRS) + 2 * j + 3)
                        project_k(7, 1)
                    if s == 5 and more:
                        pe.wait_ge(wo_added, it * (PAIRS + 1) + j + 1)
                        project_v(j + 1, 6, 0)
                    if s == 6 and more:
                        pe.wait_ge(k_ready, it * (2 * PAIRS) + 2 * j + 4)
                        project_v(j + 1, 7, 1)

                def pair(j, u, first=False, more=True):
                    for s in range(NS):
                        turn_probs(j, s)
                        if s >= 1:
                            values(j, u, s - 1)
                        if s + 2 < NS:
                            scores(j, u, s + 2)
                        elif more:
                            scores(j + 1, 1 - u, s + 2 - NS)
                        between_steps(j, s, first, more)
                    values(j, u, NS - 1).then_inc(o_ps, 1)

                project_q(0, 7)
                project_k(6, 0)
                project_k(3, 1)
                project_v(0, 4, 0)
                project_v(0, 5, 1)
                scores(0, 0, 0)
                scores(0, 0, 1)
                pair(0, 0, first=True)
                with pe.Fori(0, PAIRS // 2 - 1) as jj:
                    pair(2 * jj + 1, 1)
                    pair(2 * jj + 2, 0)
                pair(PAIRS - 1, 1, more=False)
                turn_context(PAIRS - 1)
                project_out(PAIRS - 1, 7)

            def mixture_top2(it):
                turn_x(it, 5, 5)
                for t in range(TT):
                    o = ps[:, 1, t * E:(t + 1) * E]
                    pe.matmul(o, ones[0:1, :], rows[0:1, V_BR:V_BR + E], start=True, stop=False)
                    last = pe.matmul(o, XT[:, t * P:(t + 1) * P], wr1[:, :], start=False, stop=True)
                last.then_inc(r1_ps, 1)
                pe.wait_ge(two_hot, it + 1)
                for t in range(TT):
                    o = ps[:, 2, t * E:(t + 1) * E]
                    if t % QT:
                        pe.matmul(o, ones_bf[:, :], A_bf[:, t - 1, :], start=True, stop=False)
                    last = pe.matmul(o, before[:, :], A_bf[:, t, :], start=(t % QT == 0), stop=True)
                last.then_inc(pos_ps, 1)
                pe.wait_ge(disp_ready, it + 1)
                for b in range(GROUP):
                    for tq in range(QT):
                        t = b * QT + tq
                        last = pe.matmul(ps[:, 3 + b, 0:SLOTS], X[:, t, :], disp[:, t, :], start=(tq == 0),
                                         stop=(tq == QT - 1))
                    last.then_inc(xb_ps, 1)
                pe.wait_ge(comb_ready, it + 1)
                for t in range(TT):
                    for k in range(SB):
                        n = min(P, SLOTS - k * P)
                        last = pe.transpose(ps[0:n, 5 + k, t * P:(t + 1) * P], comb[:, t, k * P:k * P + n], ident[:, :])
                last.then_inc(combT_ps, 1)
                pe.wait_ge(xb_ready, it * GROUP + GROUP)
                W = GROUP * CAP

                def up(e):
                    if e >= 2:
                        pe.wait_ge(hid_biased, it * E + e - 1)
                    for h in range(HT):
                        last = pe.matmul(ps[:, e % 2, h * W:(h + 1) * W], w1b[:, e, h * P:(h + 1) * P],
                                         xb[:, :, e * CAP:(e + 1) * CAP], start=True, stop=True)
                    last.then_inc(hid_ps, 1)

                def down(e):
                    pe.wait_ge(hid_ready, it * E + e + 1)
                    if e >= 2:
                        pe.wait_ge(y_ready, it * E + e - 1)
                    for h in range(HT):
                        last = pe.matmul(ps[:, 2 + e % 2, 0:W], w2b[:, e, h, :], hid[:, e % 2, h, :],
                                         start=(h == 0), stop=(h == HT - 1))
                    last.then_inc(y_ps, 1)

                up(0)
                for e in range(E):
                    if e + 1 < E:
                        up(e + 1)
                    down(e)
                pe.wait_ge(y_ready, it * E + E)
                pe.wait_ge(combT_ready, it + 1)
                for b in range(GROUP):
                    for k in range(SB):
                        n = min(P, SLOTS - k * P)
                        last = pe.transpose(ps[0:n, 5 + b, k * D:(k + 1) * D], yT[:, b, k * P:k * P + n], ident[:, :])
                    last.then_inc(ysl_ps, 1)
                for t in range(TT):
                    if t % QT == 0:
                        pe.wait_ge(ysl_ready, it * GROUP + t // QT + 1)
                    for k in range(SB):
                        n = min(P, SLOTS - k * P)
                        last = pe.matmul(ps[:, 4, t * D:(t + 1) * D], combT[0:n, k, t * P:(t + 1) * P],
                                         ySl[0:n, t // QT, k, :], start=(k == 0), stop=(k == SB - 1))
                last.then_inc(comb_ps, 1)

            with pe.Fori(0, ITERS) as it:
                recurrent(it)
                memory(it)
                mixture_top1(it)
                sparse_attention(it)
                cross_attention(it)
                mixture_top2(it)

        @block.scalar
        def _(act):
            def copy(dst, src):
                return act.activation(dst, src, ACT.Copy)

            copies = [(ps[:, n % 8, :].rearrange("p (g d) -> p g d", g=4) if len(s) == 4
                      else ps[:, n % 8, 0:s[0].shape[0]], d) for n, (s, d) in enumerate(weight_turns)]
            copies += [(ps[:, (N_TURNS + i) % 8, 0:D], d[:, :])
                      for i, d in enumerate((qk_fold, gamma_bc, beta_bc, normw_bc))]
            for n, (src, dst) in enumerate(copies):
                act.wait_ge(wT_ps, n + 1)
                copy(dst, src).then_inc(wT_sb, 1)
            act.wait_ge(wT_sb, N_SETUP)
            act.activation(decay_e[:, :], col(R_DECAY), ACT.Exp).then_inc(cols_ready, 1)
            act.wait_ge(cols_ready, 5)

            def x_turned(it, n):
                act.wait_ge(xT_ps, it * 5 + n)
                copy(XT[:, :], bank(0)).then_inc(xT_ready, 1)

            def recurrent(it):
                act.wait_ge(hT_ps, it * 2 + 1)
                act.activation(hT[:, :, 1:SEQ + 1], seqs(0), ACT.Identity, bias=col(R_LNB), scale=col(R_LNG))\
                    .then_inc(hT_ready, 1)
                for i, (dst, f) in enumerate(((kS, ACT.Copy), (vS, ACT.Copy), (rS, ACT.Sigmoid))):
                    act.wait_ge(kvr_ps, it * 3 + i + 1)
                    act.activation(dst[:, :, :], seqs(1 + i), f).then_inc(kvr_ready, 1)
                for i in range(4):
                    act.wait_ge(wkv_arg, it * 4 + i + 1)
                    act.activation(ex[:, i, :, :], ex[:, i, :, :], ACT.Exp).then_inc(wkv_exp, 1)
                act.wait_ge(hT_ps, it * 2 + 2)
                act.activation(hT[:, :, 1:SEQ + 1], seqs(0), ACT.Identity, bias=col(R_FLNB), scale=col(R_FLNG))\
                    .then_inc(hT_ready, 1)
                for h, b in enumerate((1, 2, 3, 5)):
                    act.wait_ge(kf_ps, it * HT + h + 1)
                    act.activation(big[:, h, :], bank(b), ACT.Relu).then_inc(kf_relu, 1)
                act.wait_ge(rf_ps, it + 1)
                act.activation(rf[:, :, :], tiles(6), ACT.Sigmoid).then_inc(rf_ready, 1)

            def memory(it):
                act.wait_ge(layer_done, it * LAYERS + 1)
                for t in range(TT):
                    if t:
                        act.drain()
                    last = act.activation(junk[:, :], X[:, t, :], ACT.Square, scale=float(D) ** -0.5,
                                          accum_out=ssq[:, t:t + 1])
                last.then_inc(ssq_ready, 1)
                for g in range(2):
                    act.wait_ge(ctxT_ps, it * 2 + g + 1)
                    copy(ctxT[:, g * 512:(g + 1) * 512], bank(6 + g)).then_inc(ctxT_ready, 1)
                x_turned(it, 1)
                act.wait_ge(nT_ps, it + 1)
                act.activation(nT[:, :], bank(1), ACT.Identity, scale=col(R_NORMW)).then_inc(nT_ready, 1)
                act.wait_ge(gate_ps, it + 1)
                act.activation(alpha[:, :, :], tiles(2), ACT.Sigmoid).then_inc(alpha_ready, 1)
                act.wait_ge(qp_ps, it + 1)
                act.activation(qpT[:, :], bank(3), ACT.Copy, scale=float(D) ** -0.5).then_inc(qp_ready, 1)

                def exps(t):
                    n = CTX + (t % QT + 1) * P
                    act.wait_ge(lg_max, it * TT + t + 1)
                    lo = 2 * (t % 2) * 512
                    act.activation(prob[:, t % 2, 0:n], psf[:, lo:lo + n], ACT.Exp, bias=nmax[:, t:t + 1],
                                   accum_out=rsum[:, 0, t:t + 1]).then_inc(lg_exp, 1)

                exps(0)
                exps(1)
                for t in range(TT):
                    n = CTX + (t % QT + 1) * P
                    act.wait_ge(pT_ps, it * TT + t + 1)
                    copy(probT[:, 0, 0:n], psf[:, 4 * 512:4 * 512 + n]).then_inc(pT_ready, 1)
                    if t + 2 < TT:
                        exps(t + 2)

            def mixture_top1(it):
                x_turned(it, 2)
                act.wait_ge(ohT_ps, it + 1)
                copy(ohT_bf[:, :], ps[0:E, 2, :]).then_inc(ohT_ready, 1)
                copy(ohT[:, :], ps[0:E, 2, :]).then_inc(ohT_ready, 1)
                for h, b in enumerate((5, 6, 7, 0)):
                    act.wait_ge(pre_ps, it * HT + h + 1)
                    act.activation(big[:, h, :], bank(b), ACT.Gelu).then_inc(inter_ready, 1)

            def sparse_attention(it):
                x_turned(it, 3)
                act.wait_ge(qkv_ps, it * 4 + 1)
                act.activation(qT[:, :], bank(1), ACT.Identity, bias=battq_scaled[:, 0:1], scale=float(HD) ** -0.5)\
                    .then_inc(qk_ready, 1)
                act.wait_ge(qkv_ps, it * 4 + 2)
                act.activation(kT[:, :], bank(2), ACT.Identity, bias=col(R_BATT + 1)).then_inc(qk_ready, 1)
                act.wait_ge(qkv_ps, it * 4 + 3)
                copy(V[:, :, :], tiles(3)).then_inc(v_ready, 1)
                act.wait_ge(qkv_ps, it * 4 + 4)
                copy(Vs[:, :, :], ps[0:CB, 4, 0:GROUP * D].rearrange("p (b d) -> p b d", b=GROUP))\
                    .then_inc(v_ready, 1)

                def exps(hh, u):
                    act.wait_ge(s_max, it * NH + 2 * hh + u + 1)
                    for t in range(TT):
                        c = (t % QT) * KW
                        last = act.activation(SP_[:, u, t, :], ps[:, 2 * u + t // QT, c:c + KW], ACT.Exp,
                                              bias=snm[:, u, t:t + 1], accum_out=srs[:, u, t:t + 1])
                    last.then_inc(s_exp, 1)

                def turned(hh, u):
                    act.wait_ge(sT_ps, it * NH + 2 * hh + u + 1)
                    copy(spT[:, u, :], bank(4 + u)).then_inc(sT_ready, 1)

                exps(0, 0)
                exps(0, 1)
                with act.Fori(0, NH // 2 - 1) as hh:
                    turned(hh, 0)
                    turned(hh, 1)
                    exps(hh + 1, 0)
                    exps(hh + 1, 1)
                turned(NH // 2 - 1, 0)
                turned(NH // 2 - 1, 1)
                act.wait_ge(oT_ps, it + 1)
                copy(OT[:, :], bank(0)).then_inc(oT_ready, 1)

            def cross_attention(it):
                x_turned(it, 4)

                def queries(j, u, b):
                    act.wait_ge(q_ps, it * PAIRS + j + 1)
                    act.wait_ge(cols_ready, 5)
                    act.activation(QTs[:, u, :], bank(b), ACT.Identity, bias=bq_scaled[:, bass.ds(j, 1)],
                                   scale=float(DK) ** -0.5).then_inc(q_ready, 1)

                def keys(j, u, b, seq):
                    if seq == 0 or isinstance(j, int):
                        act.wait_ge(k_ps, it * (2 * PAIRS) + 2 * j + seq + 1)
                    act.wait_ge(cols_ready, 5)
                    act.activation(KTs[:, u, seq * CTX:(seq + 1) * CTX], bank(b), ACT.Identity,
                                   bias=cols[:, bass.ds(R_BK + j, 1)]).then_inc(k_ready, 1)

                def exps(j, u, s):
                    act.wait_ge(c_max, it * (NS * PAIRS) + j * NS + s + 1)
                    act.activation(cprob[:, s % 2, :], bank(s % 2), ACT.Exp, bias=nmax[:, s:s + 1],
                                   accum_out=rsum[:, u, s:s + 1]).then_inc(c_exp, 1)

                def context(j):
                    act.wait_ge(ctT_ps, it * PAIRS + j + 1)
                    act.wait_ge(cols_ready, 5)
                    act.activation(CTs[:, :], bank(6), ACT.Identity, bias=cols[:, bass.ds(R_BV + j, 1)])\
                        .then_inc(ctT_ready, 1)

                def pair(j, u, first=False, more=True):
                    for s in range(NS):
                        if s + 1 < NS:
                            exps(j, u, s + 1)
                        elif more:
                            exps(j + 1, 1 - u, 0)
                        if s % 2:
                            act.wait_ge(cT_ps, it * (NS * PAIRS) + j * NS + s + 1)
                            copy(cprobT[:, 1, :], bank(3)).then_inc(cT_odd, 1)
                        if s == 1 and more:
                            queries(j + 1, 1 - u, 7)
                        if s == 2 and not first:
                            context(j - 1)
                        if s == 3 and more:
                            keys(j + 1, 1 - u, 7, 0)
                        if s == 5 and more:
                            keys(j + 1, 1 - u, 7, 1)

                queries(0, 0, 7)
                keys(0, 0, 6, 0)
                keys(0, 0, 3, 1)
                exps(0, 0, 0)
                pair(0, 0, first=True)
                with act.Fori(0, PAIRS // 2 - 1) as jj:
                    pair(2 * jj + 1, 1)
                    pair(2 * jj + 2, 0)
                pair(PAIRS - 1, 1, more=False)
                context(PAIRS - 1)

            def mixture_top2(it):
                x_turned(it, 5)
                act.wait_ge(e1_arg, it + 1)
                act.activation(ex1[:, :, :], ex1[:, :, :], ACT.Exp).then_inc(e1_exp, 1)
                for b in range(GROUP):
                    act.wait_ge(xb_ps, it * GROUP + b + 1)
                    copy(xb[:, b, :], ps[:, 3 + b, 0:SLOTS]).then_inc(xb_ready, 1)
                act.wait_ge(combT_ps, it + 1)
                for k in range(SB):
                    n = min(P, SLOTS - k * P)
                    last = copy(combT[0:n, k, :], ps[0:n, 5 + k, :])
                last.then_inc(combT_ready, 1)

                def relu(e):
                    act.wait_ge(hid_biased, it * E + e + 1)
                    act.activation(hid[:, e % 2, :, :], hpre[:, e % 2, :, :], ACT.Relu).then_inc(hid_ready, 1)

                relu(0)
                for e in range(E):
                    if e + 1 < E:
                        relu(e + 1)
                    act.wait_ge(y_ps, it * E + e + 1)
                    act.activation(yT[:, :, e * CAP:(e + 1) * CAP],
                                   ps[:, 2 + e % 2, 0:GROUP * CAP].rearrange("p (b c) -> p b c", b=GROUP),
                                   ACT.Identity, bias=col(R_B2 + e)).then_inc(y_ready, 1)
                for b in range(GROUP):
                    act.wait_ge(ysl_ps, it * GROUP + b + 1)
                    for k in range(SB):
                        n = min(P, SLOTS - k * P)
                        last = copy(ySl[0:n, b, k, :], ps[0:n, 5 + b, k * D:(k + 1) * D])
                    last.then_inc(ysl_ready, 1)

            with act.Fori(0, ITERS) as it:
                recurrent(it)
                memory(it)
                mixture_top1(it)
                sparse_attention(it)
                cross_attention(it)
                mixture_top2(it)

        @block.gpsimd
        def _(pool):
            pool.memset(ident[:, :], 0.0)
            pool.memset(causal_f[:, :], 0.0)
            pool.memset(sparse_f[:, :, :], 0.0)
            pool.memset(before_f[:, :], 1.0)
            pool.memset(ones_bf[:, :], 1.0)
            pool.memset(ones[:, :], 1.0)
            pool.memset(pick_f[:, :, :], 0.0)
            pool.memset(head_mask[:, :], 1.0)
            pool.memset(neg_half[:, :], -0.5)
            pool.memset(eps_ln[:, :], 1e-5)
            pool.memset(eps_rms[:, :], 1e-6)
            pool.memset(eps_post[:, :], 1e-12)
            pool.iota(iota_ei[:, :], pattern=[[1, E]], base=0, channel_multiplier=0)
            pool.iota(iota_ci[:, :], pattern=[[1, CAP]], base=1, channel_multiplier=0)
            pool.drain()

            def select(m, op, fill, base, pattern, cm):
                pool.affine_select(out=m, in_=m, compare_op=op, fill=fill, base=base, pattern=pattern,
                                   channel_multiplier=cm)

            select(ident[:, :], ALU.not_equal, 1.0, 0, [[-1, P]], 1)
            select(causal_f[:, :], ALU.is_ge, MASKED, 0, [[-1, P]], 1)
            for tq in range(QT):
                select(sparse_f[:, tq, :], ALU.is_ge, MASKED, tq * CB, [[-1, KW]], 1)
            select(before_f[:, :], ALU.is_ge, 0.0, -1, [[1, P]], -1)
            select(pick_f[:, :, :], ALU.not_equal, 1.0, 0, [[-1, E], [0, P]], 1)
            select(head_mask[:, :], ALU.is_ge, 0.0, 0, [[-HD, NH]], 1)
            pool.drain()
            select(head_mask[:, :], ALU.is_ge, 0.0, HD - 1, [[HD, NH]], -1)
            for dst, src in ((ident_bf, ident), (causal, causal_f), (before, before_f), (iota_e, iota_ei),
                             (iota_c, iota_ci)):
                pool.tensor_copy(dst[:, :], src[:, :])
            pool.tensor_copy(pick[:, :, :], pick_f[:, :, :])
            pool.tensor_copy(sparse[:, :], sparse_f[:, :, :].rearrange("p a b -> p (a b)"))
            pool.drain().then_inc(consts_ready, 1)

            def rstd_of(it, n, var, eps):
                pool.wait_ge(var_ready, it * LNS + n)
                pool.tensor_tensor(vare[:, :], var, eps[:, :], ALU.add)
                pool.drain()
                pool.tensor_tensor(rstd[:, :], vare[:, :], neg_half[:, :], ALU.pow).then_inc(rstd_ready, 1)

            variance = mv[:, :, 1:2].rearrange("p t o -> p (t o)")

            def stage(it, j):
                pool.tensor_copy(wq_s[:, :], xwT[:, 0, bass.ds(j, 1), :])
                pool.tensor_copy(wk_s[:, :], xwT[:, 1, bass.ds(j, 1), :])
                pool.drain().then_inc(staged, 1)

            pool.wait_ge(wT_sb, N_SETUP)
            pool.wait_ge(cols_ready, 5)
            with pool.Fori(0, ITERS) as it:
                rstd_of(it, 1, variance, eps_ln)
                pool.wait_ge(wkv_exp, it * 4 + 2)
                pool.tensor_tensor(b2v[:, :, :], ex[:, 1, :, :], vS[:, :, :], ALU.mult).then_inc(b2v_ready, 1)
                pool.wait_ge(wkv_exp, it * 4 + 4)
                pool.tensor_tensor(bv_[:, :, :], ex[:, 3, :, :], vS[:, :, :], ALU.mult).then_inc(bv_ready, 1)
                rstd_of(it, 2, variance, eps_ln)
                for h in range(HT):
                    pool.wait_ge(kf_relu, it * HT + h + 1)
                    pool.tensor_tensor(big2[:, h, :], big[:, h, :], big[:, h, :], ALU.mult).then_inc(kf_ready, 1)
                rstd_of(it, 3, variance, eps_ln)
                pool.wait_ge(ssq_ready, it + 1)
                pool.tensor_tensor(vare[:, :], ssq[:, :], eps_rms[:, :], ALU.add)
                pool.drain()
                pool.tensor_tensor(rstd[:, :], vare[:, :], neg_half[:, :], ALU.pow).then_inc(rms_ready, 1)
                pool.wait_ge(nhat_ready, it + 1)
                for t in range(TT):
                    last = pool.tensor_tensor(nTok[:, t, :], NHAT[:, t, :], normw_bc[:, :], ALU.mult)
                last.then_inc(ntok_ready, 1)
                rstd_of(it, 4, variance, eps_ln)
                rstd_of(it, 5, variance, eps_post)
                rstd_of(it, 6, variance, eps_ln)
                stage(it, 0)
                rstd_of(it, 7, variance, eps_ln)
                with pool.Fori(0, PAIRS - 1) as j:
                    pool.wait_ge(k_ps, it * (2 * PAIRS) + 2 * j + 2)
                    stage(it, j + 1)
                rstd_of(it, 8, variance, eps_ln)
                rstd_of(it, 9, variance, eps_ln)

        @block.vector
        def _(dve):
            def layer_norm(it, n, src, dst):
                for t in range(TT):
                    dve.bn_stats(bn[:, t, :], src[:, t, :])
                dve.drain()
                for t in range(TT):
                    last = dve.bn_aggr(mv[:, t, :], bn[:, t, :])
                last.then_inc(var_ready, 1)
                dve.wait_ge(rstd_ready, it * LNS + n)
                for t in range(TT):
                    last = dve.tensor_scalar(dst[:, t, :], src[:, t, :], mv[:, t, 0:1], rstd[:, t:t + 1],
                                             ALU.subtract, ALU.mult)
                return last

            def token_shift(rows_of):
                now, prev = hT[:, :, 1:SEQ + 1], hT[:, :, 0:SEQ]
                dve.tensor_tensor(dT[:, :, :], now, prev, ALU.subtract)
                dve.drain()
                for z, r in rows_of:
                    for b in range(GROUP):
                        last = dve.scalar_tensor_tensor(out=z[:, b, :], in0=dT[:, b, :], scalar=col(r),
                                                        in1=hT[:, b, 0:SEQ], op0=ALU.mult, op1=ALU.add)
                    last.then_inc(mix_ready, 1)

            dve.memset(hT[:, :, 0:1], 0.0).then_inc(out_stored, 1)
            dve.memset(o_max[:, :, 0:1], -1e38).then_inc(so_ready, 1)
            dve.memset(p_num[:, :, 0:1], 0.0).then_inc(so_ready, 1)
            dve.memset(q_den[:, :, 0:1], 0.0)
            dve.memset(w_bc[:, :], 0.0)
            dve.wait_ge(cols_ready, 1)
            dve.tensor_scalar(decay_w[:, :], decay_e[:, :], -1.0, None, ALU.mult).then_inc(cols_ready, 1)
            dve.tensor_scalar(bq_scaled[:, :], cols[:, R_BQ:R_BQ + PAIRS], float(DK) ** -0.5, None, ALU.mult)\
                .then_inc(cols_ready, 1)
            dve.tensor_scalar(battq_scaled[:, :], col(R_BATT), float(HD) ** -0.5, None, ALU.mult)\
                .then_inc(cols_ready, 1)
            dve.drain()
            dve.tensor_scalar(w_bc[:, :], w_bc[:, :], decay_w[:, 0:1], None, ALU.add).then_inc(cols_ready, 1)
            dve.drain()

            def recurrent(it):
                dve.wait_ge(x_loaded, it * 16 + 16)
                layer_norm(it, 1, X0, NHAT).then_inc(xhat_ready, 1)
                dve.wait_ge(hT_ready, it * 2 + 1)
                token_shift(((zk, R_MK), (zv, R_MV), (zr, R_MR)))
                dve.wait_ge(kvr_ready, it * 3 + 1)
                for b in range(GROUP):
                    dve.tensor_tensor_scan(o_max[:, b, 1:SEQ + 1], w_bc[:, :], kS[:, b, :], -1e38, ALU.add, ALU.max)
                dve.drain()
                for b in range(GROUP):
                    last = dve.scalar_tensor_tensor(out=ex[:, 0, b, :], in0=o_max[:, b, 0:SEQ], scalar=decay_w[:, 0:1],
                                                    in1=o_max[:, b, 1:SEQ + 1], op0=ALU.add, op1=ALU.subtract)
                last.then_inc(wkv_arg, 1)
                dve.tensor_tensor(ex[:, 1, :, :], kS[:, :, :], o_max[:, :, 1:SEQ + 1], ALU.subtract)\
                    .then_inc(wkv_arg, 1)
                for b in range(GROUP):
                    dve.scalar_tensor_tensor(out=o_new[:, b, :], in0=kS[:, b, :], scalar=col(R_FIRST),
                                             in1=o_max[:, b, 0:SEQ], op0=ALU.add, op1=ALU.max)
                dve.drain()
                dve.tensor_tensor(ex[:, 2, :, :], o_max[:, :, 0:SEQ], o_new[:, :, :], ALU.subtract)\
                    .then_inc(wkv_arg, 1)
                dve.scalar_tensor_tensor(out=ex[:, 3, :, :], in0=kS[:, :, :], scalar=col(R_FIRST), in1=o_new[:, :, :],
                                         op0=ALU.add, op1=ALU.subtract).then_inc(wkv_arg, 1)
                dve.wait_ge(wkv_exp, it * 4 + 2)
                for b in range(GROUP):
                    dve.tensor_tensor_scan(q_den[:, b, 1:SEQ + 1], ex[:, 0, b, :], ex[:, 1, b, :], 0.0, ALU.mult, ALU.add)
                dve.wait_ge(b2v_ready, it + 1)
                for b in range(GROUP):
                    dve.tensor_tensor_scan(p_num[:, b, 1:SEQ + 1], ex[:, 0, b, :], b2v[:, b, :], 0.0, ALU.mult, ALU.add)
                dve.drain()
                dve.wait_ge(wkv_exp, it * 4 + 4)
                dve.tensor_tensor(t_den[:, :, :], ex[:, 2, :, :], q_den[:, :, 0:SEQ], ALU.mult)
                dve.tensor_tensor(t_num[:, :, :], ex[:, 2, :, :], p_num[:, :, 0:SEQ], ALU.mult)
                dve.drain()
                dve.tensor_tensor(t_den[:, :, :], t_den[:, :, :], ex[:, 3, :, :], ALU.add)
                dve.wait_ge(bv_ready, it + 1)
                dve.tensor_tensor(t_num[:, :, :], t_num[:, :, :], bv_[:, :, :], ALU.add)
                dve.drain()
                dve.reciprocal(rec[:, :, :], t_den[:, :, :])
                dve.wait_ge(kvr_ready, it * 3 + 3)
                dve.tensor_tensor(t_num[:, :, :], t_num[:, :, :], rS[:, :, :], ALU.mult)
                dve.drain()
                dve.tensor_tensor(rec[:, :, :], rec[:, :, :], t_num[:, :, :], ALU.mult).then_inc(wkv_ready, 1)
                dve.wait_ge(att_ps, it + 1)
                dve.tensor_tensor(X1[:, :, :], X0[:, :, :], tiles(4), ALU.add)
                dve.drain()
                layer_norm(it, 2, X1, NHAT).then_inc(xhat_ready, 1)
                dve.wait_ge(hT_ready, it * 2 + 2)
                token_shift(((zk, R_FMK), (zr, R_FMR)))
                dve.wait_ge(rf_ready, it + 1)
                dve.wait_ge(ffn_ps, it + 1)
                dve.tensor_tensor(Y[:, :, :], rf[:, :, :], tiles(7), ALU.mult)
                dve.tensor_tensor(X1[:, :, :], X1[:, :, :], X0[:, :, :], ALU.add)
                dve.drain()
                dve.tensor_tensor(Y[:, :, :], Y[:, :, :], X1[:, :, :], ALU.add)
                dve.drain()
                dve.wait_ge(out_stored, it * 16 + 1)
                layer_norm(it, 3, Y, X).then_inc(layer_done, 1)

            def memory(it):
                dve.wait_ge(rms_ready, it + 1)
                for t in range(TT):
                    last = dve.tensor_scalar(NHAT[:, t, :], X[:, t, :], rstd[:, t:t + 1], None, ALU.mult)
                last.then_inc(nhat_ready, 1)
                for t in range(TT):
                    n, lo = CTX + (t % QT + 1) * P, 2 * (t % 2) * 512
                    dve.wait_ge(lg_ps, it * TT + t + 1)
                    dve.tensor_reduce(nmax[:, t:t + 1], psf[:, lo:lo + n], AX.X, ALU.max, negate=True)\
                        .then_inc(lg_max, 1)
                dve.wait_ge(lg_exp, it * TT + TT)
                dve.reciprocal(rinv[:, 0:TT], rsum[:, 0, 0:TT])
                dve.drain()
                dve.wait_ge(av_ps, it + 1)
                for t in range(TT):
                    dve.scalar_tensor_tensor(out=Y[:, t, :], in0=ps[:, 6, t * D:(t + 1) * D], scalar=rinv[:, t:t + 1],
                                             in1=X[:, t, :], op0=ALU.mult, op1=ALU.subtract)
                dve.drain()
                dve.wait_ge(alpha_ready, it + 1)
                dve.tensor_tensor(Y[:, :, :], Y[:, :, :], alpha[:, :, :], ALU.mult)
                dve.drain()
                dve.scalar_tensor_tensor(out=Y[:, :, :], in0=X[:, :, :], scalar=2.0, in1=Y[:, :, :],
                                         op0=ALU.mult, op1=ALU.add)
                dve.drain()
                layer_norm(it, 4, Y, X).then_inc(layer_done, 1)

            def mixture_top1(it):
                dve.wait_ge(route_ps, it + 1)
                dve.tensor_copy(lg[:, :, :], ps[:, 1, 0:TT * E].rearrange("p (t e) -> p t e", t=TT))
                dve.drain()
                for t in range(TT):
                    dve.max(top[:, t, :], lg[:, t, :])
                dve.drain()
                for t in range(TT):
                    dve.max_index(topi[:, t, :], top[:, t, :], lg[:, t, :])
                dve.drain()
                dve.tensor_copy(topf[:, :, 0:1], topi[:, :, 0:1])
                dve.drain()
                for t in range(TT):
                    last = dve.tensor_scalar(onehot[:, t, :], iota_e[:, :], topf[:, t, 0:1], None, ALU.is_equal)
                last.then_inc(onehot_ready, 1)
                dve.wait_ge(xT_ready, it * 5 + 2)
                for e in range(E):
                    dve.wait_ge(pick_ps, it * E + e + 1)
                    dve.tensor_tensor(XE[:, e % 2, :], XT[:, :], bank(3 + e % 2), ALU.mult).then_inc(xe_ready, 1)
                dve.wait_ge(moe_ps, it + 1)
                dve.tensor_tensor(Y[:, :, :], X[:, :, :], tiles(1), ALU.add)
                dve.drain()
                layer_norm(it, 5, Y, Y)
                dve.drain()
                for t in range(TT):
                    dve.tensor_tensor(Y[:, t, :], Y[:, t, :], gamma_bc[:, :], ALU.mult)
                dve.tensor_tensor(X1[:, 0, :], X[:, 0, :], beta_bc[:, :], ALU.add)
                for t in range(1, TT):
                    dve.tensor_tensor(X1[:, t, :], X[:, t, :], beta_bc[:, :], ALU.add)
                dve.drain()
                dve.tensor_tensor(Y[:, :, :], Y[:, :, :], X1[:, :, :], ALU.add)
                dve.drain()
                layer_norm(it, 6, Y, X).then_inc(layer_done, 1)

            def sparse_attention(it):
                def mask_head(hh, u):
                    dve.tensor_scalar(qm[:, u, :], qT[:, :], head_mask[:, bass.ds(2 * hh + u, 1)], None, ALU.mult)\
                        .then_inc(qm_ready, 1)

                def row_max(hh, u):
                    dve.wait_ge(s_ps, it * NH + 2 * hh + u + 1)
                    dve.tensor_reduce(snm[:, u, :].rearrange("p (b t) -> p b t", b=GROUP),
                                      ps[:, 2 * u:2 * u + 2, 0:QT * KW].rearrange("p b (t k) -> p b t k", t=QT),
                                      AX.X, ALU.max, negate=True).then_inc(s_max, 1)

                def turned(hh, u):
                    dve.wait_ge(sT_ps, it * NH + 2 * hh + u + 1)
                    dve.reciprocal(sri[:, u, :], srs[:, u, :])
                    dve.tensor_copy(spTs[:, u, :, :], ps[0:CB, 6 + u, 0:GROUP * P].rearrange("p (b q) -> p b q", b=GROUP))\
                        .then_inc(sTs_ready, 1)

                def normalise(hh, u):
                    dve.wait_ge(so_ps, it * NH + 2 * hh + u + 1)
                    c = GROUP * P
                    dve.tensor_tensor(O[:, :, bass.ds((2 * hh + u) * HD, HD)],
                                      ps[:, 6 + u, c:c + TT * HD].rearrange("p (t d) -> p t d", t=TT),
                                      sri[:, u, :].unsqueeze(2).to_broadcast([P, TT, HD]), ALU.mult)\
                        .then_inc(so_ready, 1)

                def two_heads(hh, more, masks):
                    turned(hh, 0)
                    if more:
                        row_max(hh + 1, 0)
                    if masks:
                        mask_head(hh + 2, 0)
                    turned(hh, 1)
                    normalise(hh, 0)
                    if more:
                        row_max(hh + 1, 1)
                    if masks:
                        mask_head(hh + 2, 1)
                    normalise(hh, 1)

                dve.wait_ge(qk_ready, it * 2 + 1)
                mask_head(0, 0)
                mask_head(0, 1)
                for u in range(2):
                    row_max(0, u)
                    mask_head(1, u)
                with dve.Fori(0, NH // 2 - 2) as hh:
                    two_heads(hh, True, True)
                two_heads(NH // 2 - 2, True, False)
                two_heads(NH // 2 - 1, False, False)
                dve.wait_ge(proj_ps, it + 1)
                dve.tensor_tensor(Y[:, :, :], X[:, :, :], tiles(1), ALU.add)
                dve.drain()
                layer_norm(it, 7, Y, X).then_inc(layer_done, 1)

            def cross_attention(it):
                def context_values(j, u, b, seq):
                    dve.wait_ge(vx_ps, it * (2 * PAIRS) + 2 * j + seq + 1)
                    dve.tensor_copy(Vx[u][:, seq * KT:(seq + 1) * KT, :], tiles(b)).then_inc(vx_ready, 1)

                def row_max(j, s):
                    dve.wait_ge(c_ps, it * (NS * PAIRS) + j * NS + s + 1)
                    dve.tensor_reduce(nmax[:, s:s + 1], bank(s % 2), AX.X, ALU.max, negate=True)\
                        .then_inc(c_max, 1)

                def turned(j, s):
                    dve.wait_ge(cT_ps, it * (NS * PAIRS) + j * NS + s + 1)
                    dve.tensor_copy(cprobT[:, 0, :], bank(2)).then_inc(cT_even, 1)

                def normalise(j, u):
                    dve.wait_ge(o_ps, it * PAIRS + j + 1)
                    for h in range(2):
                        last = dve.tensor_tensor(
                            Cx[:, :, h * DK:(h + 1) * DK], tiles(4 + u)[:, :, h * DK:(h + 1) * DK],
                            rinv[:, h * TT:(h + 1) * TT].unsqueeze(2).to_broadcast([P, TT, DK]), ALU.mult)
                    last.then_inc(o_ready, 1)

                def add_projected(j, b):
                    dve.wait_ge(wo_ps, it * PAIRS + j + 1)
                    dve.tensor_tensor(X1[:, :, :], X1[:, :, :], tiles(b), ALU.add).then_inc(wo_added, 1)

                def pair(j, u, first=False, more=True):
                    for s in range(NS):
                        if s == 0 and not first:
                            normalise(j - 1, 1 - u)
                        if s % 2 == 0:
                            turned(j, s)
                        if s == 4 and not first:
                            add_projected(j - 1, 6)
                        if s == 6 and more:
                            context_values(j + 1, 1 - u, 6, 0)
                        if s == 7 and more:
                            context_values(j + 1, 1 - u, 7, 1)
                        if s + 2 < NS:
                            row_max(j, s + 2)
                        elif more:
                            row_max(j + 1, s + 2 - NS)
                    dve.wait_ge(c_exp, it * (NS * PAIRS) + (j + 1) * NS)
                    dve.reciprocal(rinv[:, :], rsum[:, u, :])
                    dve.drain()

                dve.drain()
                dve.tensor_copy(X1[:, :, :], X[:, :, :]).then_inc(wo_added, 1)
                context_values(0, 0, 4, 0)
                context_values(0, 0, 5, 1)
                row_max(0, 0)
                row_max(0, 1)
                pair(0, 0, first=True)
                with dve.Fori(0, PAIRS // 2 - 1) as jj:
                    pair(2 * jj + 1, 1)
                    pair(2 * jj + 2, 0)
                pair(PAIRS - 1, 1, more=False)
                normalise(PAIRS - 1, 1)
                add_projected(PAIRS - 1, 7)
                dve.drain()
                layer_norm(it, 8, X1, X).then_inc(layer_done, 1)

            def mixture_top2(it):
                dve.wait_ge(r1_ps, it + 1)
                dve.tensor_copy(lg[:, :, :], ps[:, 1, 0:TT * E].rearrange("p (t e) -> p t e", t=TT))
                dve.drain()
                for t in range(TT):
                    dve.max(top[:, t, :], lg[:, t, :])
                dve.drain()
                dve.tensor_tensor(ex1[:, :, :], lg[:, :, :], top[:, :, 0:1].to_broadcast([P, TT, E]), ALU.subtract)\
                    .then_inc(e1_arg, 1)
                for t in range(TT):
                    dve.max_index(topi[:, t, :], top[:, t, :], lg[:, t, :])
                dve.drain()
                dve.tensor_copy(topf[:, :, :], topi[:, :, 0:2])
                dve.drain()
                for t in range(TT):
                    dve.tensor_scalar(A[:, t, :], iota_e[:, :], topf[:, t, 0:1], None, ALU.is_equal)
                    dve.tensor_scalar(onehot[:, t, :], iota_e[:, :], topf[:, t, 1:2], None, ALU.is_equal)
                dve.drain()
                dve.tensor_tensor(A[:, :, :], A[:, :, :], onehot[:, :, :], ALU.add)
                dve.drain()
                dve.tensor_copy(A_bf[:, :, :], A[:, :, :]).then_inc(two_hot, 1)
                dve.wait_ge(e1_exp, it + 1)
                dve.tensor_reduce(esum[:, :], ex1[:, :, :], AX.X, ALU.add)
                dve.drain()
                dve.reciprocal(einv[:, :], esum[:, :])
                dve.drain()
                dve.tensor_tensor(ex1[:, :, :], ex1[:, :, :], einv[:, :].unsqueeze(2).to_broadcast([P, TT, E]), ALU.mult)
                dve.wait_ge(pos_ps, it + 1)
                dve.scalar_tensor_tensor(out=posA[:, :, :], in0=ps[:, 2, 0:TT * E].rearrange("p (t e) -> p t e", t=TT),
                                         scalar=1.0, in1=A[:, :, :], op0=ALU.add, op1=ALU.mult)
                dve.drain()

                def slots(m, t):
                    return m[:, t, :].rearrange("p (e c) -> p e c", e=E)

                def per_expert(m, t):
                    return m[:, t, :].unsqueeze(2).to_broadcast([P, E, CAP])

                for t in range(TT):
                    last = dve.tensor_tensor(slots(disp, t), iota_c[:, :].unsqueeze(1).to_broadcast([P, E, CAP]),
                                             per_expert(posA, t), ALU.is_equal)
                last.then_inc(disp_ready, 1)
                dve.drain()
                for t in range(TT):
                    last = dve.tensor_tensor(slots(comb, t), slots(disp, t), per_expert(ex1, t), ALU.mult)
                last.then_inc(comb_ready, 1)
                W = GROUP * CAP
                for e in range(E):
                    dve.wait_ge(hid_ps, it * E + e + 1)
                    if e >= 2:
                        dve.wait_ge(hid_ready, it * E + e - 1)
                    dve.tensor_tensor(hpre[:, e % 2, :, :], ps[:, e % 2, 0:HT * W].rearrange("p (h w) -> p h w", h=HT),
                                      cols[:, R_B1 + e * HT:R_B1 + (e + 1) * HT].unsqueeze(2).to_broadcast([P, HT, W]),
                                      ALU.add).then_inc(hid_biased, 1)
                dve.wait_ge(comb_ps, it + 1)
                dve.tensor_tensor(Y[:, :, :], X[:, :, :], tiles(4), ALU.add)
                dve.drain()
                layer_norm(it, 9, Y, X).then_inc(layer_done, 1)

            with dve.Fori(0, ITERS) as it:
                recurrent(it)
                memory(it)
                mixture_top1(it)
                sparse_attention(it)
                cross_attention(it)
                mixture_top2(it)


_INS = [
    'x', 'ctx_1024', 'L0_attn_ln_att_g', 'L0_attn_ln_att_b', 'L0_attn_ln_ffn_g', 'L0_attn_ln_ffn_b',
    'L0_attn_att_time_decay', 'L0_attn_att_time_first', 'L0_attn_att_mix_k', 'L0_attn_att_mix_v',
    'L0_attn_att_mix_r', 'L0_attn_att_wk', 'L0_attn_att_wv', 'L0_attn_att_wr', 'L0_attn_att_wo',
    'L0_attn_ffn_mix_k', 'L0_attn_ffn_mix_r', 'L0_attn_ffn_wk', 'L0_attn_ffn_wv', 'L0_attn_ffn_wr',
    'L0_xattn_q_w', 'L0_xattn_k_w', 'L0_xattn_norm_w', 'L0_xattn_gate_w', 'L0_xattn_gate_b',
    'L0_ffn_Wr', 'L0_ffn_W1', 'L0_ffn_b1', 'L0_ffn_Wo', 'L0_ffn_bo', 'L0_ffn_gamma', 'L0_ffn_beta',
    'L1_attn_W_attn', 'L1_attn_b_attn', 'L1_attn_W_proj', 'L1_attn_b_proj',
    'L1_xattn_Wq', 'L1_xattn_bq', 'L1_xattn_Wk', 'L1_xattn_bk', 'L1_xattn_Wv', 'L1_xattn_bv', 'L1_xattn_Wo',
    'L1_ffn_Wr', 'L1_ffn_br', 'L1_ffn_W1', 'L1_ffn_b1', 'L1_ffn_W2', 'L1_ffn_b2',
]


def kernel(**inputs):
    import numpy as _np
    import concourse.bacc as _bacc
    from concourse import mybir as _mybir
    from concourse.bass_utils import run_bass_kernel_spmd as _run

    nc = _bacc.Bacc("TRN2", target_bir_lowering=False, num_devices=1)
    arrays, args = {}, []
    for name in _INS:
        a = _np.ascontiguousarray(inputs[name])
        arrays[f"in_{name}_dram"] = a
        args.append(nc.dram_tensor(f"in_{name}_dram", a.shape, _mybir.dt.from_np(a.dtype), kind="ExternalInput").ap())
    out = nc.dram_tensor("out_0_dram", (BATCH, SEQ, D), F32, kind="ExternalOutput").ap()
    decoder_kernel(nc, *args, out)
    r = _run(nc, [arrays], core_ids=[0])
    return r.results[0]["out_0_dram"]
```

```python
from contextlib import ExitStack

import concourse.bass as bass
from concourse import mybir

F32 = mybir.dt.float32
BF16 = mybir.dt.bfloat16
U32 = mybir.dt.uint32
ALU = mybir.AluOpType
ACT = mybir.ActivationFunctionType
AX = mybir.AxisListType

P = 128
D = 128
BATCH, SEQ, CTX = 8, 256, 512
GROUP = 2
ITERS = BATCH // GROUP
TOK = GROUP * SEQ
TT = TOK // P
QT = SEQ // P
KT = CTX // P
CT = GROUP * KT
LIN = 512
HT = LIN // P
E = 8
NH, HD = 16, 8
CB = 8
KW = CB + P
XH, DK = 16, 64
PAIRS = XH // 2
CAP = max(1, int(SEQ / E * 1.25))
SLOTS = E * CAP
SB = (SLOTS + P - 1) // P
MASKED = -1.0e30

R_LNG, R_LNB, R_FLNG, R_FLNB, R_DECAY, R_FIRST, R_MK, R_MV, R_MR, R_FMK, R_FMR, R_NORMW = range(12)
R_BATT = 12
R_BQ = 14
R_BK = R_BQ + PAIRS
R_BV = R_BK + PAIRS
R_B1 = R_BV + PAIRS
R_B2 = R_B1 + E * HT
N_COL = R_B2 + E

V_GATEB, V_BV, V_BO, V_BPROJ, V_GAMMA, V_BETA, V_NORMW = range(7)
V_BR = 7 * D
N_ROW = V_BR + E


def decoder_kernel(
    nc, x, ctx_in,
    ln_att_g, ln_att_b, ln_ffn_g, ln_ffn_b, time_decay, time_first, mix_k, mix_v, mix_r,
    att_wk, att_wv, att_wr, att_wo, ffn_mix_k, ffn_mix_r, ffn_wk, ffn_wv, ffn_wr,
    q_w, k_w, norm_w, gate_w, gate_b,
    m0_wr, m0_w1, m0_b1, m0_wo, m0_bo, m0_gamma, m0_beta,
    a1_w, a1_b, a1_wp, a1_bp,
    x1_wq, x1_bq, x1_wk, x1_bk, x1_wv, x1_bv, x1_wo,
    m1_wr, m1_br, m1_w1, m1_b1, m1_w2, m1_b2,
    out,
):
    with ExitStack() as stack:
        def sb(name, shape, dt=F32):
            return stack.enter_context(nc.sbuf_tensor(name, shape, dt))

        def semaphore(name):
            return stack.enter_context(nc.semaphore(name))

        wk, wv, wr, wo = (sb(n, [P, D]) for n in ("wk", "wv", "wr", "wo"))
        fwk = sb("fwk", [P, LIN])
        fwv = sb("fwv", [P, HT, D])
        fwr = sb("fwr", [P, D])
        qw, kw, gw_raw = (sb(n, [P, D]) for n in ("qw", "kw", "gw_raw"))
        qk_fold = sb("qk_fold", [P, D])
        gwT = sb("gwT", [P, D])
        wr0_raw = sb("wr0_raw", [E, D])
        wr0T = sb("wr0T", [P, E])
        w1a = sb("w1a", [P, E, LIN])
        b1a = sb("b1a", [E, LIN])
        wo0 = sb("wo0", [P, HT, D])
        wattn = sb("wattn", [P, 3 * D])
        wproj = sb("wproj", [P, D])
        xwT = sb("xwT", [P, 4, PAIRS, D])
        wr1 = sb("wr1", [P, E])
        w1b = sb("w1b", [P, E, LIN])
        w2b = sb("w2b", [P, E, HT, D])
        col_rows = sb("col_rows", [N_COL, D])
        cols = sb("cols", [P, N_COL])
        decay_w = sb("decay_w", [P, 1])
        decay_e = sb("decay_e", [P, 1])
        bq_scaled = sb("bq_scaled", [P, PAIRS])
        battq_scaled = sb("battq_scaled", [P, 1])
        rows = sb("rows", [1, N_ROW])
        gamma_bc, beta_bc, normw_bc, bo_bc = (sb(n, [P, D]) for n in ("gamma_bc", "beta_bc", "normw_bc", "bo_bc"))

        ident = sb("ident", [P, P])
        ident_bf = sb("ident_bf", [P, P], BF16)
        causal = sb("causal", [P, P], BF16)
        sparse = sb("sparse", [P, QT * KW], BF16)
        before = sb("before", [P, P], BF16)
        ones_bf = sb("ones_bf", [P, P], BF16)
        ones = sb("ones", [1, P])
        pick = sb("pick", [E, E, P], BF16)
        head_mask = sb("head_mask", [P, NH])
        iota_e = sb("iota_e", [P, E])
        iota_ei = sb("iota_ei", [P, E], mybir.dt.int32)
        iota_c = sb("iota_c", [P, CAP])
        iota_ci = sb("iota_ci", [P, CAP], mybir.dt.int32)
        neg_half = sb("neg_half", [P, TT])
        eps_ln = sb("eps_ln", [P, TT])
        eps_rms = sb("eps_rms", [P, TT])
        eps_post = sb("eps_post", [P, TT])

        arena = sb("arena", [P, 17 * TOK])

        class Carve:

            def __init__(self):
                self.at = 0

            def __call__(self, *shape, parts=P):
                n = 1
                for k in shape:
                    n *= k
                view = arena[0:parts, self.at:self.at + n]
                self.at += n
                assert self.at <= 17 * TOK
                if len(shape) == 2:
                    return view.rearrange("p (a b) -> p a b", b=shape[1])
                if len(shape) == 3:
                    return view.rearrange("p (a b c) -> p a b c", b=shape[1], c=shape[2])
                return view

        setup, att_c, sparse_c, cross_c, mix_c = (Carve() for _ in range(5))
        xw_raw = setup(4, PAIRS, D)
        causal_f, before_f = setup(P), setup(P)
        sparse_f = setup(QT, KW)
        pick_f = setup(E, P, parts=E)

        X0 = sb("X0", [P, TT, D])
        X1 = sb("X1", [P, TT, D])
        X = sb("X", [P, TT, D])
        Y = sb("Y", [P, TT, D])
        NHAT = sb("NHAT", [P, TT, D])
        XT = sb("XT", [P, TOK])
        ctx = sb("ctx", [P, CT, D])
        ctxT = sb("ctxT", [P, CT * P])
        bn = sb("bn", [P, TT, 6])
        mv = sb("mv", [P, TT, 2])
        vare = sb("vare", [P, TT])
        rstd = sb("rstd", [P, TT])
        hT = sb("hT", [P, GROUP, SEQ + 1])
        o_max, p_num, q_den = (sb(n, [P, GROUP, SEQ + 1]) for n in ("o_max", "p_num", "q_den"))
        w_bc = sb("w_bc", [P, SEQ])
        big = sb("big", [P, HT, TOK])
        big2 = sb("big2", [P, HT, TOK])
        rf = sb("rf", [P, TT, D])
        junk = sb("junk", [P, D])
        ssq, ssq_eps, rms_inv = (sb(n, [P, TT]) for n in ("ssq", "ssq_eps", "rms_inv"))
        nT = sb("nT", [P, TOK])
        nTok = sb("nTok", [P, TT, D])
        qpT = sb("qpT", [P, TOK])
        alpha = sb("alpha", [P, TT, D])
        prob = att_c(2, CTX + SEQ)
        probT = att_c(2, CTX + SEQ)
        nmax = sb("nmax", [P, 8])
        rsum = sb("rsum", [P, 2, 8])
        rinv = sb("rinv", [P, 8])
        lg = sb("lg", [P, TT, E])
        top = sb("top", [P, TT, E])
        topi = sb("topi", [P, TT, E], U32)
        topf = sb("topf", [P, TT, 2])
        onehot = sb("onehot", [P, TT, E])
        ohT = sb("ohT", [E, TOK])
        ohT_bf = sb("ohT_bf", [E, TOK], BF16)
        XE = big2[:, 0:2, :]
        qT, kT = sb("qT", [P, TOK]), sb("kT", [P, TOK])
        V = sb("V", [P, TT, D])
        qm = sparse_c(2, TOK)
        SP_ = sparse_c(2, TT, KW)
        spT = sparse_c(2, TOK)
        XTg = sparse_c(GROUP, NH, CB)
        Vg = sparse_c(GROUP, D)
        G = sparse_c(GROUP, NH, CB)
        GT = sparse_c(GROUP, P)
        Og = sparse_c(GROUP, NH, HD)
        sri_all = sparse_c(NH, TT)
        snm = sb("snm", [P, 2, TT])
        srs = sb("srs", [P, 2, TT])
        sri = sb("sri", [P, 2, TT])
        O = sb("O", [P, TT, D])
        OT = sb("OT", [P, TOK])
        wq_s, wk_s = sb("wq_s", [P, D]), sb("wk_s", [P, D])
        cprob, cprobT = cross_c(2, CTX), cross_c(2, CTX)
        QTs = cross_c(2, TOK)
        KTs = cross_c(2, CT * P)
        Vx = [cross_c(CT, P) for _ in range(2)]
        Cx = cross_c(TT, P)
        CTs = cross_c(TOK)
        ex1 = sb("ex1", [P, TT, E])
        esum = sb("esum", [P, TT])
        einv = sb("einv", [P, TT])
        A = sb("A", [P, TT, E])
        A_bf = sb("A_bf", [P, TT, E], BF16)
        posA = sb("posA", [P, TT, E])
        disp = mix_c(TT, SLOTS)
        comb = mix_c(TT, SLOTS)
        combT = mix_c(SB, TOK)
        xb = mix_c(GROUP, SLOTS)
        hid = mix_c(2, HT, GROUP * CAP)
        yT = mix_c(GROUP, SLOTS)
        ySl = mix_c(GROUP, SB, D)

        def by_seq(view):
            return view.rearrange("p (b s) -> p b s", b=GROUP)

        def flat(view):
            return view[:, :, :].rearrange("p t d -> p (t d)")

        zk, zv, zr = by_seq(qT[:, :]), by_seq(kT[:, :]), by_seq(qpT[:, :])
        dT, kS, vS = by_seq(OT[:, :]), by_seq(nT[:, :]), by_seq(flat(V))
        rS, o_new, rec = by_seq(flat(O)), by_seq(flat(nTok)), by_seq(flat(alpha))
        ex = [by_seq(big[:, i, :]) for i in range(4)]
        b2v, bv_, t_num, t_den = (by_seq(big2[:, i, :]) for i in range(4))

        ps = stack.enter_context(nc.psum_tensor("ps", [P, 8, 512], F32))

        def bank(i):
            return ps[:, i, :]

        def tiles(i):
            return ps[:, i, :].rearrange("p (t d) -> p t d", t=TT)

        def seqs(i):
            return ps[:, i, :].rearrange("p (b s) -> p b s", b=GROUP)

        psf = ps[:, :, :].rearrange("p b n -> p (b n)")

        rec_loaded, weights_loaded = semaphore("rec_loaded"), semaphore("weights_loaded")
        consts_ready = semaphore("consts_ready")
        wT_ps = semaphore("wT_ps")
        wT_sb = semaphore("wT_sb")
        cols_ready = semaphore("cols_ready")
        x_loaded, ctx_loaded, out_stored = (semaphore(n) for n in ("x_loaded", "ctx_loaded", "out_stored"))
        RNS, LNS = 3, 6
        rvar_ready, rrstd_ready = semaphore("rvar_ready"), semaphore("rrstd_ready")
        var_ready, rstd_ready = semaphore("var_ready"), semaphore("rstd_ready")
        p_ready, tnum_ready = semaphore("p_ready"), semaphore("tnum_ready")
        xhat_ready, hT_ps, hT_ready = semaphore("xhat_ready"), semaphore("hT_ps"), semaphore("hT_ready")
        mix_ready, kvr_ps, kvr_ready = semaphore("mix_ready"), semaphore("kvr_ps"), semaphore("kvr_ready")
        wkv_arg, wkv_exp = semaphore("wkv_arg"), semaphore("wkv_exp")
        b2v_ready, bv_ready, wkv_ready = semaphore("b2v_ready"), semaphore("bv_ready"), semaphore("wkv_ready")
        att_ps = semaphore("att_ps")
        kf_ps, kf_relu, kf_ready = semaphore("kf_ps"), semaphore("kf_relu"), semaphore("kf_ready")
        rf_ps, rf_ready, ffn_ps = semaphore("rf_ps"), semaphore("rf_ready"), semaphore("ffn_ps")
        LAYERS = 5
        layer_done, out_ready = semaphore("layer_done"), semaphore("out_ready")
        xT_ps, xT_ready = semaphore("xT_ps"), semaphore("xT_ready")
        ctxT_ps, ctxT_ready = semaphore("ctxT_ps"), semaphore("ctxT_ready")
        ssq_ready, rms_ready, nhat_ready = semaphore("ssq_ready"), semaphore("rms_ready"), semaphore("nhat_ready")
        ntok_ready, nT_ps, nT_ready = semaphore("ntok_ready"), semaphore("nT_ps"), semaphore("nT_ready")
        gate_ps, alpha_ready = semaphore("gate_ps"), semaphore("alpha_ready")
        qp_ps, qp_ready = semaphore("qp_ps"), semaphore("qp_ready")
        lg_ps, lg_max, lg_exp = semaphore("lg_ps"), semaphore("lg_max"), semaphore("lg_exp")
        pT_ps, pT_ready, av_ps = semaphore("pT_ps"), semaphore("pT_ready"), semaphore("av_ps")
        route_ps, onehot_ready = semaphore("route_ps"), semaphore("onehot_ready")
        ohT_ps, ohT_ready = semaphore("ohT_ps"), semaphore("ohT_ready")
        pick_ps, xe_ready = semaphore("pick_ps"), semaphore("xe_ready")
        pre_ps, inter_ready, moe_ps = semaphore("pre_ps"), semaphore("inter_ready"), semaphore("moe_ps")
        qkv_ps, qk_ready, v_ready = semaphore("qkv_ps"), semaphore("qk_ready"), semaphore("v_ready")
        qm_ready, s_ps, s_max, s_exp = (semaphore(n) for n in ("qm_ready", "s_ps", "s_max", "s_exp"))
        sT_ps, sT_ready = semaphore("sT_ps"), semaphore("sT_ready")
        xg_ready, g_ready, gT_ps, gT_ready, og_ps = (
            semaphore(n) for n in ("xg_ready", "g_ready", "gT_ps", "gT_ready", "og_ps"))
        so_ps, so_ready = semaphore("so_ps"), semaphore("so_ready")
        oT_ps, oT_ready, proj_ps = semaphore("oT_ps"), semaphore("oT_ready"), semaphore("proj_ps")
        NS = 2 * TT
        staged = semaphore("staged")
        q_ps, k_ps, vx_ps = semaphore("q_ps"), semaphore("k_ps"), semaphore("vx_ps")
        q_ready, k_ready = semaphore("q_ready"), semaphore("k_ready")
        vx_ready = semaphore("vx_ready")
        c_ps, c_max, c_exp = (semaphore(n) for n in ("c_ps", "c_max", "c_exp"))
        cT_ps, cT_even, cT_odd = semaphore("cT_ps"), semaphore("cT_even"), semaphore("cT_odd")
        o_ps, o_ready, ctT_ps, ctT_ready = (semaphore(n) for n in ("o_ps", "o_ready", "ctT_ps", "ctT_ready"))
        wo_ps, wo_added = semaphore("wo_ps"), semaphore("wo_added")
        r1_ps, e1_arg, e1_exp = semaphore("r1_ps"), semaphore("e1_arg"), semaphore("e1_exp")
        two_hot, pos_ps, disp_ready = semaphore("two_hot"), semaphore("pos_ps"), semaphore("disp_ready")
        comb_ready, combT_ps, combT_ready = semaphore("comb_ready"), semaphore("combT_ps"), semaphore("combT_ready")
        xb_ps, xb_ready = semaphore("xb_ps"), semaphore("xb_ready")
        hid_ps, hid_ready = semaphore("hid_ps"), semaphore("hid_ready")
        y_ps, y_ready = semaphore("y_ps"), semaphore("y_ready")
        ysl_ps, ysl_ready, comb_ps = semaphore("ysl_ps"), semaphore("ysl_ready"), semaphore("comb_ps")

        def one_row(v):
            return v.rearrange("(a n) -> a n", a=1)

        def half(w, n):
            return w.rearrange("(t p) n -> p t n", p=P)

        loads = [
            (qw[:, :], q_w), (kw[:, :], k_w), (gw_raw[:, :], gate_w),
            (wr0_raw[:, :], m0_wr), (b1a[:, :], m0_b1), (wo0[:, :, :], half(m0_wo, D)),
            (wattn[:, :], a1_w), (wproj[:, :], a1_wp), (wr1[:, :], m1_wr),
            (xw_raw[:, 0, :, :], half(x1_wq, D)), (xw_raw[:, 1, :, :], half(x1_wk, D)),
            (xw_raw[:, 2, :, :], half(x1_wv, D)),
            (xw_raw[:, 3, :, :], x1_wo.rearrange("p (j f) -> p j f", f=P)),
            (w1a[:, :, :], m0_w1.rearrange("e c h -> c e h")),
            (w1b[:, :, :], m1_w1.rearrange("e c h -> c e h")),
        ] + [(w2b[:, e, :, :], half(m1_w2[e, :, :], D)) for e in range(E)]
        rec_loads = []
        for row, v in ((R_LNG, ln_att_g), (R_LNB, ln_att_b), (R_FLNG, ln_ffn_g), (R_FLNB, ln_ffn_b),
                       (R_DECAY, time_decay), (R_FIRST, time_first), (R_MK, mix_k), (R_MV, mix_v),
                       (R_MR, mix_r), (R_FMK, ffn_mix_k), (R_FMR, ffn_mix_r), (R_NORMW, norm_w)):
            rec_loads.append((col_rows[row:row + 1, :], one_row(v)))
        rec_loads += [
            (col_rows[R_BATT:R_BATT + 2, :], a1_b[0:2 * D].rearrange("(j p) -> j p", p=P)),
            (col_rows[R_BQ:R_BQ + PAIRS, :], x1_bq.rearrange("(j p) -> j p", p=P)),
            (col_rows[R_BK:R_BK + PAIRS, :], x1_bk.rearrange("(j p) -> j p", p=P)),
            (col_rows[R_BV:R_BV + PAIRS, :], x1_bv.rearrange("(j p) -> j p", p=P)),
            (col_rows[R_B1:R_B1 + E * HT, :], m1_b1.rearrange("e (h p) -> (e h) p", p=P)),
            (col_rows[R_B2:R_B2 + E, :], m1_b2),
            (wk[:, :], att_wk), (wv[:, :], att_wv), (wr[:, :], att_wr), (wo[:, :], att_wo),
            (fwk[:, :], ffn_wk), (fwv[:, :, :], half(ffn_wv, D)), (fwr[:, :], ffn_wr),
        ]
        for i, v in enumerate((gate_b, a1_b[2 * D:3 * D], m0_bo, a1_bp, m0_gamma, m0_beta, norm_w)):
            loads.append((rows[0:1, i * D:(i + 1) * D], one_row(v)))
        loads.append((rows[0:1, V_BR:V_BR + E], one_row(m1_br)))

        def row_of(i):
            return rows[0:1, i * D:(i + 1) * D]

        def col(i):
            return cols[:, i:i + 1]

        weight_turns = [([col_rows[:, :]], cols[:, :])]
        for w in range(4):
            for g in range(0, PAIRS, 4):
                weight_turns.append(([xw_raw[:, w, g + i, :] for i in range(4)], xwT[:, w, g:g + 4, :]))
        weight_turns.append(([gw_raw[:, :]], gwT[:, :]))
        weight_turns.append(([wr0_raw[:, :]], wr0T[:, :]))
        N_TURNS = len(weight_turns)
        N_SETUP = N_TURNS + 5
        SETUP_BANKS = 4

        x_v = x.rearrange("(i b) (t p) d -> i p (b t) d", b=GROUP, p=P)
        out_v = out.rearrange("(i b) (t p) d -> i p (b t) d", b=GROUP, p=P)
        ctx_v = ctx_in.rearrange("(i b) (t p) d -> i p (b t) d", b=GROUP, p=P)

        def at(view, it):
            if isinstance(it, int):
                return view[it, :, :, :]
            return view[bass.ds(it, 1), :, :, :].squeeze(0)

        block = stack.enter_context(nc.Block())

        @block.sync
        def _(sp):
            def load_x(it):
                sp.dma_start(X0[:, :, :], at(x_v, it)).then_inc(x_loaded, 16)

            def load_ctx(it):
                sp.dma_start(ctx[:, :, :], at(ctx_v, it)).then_inc(ctx_loaded, 16)

            def store(it):
                sp.wait_ge(out_ready, it + 1)
                sp.dma_start(at(out_v, it), Y[:, :, :]).then_inc(out_stored, 16)

            load_x(0)
            for dst, src in rec_loads:
                sp.dma_start(dst, src).then_inc(rec_loaded, 16)
            for dst, src in loads:
                sp.dma_start(dst, src).then_inc(weights_loaded, 16)
            load_ctx(0)
            with sp.Fori(0, ITERS - 1) as it:
                sp.wait_ge(layer_done, it * LAYERS + 1)
                load_x(it + 1)
                sp.wait_ge(av_ps, it + 1)
                load_ctx(it + 1)
                store(it)
            store(ITERS - 1)
            sp.wait_ge(out_stored, 16 * ITERS + 1)

        @block.tensor
        def _(pe):
            def turn(src, b):
                for t in range(TT):
                    last = pe.transpose(ps[:, b, t * P:(t + 1) * P], src[:, t, :], ident[:, :])
                return last

            def turn_x(it, n, layers):
                pe.wait_ge(layer_done, it * LAYERS + layers)
                turn(X, 0).then_inc(xT_ps, 1)
                pe.wait_ge(xT_ready, it * 5 + n)

            def token_major(b, lhs, w, row=None):
                for t in range(TT):
                    o = ps[:, b, t * D:(t + 1) * D]
                    if row is not None:
                        pe.matmul(o, ones[0:1, :], row, start=True, stop=False)
                    last = pe.matmul(o, lhs[:, t * P:(t + 1) * P], w, start=row is None, stop=True)
                return last

            def set_up(n):
                if n >= SETUP_BANKS:
                    pe.wait_ge(wT_sb, n - SETUP_BANKS + 1)
                b, i = n % SETUP_BANKS, n - N_TURNS
                if n < N_TURNS:
                    for g, src in enumerate(weight_turns[n][0]):
                        k = src.shape[0]
                        last = pe.transpose(ps[:, b, g * P:g * P + k], src, ident[0:k, 0:k])
                elif i == 0:
                    last = pe.matmul(ps[:, b, 0:D], qw[:, :], kw[:, :], start=True, stop=True)
                else:
                    last = pe.matmul(ps[:, b, 0:D], ones[0:1, :], row_of((V_GAMMA, V_BETA, V_NORMW, V_BO)[i - 1]),
                                     start=True, stop=True)
                last.then_inc(wT_ps, 1)

            pe.wait_ge(consts_ready, 1)
            pe.wait_ge(rec_loaded, 16 * len(rec_loads))
            set_up(0)

            def turn_ctx(n, more_y=None):
                pe.wait_ge(ctx_loaded, n * 16 + 16)
                if more_y is not None:
                    pe.wait_ge(y_ready, more_y * E + E)
                for g in range(2):
                    for i in range(4):
                        last = pe.transpose(ps[:, 2 + g, i * P:(i + 1) * P], ctx[:, 4 * g + i, :], ident[:, :])
                    last.then_inc(ctxT_ps, 1)

            def rec_turn(n, k, b):
                pe.wait_ge(xhat_ready, n * 2 + k)
                turn(NHAT, b).then_inc(hT_ps, 1)

            def rec_project(n, i, b):
                z, w = ((zk, wk), (zv, wv), (zr, wr))[i]
                pe.wait_ge(mix_ready, n * 5 + i + 1)
                pe.matmul(bank(b), w[:, :], z[:, :, :], start=True, stop=True).then_inc(kvr_ps, 1)

            def rec_attend(n):
                pe.wait_ge(wkv_ready, n + 1)
                token_major(6, rec[:, :, :].rearrange("p b s -> p (b s)"), wo[:, :]).then_inc(att_ps, 1)

            def rec_widen(n):
                pe.wait_ge(mix_ready, n * 5 + 4)
                for h, b in enumerate((6, 7, 5, 6)):
                    if h == 3:
                        pe.wait_ge(kf_relu, n * HT + 1)
                    pe.matmul(bank(b), fwk[:, h * P:(h + 1) * P], zk[:, :, :], start=True, stop=True)\
                        .then_inc(kf_ps, 1)
                pe.wait_ge(mix_ready, n * 5 + 5)
                pe.wait_ge(kf_relu, n * HT + 2)
                token_major(7, zr[:, :, :].rearrange("p b s -> p (b s)"), fwr[:, :]).then_inc(rf_ps, 1)

            def rec_narrow(n):
                pe.wait_ge(kf_ready, n * HT + HT)
                for t in range(TT):
                    for h in range(HT):
                        last = pe.matmul(ps[:, 5, t * D:(t + 1) * D], big2[:, h, t * P:(t + 1) * P],
                                         fwv[:, h, :], start=(h == 0), stop=(h == HT - 1))
                last.then_inc(ffn_ps, 1)

            def first_recurrent(n):
                rec_turn(n, 1, 5)
                rec_project(n, 0, 4)
                rec_project(n, 1, 7)
                rec_project(n, 2, 5)
                pe.wait_ge(weights_loaded, 16 * len(loads))
                for i in range(1, N_SETUP):
                    set_up(i)
                pe.wait_ge(wT_sb, N_SETUP)
                rec_attend(n)
                turn_ctx(n)
                rec_turn(n, 2, 5)
                rec_widen(n)
                rec_narrow(n)

            def memory(it):
                turn_x(it, 1, 1)
                pe.wait_ge(nhat_ready, it + 1)
                turn(NHAT, 1).then_inc(nT_ps, 1)
                pe.wait_ge(nT_ready, it + 1)
                pe.matmul(bank(3), qk_fold[:, :], nT[:, :], start=True, stop=True).then_inc(qp_ps, 1)
                pe.wait_ge(ctxT_ready, it * 2 + 2)
                pe.wait_ge(qp_ready, it + 1)

                def logits(t):
                    b, tq, base = t // QT, t % QT, 2 * (t % 2)
                    nk = (tq + 1) * P
                    q = qpT[:, t * P:(t + 1) * P]
                    pe.matmul(bank(base), q, ctxT[:, b * CTX:(b + 1) * CTX], start=True, stop=True)
                    k0 = b * SEQ + nk - P
                    if tq:
                        pe.matmul(ps[:, base + 1, 0:nk - P], q, nT[:, b * SEQ:k0], start=True, stop=True)
                    pe.matmul(ps[:, base + 1, nk - P:nk], ident_bf[:, :], causal[:, :], start=True, stop=False)
                    pe.matmul(ps[:, base + 1, nk - P:nk], q, nT[:, k0:k0 + P], start=False, stop=True)\
                        .then_inc(lg_ps, 1)

                def turn_probs(t):
                    pe.wait_ge(lg_exp, it * TT + t + 1)
                    for k in range(KT + t % QT + 1):
                        last = pe.transpose(psf[:, 4 * 512 + k * P:4 * 512 + (k + 1) * P],
                                            prob[:, t % 2, k * P:(k + 1) * P], ident[:, :])
                    last.then_inc(pT_ps, 1)

                def values(t):
                    b, tq = t // QT, t % QT
                    if t == 0:
                        pe.wait_ge(ntok_ready, it + 1)
                    pe.wait_ge(pT_ready, it * TT + t + 1)
                    n = KT + tq + 1
                    for k in range(n):
                        v = ctx[:, b * KT + k, :] if k < KT else nTok[:, b * QT + k - KT, :]
                        last = pe.matmul(ps[:, 6, t * D:(t + 1) * D], probT[:, 0, k * P:(k + 1) * P], v,
                                         start=(k == 0), stop=(k == n - 1))
                    return last

                logits(0)
                logits(1)
                token_major(7, XT, gwT[:, :], row_of(V_GATEB)).then_inc(gate_ps, 1)
                for t in range(TT):
                    turn_probs(t)
                    if t + 2 < TT:
                        logits(t + 2)
                    last = values(t)
                last.then_inc(av_ps, 1)

            def mixture_top1(it):
                turn_x(it, 2, 2)
                for t in range(TT):
                    last = pe.matmul(ps[:, 1, t * E:(t + 1) * E], XT[:, t * P:(t + 1) * P], wr0T[:, :],
                                     start=True, stop=True)
                last.then_inc(route_ps, 1)
                pe.wait_ge(onehot_ready, it + 1)
                for t in range(TT):
                    last = pe.transpose(ps[0:E, 2, t * P:(t + 1) * P], onehot[:, t, :], ident[:, :])
                last.then_inc(ohT_ps, 1)

                def pick_rows(e):
                    pe.matmul(bank(3 + e % 2), pick[:, e, :], ohT_bf[:, :], start=True, stop=True)\
                        .then_inc(pick_ps, 1)

                acc = (5, 6, 7, 0)
                pe.wait_ge(ohT_ready, it * 2 + 1)
                pick_rows(0)
                pick_rows(1)
                pe.wait_ge(ohT_ready, it * 2 + 2)
                for e in range(E):
                    pe.wait_ge(xe_ready, it * E + e + 1)
                    for h in range(HT):
                        last = pe.matmul(bank(acc[h]), w1a[:, e, h * P:(h + 1) * P], XE[:, e % 2, :],
                                         start=(e == 0), stop=(e == E - 1))
                        if e == E - 1:
                            last.then_inc(pre_ps, 1)
                    if 1 <= e <= HT:
                        pe.matmul(bank(acc[e - 1]), b1a[:, (e - 1) * P:e * P], ohT[:, :], start=False, stop=False)
                    if e + 2 < E:
                        pick_rows(e + 2)
                pe.wait_ge(inter_ready, it * HT + HT)
                for t in range(TT):
                    o = ps[:, 1, t * D:(t + 1) * D]
                    for h in range(HT):
                        last = pe.matmul(o, big[:, h, t * P:(t + 1) * P], wo0[:, h, :], start=(h == 0), stop=(h == HT - 1))
                last.then_inc(moe_ps, 1)

            def project_q(it, j, b):
                pe.wait_ge(staged, it * PAIRS + j + 1)
                pe.matmul(bank(b), wq_s[:, :], XT[:, :], start=True, stop=True).then_inc(q_ps, 1)

            def project_k(b, seq):
                pe.matmul(bank(b), wk_s[:, :], ctxT[:, seq * CTX:(seq + 1) * CTX], start=True, stop=True)\
                    .then_inc(k_ps, 1)

            def project_v(j, b, seq):
                for k in range(KT):
                    c = seq * KT + k
                    last = pe.matmul(ps[:, b, k * P:(k + 1) * P], ctxT[:, c * P:(c + 1) * P],
                                     xwT[:, 2, bass.ds(j, 1), :], start=True, stop=True)
                last.then_inc(vx_ps, 1)

            def sparse_attention(it):
                turn_x(it, 3, 3)
                pe.matmul(bank(1), wattn[:, 0:D], XT[:, :], start=True, stop=True).then_inc(qkv_ps, 1)
                pe.matmul(bank(2), wattn[:, D:2 * D], XT[:, :], start=True, stop=True).then_inc(qkv_ps, 1)
                token_major(3, XT, wattn[:, 2 * D:3 * D], row_of(V_BV)).then_inc(qkv_ps, 1)
                pe.wait_ge(xg_ready, it + 1)
                for b in range(GROUP):
                    o = ps[:, 4, b * D:(b + 1) * D]
                    pe.matmul(o, ones[0:1, :], row_of(V_BV), start=True, stop=False)
                    last = pe.matmul(o, XTg[:, b, :, :], wattn[:, 2 * D:3 * D], start=False, stop=True)
                last.then_inc(qkv_ps, 1)

                def scores(hh, u):
                    pe.wait_ge(qm_ready, it * NH + 2 * hh + u + 1)
                    for b in range(GROUP):
                        o = 2 * u + b
                        for tq in range(QT):
                            c = tq * KW
                            k0 = b * SEQ + tq * (SEQ - KW)
                            pe.matmul(ps[:, o, c:c + KW], ident_bf[:, :], sparse[:, c:c + KW], start=True, stop=False)
                            last = pe.matmul(ps[:, o, c:c + KW], qm[:, u, b * SEQ + tq * P:b * SEQ + (tq + 1) * P],
                                             kT[:, k0:k0 + KW], start=False, stop=True)
                    last.then_inc(s_ps, 1)

                def turn_probs(hh, u):
                    pe.wait_ge(s_exp, it * NH + 2 * hh + u + 1)
                    pe.wait_ge(so_ready, it * (NH + 1) + 2 * hh + u + 1)
                    for t in range(TT):
                        lo = 0 if t % QT == 0 else CB
                        last = pe.transpose(ps[:, 4 + u, t * P:(t + 1) * P], SP_[:, u, t, lo:lo + P], ident[:, :])
                    last.then_inc(sT_ps, 1)

                def values(hh, u):
                    h = 2 * hh + u
                    pe.wait_ge(sT_ready, it * NH + h + 1)
                    for t in range(TT):
                        last = pe.matmul(ps[:, 6 + u, t * HD:(t + 1) * HD], spT[:, u, t * P:(t + 1) * P],
                                         V[:, t, bass.ds(h * HD, HD)], start=True, stop=True)
                    last.then_inc(so_ps, 1)

                def two_heads(hh, more):
                    turn_probs(hh, 0)
                    if more:
                        scores(hh + 1, 0)
                    turn_probs(hh, 1)
                    values(hh, 0)
                    if more:
                        scores(hh + 1, 1)
                    values(hh, 1)

                pe.wait_ge(qk_ready, it * 2 + 2)
                pe.wait_ge(v_ready, it + 1)
                scores(0, 0)
                scores(0, 1)
                with pe.Fori(0, NH // 2 - 1) as hh:
                    two_heads(hh, True)
                two_heads(NH // 2 - 1, False)
                pe.wait_ge(g_ready, it + 1)
                for b in range(GROUP):
                    last = pe.transpose(ps[:, 4, b * P:(b + 1) * P], G[:, b, :, :], ident[:, :])
                last.then_inc(gT_ps, 1)
                pe.wait_ge(gT_ready, it + 1)
                for b in range(GROUP):
                    last = pe.matmul(ps[:, 5, b * D:(b + 1) * D], GT[:, b, :], Vg[:, b, :], start=True, stop=True)
                last.then_inc(og_ps, 1)
                pe.wait_ge(so_ready, it * (NH + 1) + NH + 3)
                turn(O, 0).then_inc(oT_ps, 1)
                pe.wait_ge(oT_ready, it + 1)
                token_major(1, OT, wproj[:, :], row_of(V_BPROJ)).then_inc(proj_ps, 1)
                pe.wait_ge(staged, it * PAIRS + 1)
                project_k(6, 0)
                project_k(3, 1)
                project_v(0, 4, 0)
                project_v(0, 5, 1)

            def cross_attention(it, more_groups=True):
                turn_x(it, 4, 4)

                def scores(j, u, s):
                    h, t = s // TT, s % TT
                    if s == 0:
                        pe.wait_ge(q_ready, it * PAIRS + j + 1)
                        pe.wait_ge(k_ready, it * (2 * PAIRS) + 2 * j + 1)
                    if s == QT:
                        pe.wait_ge(k_ready, it * (2 * PAIRS) + 2 * j + 2)
                    r = slice(h * DK, (h + 1) * DK)
                    pe.matmul(bank(s % 2), QTs[r, u, t * P:(t + 1) * P],
                              KTs[r, u, (t // QT) * CTX:(t // QT + 1) * CTX], start=True, stop=True).then_inc(c_ps, 1)

                def turn_probs(j, s):
                    pe.wait_ge(c_exp, it * (NS * PAIRS) + j * NS + s + 1)
                    for k in range(KT):
                        last = pe.transpose(ps[:, 2 + s % 2, k * P:(k + 1) * P], cprob[:, s % 2, k * P:(k + 1) * P],
                                            ident[:, :])
                    last.then_inc(cT_ps, 1)

                def values(j, u, s):
                    h, t = s // TT, s % TT
                    if s == 0:
                        pe.wait_ge(vx_ready, it * (2 * PAIRS) + 2 * j + 2)
                    pe.wait_ge((cT_even, cT_odd)[s % 2], it * (NS * PAIRS // 2) + j * (NS // 2) + s // 2 + 1)
                    o = ps[:, 4 + u, t * P + h * DK:t * P + (h + 1) * DK]
                    for k in range(KT):
                        last = pe.matmul(o, cprobT[:, s % 2, k * P:(k + 1) * P],
                                         Vx[u][:, (t // QT) * KT + k, h * DK:(h + 1) * DK],
                                         start=(k == 0), stop=(k == KT - 1))
                    return last

                def turn_context(j):
                    pe.wait_ge(o_ready, it * PAIRS + j + 1)
                    turn(Cx, 6).then_inc(ctT_ps, 1)

                def project_out(j, b):
                    pe.wait_ge(ctT_ready, it * PAIRS + j + 1)
                    for t in range(TT):
                        last = pe.matmul(ps[:, b, t * D:(t + 1) * D], CTs[:, t * P:(t + 1) * P],
                                         xwT[:, 3, bass.ds(j, 1), :], start=True, stop=True)
                    last.then_inc(wo_ps, 1)

                def between_steps(j, s, first, more):
                    if s == 0 and more:
                        pe.wait_ge(vx_ready, it * (2 * PAIRS) + 2 * j + 2)
                        project_q(it, j + 1, 7)
                    if s == 1 and not first:
                        turn_context(j - 1)
                    if s == 2 and more:
                        pe.wait_ge(q_ready, it * PAIRS + j + 2)
                        project_k(7, 0)
                    if s == 3 and not first:
                        project_out(j - 1, 6)
                    if s == 4 and more:
                        pe.wait_ge(k_ready, it * (2 * PAIRS) + 2 * j + 3)
                        project_k(7, 1)
                    if s == 5 and more:
                        pe.wait_ge(wo_added, it * (PAIRS + 1) + j + 1)
                        project_v(j + 1, 6, 0)
                    if s == 6 and more:
                        pe.wait_ge(k_ready, it * (2 * PAIRS) + 2 * j + 4)
                        project_v(j + 1, 7, 1)

                def pair(j, u, first=False, more=True):
                    for s in range(NS):
                        turn_probs(j, s)
                        if s >= 1:
                            values(j, u, s - 1)
                        if s + 2 < NS:
                            scores(j, u, s + 2)
                        elif more:
                            scores(j + 1, 1 - u, s + 2 - NS)
                        between_steps(j, s, first, more)
                        if more_groups and not more:
                            if s == 2:
                                rec_turn(it + 1, 1, 7)
                            if s == 6:
                                rec_project(it + 1, 0, 4)
                    values(j, u, NS - 1).then_inc(o_ps, 1)

                project_q(it, 0, 7)
                scores(0, 0, 0)
                scores(0, 0, 1)
                pair(0, 0, first=True)
                with pe.Fori(0, PAIRS // 2 - 1) as jj:
                    pair(2 * jj + 1, 1)
                    pair(2 * jj + 2, 0)
                pair(PAIRS - 1, 1, more=False)
                if more_groups:
                    rec_project(it + 1, 1, 7)
                turn_context(PAIRS - 1)
                if more_groups:
                    rec_project(it + 1, 2, 5)
                project_out(PAIRS - 1, 3)

            def mixture_top2(it, more=True):
                turn_x(it, 5, 5)
                for t in range(TT):
                    o = ps[:, 1, t * E:(t + 1) * E]
                    pe.matmul(o, ones[0:1, :], rows[0:1, V_BR:V_BR + E], start=True, stop=False)
                    last = pe.matmul(o, XT[:, t * P:(t + 1) * P], wr1[:, :], start=False, stop=True)
                last.then_inc(r1_ps, 1)
                pe.wait_ge(two_hot, it + 1)
                for t in range(TT):
                    o = ps[:, 2, t * E:(t + 1) * E]
                    if t % QT:
                        pe.matmul(o, ones_bf[:, :], A_bf[:, t - 1, :], start=True, stop=False)
                    last = pe.matmul(o, before[:, :], A_bf[:, t, :], start=(t % QT == 0), stop=True)
                last.then_inc(pos_ps, 1)
                pe.wait_ge(disp_ready, it + 1)
                for b in range(GROUP):
                    for tq in range(QT):
                        t = b * QT + tq
                        last = pe.matmul(ps[:, 3 + b, 0:SLOTS], X[:, t, :], disp[:, t, :], start=(tq == 0),
                                         stop=(tq == QT - 1))
                    last.then_inc(xb_ps, 1)
                pe.wait_ge(comb_ready, it + 1)
                if more:
                    pe.wait_ge(kvr_ready, (it + 1) * 3 + 3)
                for t in range(TT):
                    for k in range(SB):
                        n = min(P, SLOTS - k * P)
                        last = pe.transpose(ps[0:n, 5 + k, t * P:(t + 1) * P], comb[:, t, k * P:k * P + n], ident[:, :])
                last.then_inc(combT_ps, 1)
                pe.wait_ge(xb_ready, it * GROUP + GROUP)
                W = GROUP * CAP

                def up(e):
                    for h in range(HT):
                        last = pe.matmul(ps[:, e % 2, h * W:(h + 1) * W], w1b[:, e, h * P:(h + 1) * P],
                                         xb[:, :, e * CAP:(e + 1) * CAP], start=True, stop=True)
                    last.then_inc(hid_ps, 1)

                def down(e):
                    pe.wait_ge(hid_ready, it * E + e + 1)
                    if e >= 2:
                        pe.wait_ge(y_ready, it * E + e - 1)
                    for h in range(HT):
                        last = pe.matmul(ps[:, 2 + e % 2, 0:W], w2b[:, e, h, :], hid[:, e % 2, h, :],
                                         start=(h == 0), stop=(h == HT - 1))
                    last.then_inc(y_ps, 1)

                up(0)
                for e in range(E):
                    if e + 1 < E:
                        up(e + 1)
                    down(e)
                    if more and e == 1:
                        pe.wait_ge(combT_ready, it + 1)
                        rec_attend(it + 1)
                    if more and e == E - 3:
                        rec_turn(it + 1, 2, 5)
                if more:
                    turn_ctx(it + 1, it)
                    rec_widen(it + 1)
                pe.wait_ge(y_ready, it * E + E)
                for b in range(GROUP):
                    for k in range(SB):
                        n = min(P, SLOTS - k * P)
                        last = pe.transpose(ps[0:n, b, k * D:(k + 1) * D], yT[:, b, k * P:k * P + n], ident[:, :])
                    last.then_inc(ysl_ps, 1)
                if more:
                    rec_narrow(it + 1)
                pe.wait_ge(combT_ready, it + 1)
                for t in range(TT):
                    if t % QT == 0:
                        pe.wait_ge(ysl_ready, it * GROUP + t // QT + 1)
                    for k in range(SB):
                        n = min(P, SLOTS - k * P)
                        last = pe.matmul(ps[:, 4, t * D:(t + 1) * D], combT[0:n, k, t * P:(t + 1) * P],
                                         ySl[0:n, t // QT, k, :], start=(k == 0), stop=(k == SB - 1))
                last.then_inc(comb_ps, 1)

            def group(it, more=True):
                memory(it)
                mixture_top1(it)
                sparse_attention(it)
                cross_attention(it, more)
                mixture_top2(it, more)

            first_recurrent(0)
            with pe.Fori(0, ITERS - 1) as it:
                group(it)
            group(ITERS - 1, more=False)

        @block.scalar
        def _(act):
            def copy(dst, src):
                return act.activation(dst, src, ACT.Copy)

            def set_up(n):
                act.wait_ge(wT_ps, n + 1)
                b = n % SETUP_BANKS
                if n >= N_TURNS:
                    dst, src = (qk_fold, gamma_bc, beta_bc, normw_bc, bo_bc)[n - N_TURNS][:, :], ps[:, b, 0:D]
                else:
                    srcs, dst = weight_turns[n]
                    src = tiles(b) if len(srcs) == 4 else ps[:, b, 0:srcs[0].shape[0]]
                copy(dst, src).then_inc(wT_sb, 1)

            set_up(0)
            act.wait_ge(wT_sb, 1)
            act.activation(decay_e[:, :], col(R_DECAY), ACT.Exp).then_inc(cols_ready, 1)
            act.wait_ge(cols_ready, 5)

            def x_turned(it, n):
                act.wait_ge(xT_ps, it * 5 + n)
                copy(XT[:, :], bank(0)).then_inc(xT_ready, 1)

            def ctx_turned(n):
                for g in range(2):
                    act.wait_ge(ctxT_ps, n * 2 + g + 1)
                    copy(ctxT[:, g * 512:(g + 1) * 512], bank(2 + g)).then_inc(ctxT_ready, 1)

            def rec_turned(n, k, b, scale, shift):
                act.wait_ge(hT_ps, n * 2 + k)
                act.activation(hT[:, :, 1:SEQ + 1], seqs(b), ACT.Identity, bias=col(shift), scale=col(scale))\
                    .then_inc(hT_ready, 1)

            def rec_projected(n, i):
                act.wait_ge(kvr_ps, n * 3 + i + 1)
                copy((kS, vS)[i][:, :, :], seqs((4, 7)[i])).then_inc(kvr_ready, 1)

            def rec_exp(n, i):
                act.wait_ge(wkv_arg, n * 4 + i + 1)
                act.activation(ex[i][:, :, :], ex[i][:, :, :], ACT.Exp).then_inc(wkv_exp, 1)

            def rec_receptance(n):
                act.wait_ge(kvr_ps, n * 3 + 3)
                act.activation(rS[:, :, :], seqs(5), ACT.Sigmoid).then_inc(kvr_ready, 1)

            def rec_rectify(n):
                for h, b in enumerate((6, 7, 5, 6)):
                    act.wait_ge(kf_ps, n * HT + h + 1)
                    act.activation(big[:, h, :], bank(b), ACT.Relu).then_inc(kf_relu, 1)
                act.wait_ge(rf_ps, n + 1)
                act.activation(rf[:, :, :], tiles(7), ACT.Sigmoid).then_inc(rf_ready, 1)

            def first_recurrent(n):
                rec_turned(n, 1, 5, R_LNG, R_LNB)
                rec_projected(n, 0)
                rec_projected(n, 1)
                for i in range(4):
                    rec_exp(n, i)
                rec_receptance(n)
                for i in range(1, N_SETUP):
                    set_up(i)
                ctx_turned(n)
                rec_turned(n, 2, 5, R_FLNG, R_FLNB)
                rec_rectify(n)

            def memory(it):
                act.wait_ge(layer_done, it * LAYERS + 1)
                for t in range(TT):
                    if t:
                        act.drain()
                    last = act.activation(junk[:, :], X[:, t, :], ACT.Square, scale=float(D) ** -0.5,
                                          accum_out=ssq[:, t:t + 1])
                last.then_inc(ssq_ready, 1)
                x_turned(it, 1)
                act.wait_ge(nT_ps, it + 1)
                act.activation(nT[:, :], bank(1), ACT.Identity, scale=col(R_NORMW)).then_inc(nT_ready, 1)
                act.wait_ge(qp_ps, it + 1)
                act.activation(qpT[:, :], bank(3), ACT.Copy, scale=float(D) ** -0.5).then_inc(qp_ready, 1)

                def exps(t):
                    n = CTX + (t % QT + 1) * P
                    act.wait_ge(lg_max, it * TT + t + 1)
                    lo = 2 * (t % 2) * 512
                    act.activation(prob[:, t % 2, 0:n], psf[:, lo:lo + n], ACT.Exp, bias=nmax[:, t:t + 1],
                                   accum_out=rsum[:, 0, t:t + 1]).then_inc(lg_exp, 1)

                exps(0)
                exps(1)
                for t in range(TT):
                    n = CTX + (t % QT + 1) * P
                    act.wait_ge(pT_ps, it * TT + t + 1)
                    copy(probT[:, 0, 0:n], psf[:, 4 * 512:4 * 512 + n]).then_inc(pT_ready, 1)
                    if t + 2 < TT:
                        exps(t + 2)
                act.wait_ge(gate_ps, it + 1)
                act.activation(alpha[:, :, :], tiles(7), ACT.Sigmoid).then_inc(alpha_ready, 1)

            def mixture_top1(it):
                x_turned(it, 2)
                act.wait_ge(ohT_ps, it + 1)
                copy(ohT_bf[:, :], ps[0:E, 2, :]).then_inc(ohT_ready, 1)
                copy(ohT[:, :], ps[0:E, 2, :]).then_inc(ohT_ready, 1)
                for h, b in enumerate((5, 6, 7, 0)):
                    act.wait_ge(pre_ps, it * HT + h + 1)
                    act.activation(big[:, h, :], bank(b), ACT.Gelu).then_inc(inter_ready, 1)

            def sparse_attention(it):
                x_turned(it, 3)
                act.wait_ge(qkv_ps, it * 4 + 1)
                act.activation(qT[:, :], bank(1), ACT.Identity, bias=battq_scaled[:, 0:1], scale=float(HD) ** -0.5)\
                    .then_inc(qk_ready, 1)
                act.wait_ge(qkv_ps, it * 4 + 2)
                act.activation(kT[:, :], bank(2), ACT.Identity, bias=col(R_BATT + 1)).then_inc(qk_ready, 1)
                act.wait_ge(qkv_ps, it * 4 + 3)
                copy(V[:, :, :], tiles(3)).then_inc(v_ready, 1)

                def exps(hh, u):
                    act.wait_ge(s_max, it * NH + 2 * hh + u + 1)
                    for t in range(TT):
                        c = (t % QT) * KW
                        last = act.activation(SP_[:, u, t, :], ps[:, 2 * u + t // QT, c:c + KW], ACT.Exp,
                                              bias=snm[:, u, t:t + 1], accum_out=srs[:, u, t:t + 1])
                    last.then_inc(s_exp, 1)

                def turned(hh, u):
                    act.wait_ge(sT_ps, it * NH + 2 * hh + u + 1)
                    copy(spT[:, u, :], bank(4 + u)).then_inc(sT_ready, 1)

                exps(0, 0)
                exps(0, 1)
                with act.Fori(0, NH // 2 - 1) as hh:
                    turned(hh, 0)
                    turned(hh, 1)
                    exps(hh + 1, 0)
                    exps(hh + 1, 1)
                turned(NH // 2 - 1, 0)
                turned(NH // 2 - 1, 1)
                act.wait_ge(gT_ps, it + 1)
                copy(GT[:, :, :], ps[:, 4, 0:GROUP * P].rearrange("p (b q) -> p b q", b=GROUP)).then_inc(gT_ready, 1)
                act.wait_ge(oT_ps, it + 1)
                copy(OT[:, :], bank(0)).then_inc(oT_ready, 1)

            def cross_attention(it, more_groups=True):
                def queries(j, u, b):
                    act.wait_ge(q_ps, it * PAIRS + j + 1)
                    act.wait_ge(cols_ready, 5)
                    act.activation(QTs[:, u, :], bank(b), ACT.Identity, bias=bq_scaled[:, bass.ds(j, 1)],
                                   scale=float(DK) ** -0.5).then_inc(q_ready, 1)

                def keys(j, u, b, seq):
                    if seq == 0 or isinstance(j, int):
                        act.wait_ge(k_ps, it * (2 * PAIRS) + 2 * j + seq + 1)
                    act.wait_ge(cols_ready, 5)
                    act.activation(KTs[:, u, seq * CTX:(seq + 1) * CTX], bank(b), ACT.Identity,
                                   bias=cols[:, bass.ds(R_BK + j, 1)]).then_inc(k_ready, 1)

                def exps(j, u, s):
                    act.wait_ge(c_max, it * (NS * PAIRS) + j * NS + s + 1)
                    act.activation(cprob[:, s % 2, :], bank(s % 2), ACT.Exp, bias=nmax[:, s:s + 1],
                                   accum_out=rsum[:, u, s:s + 1]).then_inc(c_exp, 1)

                def context(j):
                    act.wait_ge(ctT_ps, it * PAIRS + j + 1)
                    act.wait_ge(cols_ready, 5)
                    act.activation(CTs[:, :], bank(6), ACT.Identity, bias=cols[:, bass.ds(R_BV + j, 1)])\
                        .then_inc(ctT_ready, 1)

                def pair(j, u, first=False, more=True):
                    for s in range(NS):
                        if s + 1 < NS:
                            exps(j, u, s + 1)
                        elif more:
                            exps(j + 1, 1 - u, 0)
                        if s % 2:
                            act.wait_ge(cT_ps, it * (NS * PAIRS) + j * NS + s + 1)
                            copy(cprobT[:, 1, :], bank(3)).then_inc(cT_odd, 1)
                        if s == 1 and more:
                            queries(j + 1, 1 - u, 7)
                        if s == 2 and not first:
                            context(j - 1)
                        if s == 3 and more:
                            keys(j + 1, 1 - u, 7, 0)
                        if s == 5 and more:
                            keys(j + 1, 1 - u, 7, 1)
                        if more_groups and not more:
                            if s == 3:
                                rec_turned(it + 1, 1, 7, R_LNG, R_LNB)
                            if s == 7:
                                rec_projected(it + 1, 0)

                keys(0, 0, 6, 0)
                keys(0, 0, 3, 1)
                x_turned(it, 4)
                queries(0, 0, 7)
                exps(0, 0, 0)
                pair(0, 0, first=True)
                with act.Fori(0, PAIRS // 2 - 1) as jj:
                    pair(2 * jj + 1, 1)
                    pair(2 * jj + 2, 0)
                pair(PAIRS - 1, 1, more=False)
                if more_groups:
                    rec_projected(it + 1, 1)
                context(PAIRS - 1)

            def mixture_top2(it, more=True):
                x_turned(it, 5)
                if more:
                    for i in range(4):
                        rec_exp(it + 1, i)
                act.wait_ge(e1_arg, it + 1)
                act.activation(ex1[:, :, :], ex1[:, :, :], ACT.Exp).then_inc(e1_exp, 1)
                if more:
                    rec_receptance(it + 1)
                for b in range(GROUP):
                    act.wait_ge(xb_ps, it * GROUP + b + 1)
                    copy(xb[:, b, :], ps[:, 3 + b, 0:SLOTS]).then_inc(xb_ready, 1)
                act.wait_ge(combT_ps, it + 1)
                for k in range(SB):
                    n = min(P, SLOTS - k * P)
                    last = copy(combT[0:n, k, :], ps[0:n, 5 + k, :])
                last.then_inc(combT_ready, 1)
                W = GROUP * CAP

                def relu(e):
                    act.wait_ge(hid_ps, it * E + e + 1)
                    for h in range(HT):
                        last = act.activation(hid[:, e % 2, h, :], ps[:, e % 2, h * W:(h + 1) * W], ACT.Relu,
                                              bias=col(R_B1 + e * HT + h))
                    last.then_inc(hid_ready, 1)

                relu(0)
                for e in range(E):
                    if e + 1 < E:
                        relu(e + 1)
                    act.wait_ge(y_ps, it * E + e + 1)
                    act.activation(yT[:, :, e * CAP:(e + 1) * CAP],
                                   ps[:, 2 + e % 2, 0:W].rearrange("p (b c) -> p b c", b=GROUP),
                                   ACT.Identity, bias=col(R_B2 + e)).then_inc(y_ready, 1)
                    if more and e == E - 3:
                        rec_turned(it + 1, 2, 5, R_FLNG, R_FLNB)
                if more:
                    ctx_turned(it + 1)
                    rec_rectify(it + 1)
                for b in range(GROUP):
                    act.wait_ge(ysl_ps, it * GROUP + b + 1)
                    for k in range(SB):
                        n = min(P, SLOTS - k * P)
                        last = copy(ySl[0:n, b, k, :], ps[0:n, b, k * D:(k + 1) * D])
                    last.then_inc(ysl_ready, 1)

            def group(it, more=True):
                memory(it)
                mixture_top1(it)
                sparse_attention(it)
                cross_attention(it, more)
                mixture_top2(it, more)

            first_recurrent(0)
            with act.Fori(0, ITERS - 1) as it:
                group(it)
            group(ITERS - 1, more=False)

        @block.gpsimd
        def _(pool):
            pool.memset(ident[:, :], 0.0)
            pool.memset(causal_f[:, :], 0.0)
            pool.memset(sparse_f[:, :, :], 0.0)
            pool.memset(before_f[:, :], 1.0)
            pool.memset(ones_bf[:, :], 1.0)
            pool.memset(ones[:, :], 1.0)
            pool.memset(pick_f[:, :, :], 0.0)
            pool.memset(head_mask[:, :], 1.0)
            pool.memset(neg_half[:, :], -0.5)
            pool.memset(eps_ln[:, :], 1e-5)
            pool.memset(eps_rms[:, :], 1e-6)
            pool.memset(eps_post[:, :], 1e-12)
            pool.iota(iota_ei[:, :], pattern=[[1, E]], base=0, channel_multiplier=0)
            pool.iota(iota_ci[:, :], pattern=[[1, CAP]], base=1, channel_multiplier=0)
            pool.drain()

            def select(m, op, fill, base, pattern, cm):
                pool.affine_select(out=m, in_=m, compare_op=op, fill=fill, base=base, pattern=pattern,
                                   channel_multiplier=cm)

            select(ident[:, :], ALU.not_equal, 1.0, 0, [[-1, P]], 1)
            select(causal_f[:, :], ALU.is_ge, MASKED, 0, [[-1, P]], 1)
            for tq in range(QT):
                select(sparse_f[:, tq, :], ALU.is_ge, MASKED, tq * CB, [[-1, KW]], 1)
            select(before_f[:, :], ALU.is_ge, 0.0, -1, [[1, P]], -1)
            select(pick_f[:, :, :], ALU.not_equal, 1.0, 0, [[-1, E], [0, P]], 1)
            select(head_mask[:, :], ALU.is_ge, 0.0, 0, [[-HD, NH]], 1)
            pool.drain()
            select(head_mask[:, :], ALU.is_ge, 0.0, HD - 1, [[HD, NH]], -1)
            for dst, src in ((ident_bf, ident), (causal, causal_f), (before, before_f), (iota_e, iota_ei),
                             (iota_c, iota_ci)):
                pool.tensor_copy(dst[:, :], src[:, :])
            pool.tensor_copy(pick[:, :, :], pick_f[:, :, :])
            pool.tensor_copy(sparse[:, :], sparse_f[:, :, :].rearrange("p a b -> p (a b)"))
            pool.drain().then_inc(consts_ready, 1)

            def rstd_of(it, n, eps):
                pool.wait_ge(var_ready, it * LNS + n)
                pool.tensor_tensor(vare[:, :], variance, eps[:, :], ALU.add)
                pool.drain()
                pool.tensor_tensor(rstd[:, :], vare[:, :], neg_half[:, :], ALU.pow).then_inc(rstd_ready, 1)

            def rec_rstd(n, k):
                pool.wait_ge(rvar_ready, n * RNS + k)
                pool.tensor_tensor(vare[:, :], variance, eps_ln[:, :], ALU.add)
                pool.drain()
                pool.tensor_tensor(rstd[:, :], vare[:, :], neg_half[:, :], ALU.pow).then_inc(rrstd_ready, 1)

            def rec_numerator(n):
                pool.wait_ge(wkv_exp, n * 4 + 2)
                pool.tensor_tensor(b2v[:, :, :], ex[1][:, :, :], vS[:, :, :], ALU.mult).then_inc(b2v_ready, 1)
                pool.wait_ge(wkv_exp, n * 4 + 4)
                pool.tensor_tensor(bv_[:, :, :], ex[3][:, :, :], vS[:, :, :], ALU.mult)
                pool.wait_ge(p_ready, n + 1)
                pool.tensor_tensor(t_num[:, :, :], ex[2][:, :, :], p_num[:, :, 0:SEQ], ALU.mult)
                pool.drain()
                pool.tensor_tensor(t_num[:, :, :], t_num[:, :, :], bv_[:, :, :], ALU.add)
                pool.drain()
                pool.wait_ge(kvr_ready, n * 3 + 3)
                pool.tensor_tensor(t_num[:, :, :], t_num[:, :, :], rS[:, :, :], ALU.mult).then_inc(tnum_ready, 1)

            variance = mv[:, :, 1:2].rearrange("p t o -> p (t o)")

            def stage(it, j):
                pool.tensor_copy(wq_s[:, :], xwT[:, 0, bass.ds(j, 1), :])
                pool.tensor_copy(wk_s[:, :], xwT[:, 1, bass.ds(j, 1), :])
                pool.drain().then_inc(staged, 1)

            def group(it, more=True):
                pool.wait_ge(ssq_ready, it + 1)
                pool.tensor_tensor(ssq_eps[:, :], ssq[:, :], eps_rms[:, :], ALU.add)
                pool.drain()
                pool.tensor_tensor(rms_inv[:, :], ssq_eps[:, :], neg_half[:, :], ALU.pow).then_inc(rms_ready, 1)
                pool.wait_ge(nhat_ready, it + 1)
                for t in range(TT):
                    last = pool.tensor_tensor(nTok[:, t, :], NHAT[:, t, :], normw_bc[:, :], ALU.mult)
                last.then_inc(ntok_ready, 1)
                rstd_of(it, 1, eps_ln)
                rstd_of(it, 2, eps_post)
                rstd_of(it, 3, eps_ln)
                stage(it, 0)
                rstd_of(it, 4, eps_ln)
                with pool.Fori(0, PAIRS - 1) as j:
                    pool.wait_ge(q_ps, it * PAIRS + j + 1)
                    pool.wait_ge(k_ps, it * (2 * PAIRS) + 2 * j + 2)
                    stage(it, j + 1)
                if more:
                    rec_rstd(it + 1, 1)
                rstd_of(it, 5, eps_ln)
                if more:
                    rec_numerator(it + 1)
                    rec_rstd(it + 1, 2)
                if more:
                    rec_rstd(it + 1, 3)
                rstd_of(it, 6, eps_ln)

            rec_rstd(0, 1)
            rec_numerator(0)
            rec_rstd(0, 2)
            pool.wait_ge(wT_sb, N_SETUP)
            rec_rstd(0, 3)
            with pool.Fori(0, ITERS - 1) as it:
                group(it)
            group(ITERS - 1, more=False)

        @block.vector
        def _(dve):
            def moments(src):
                for t in range(TT):
                    dve.bn_stats(bn[:, t, :], src[:, t, :])
                dve.drain()
                for t in range(TT):
                    last = dve.bn_aggr(mv[:, t, :], bn[:, t, :])
                return last

            def normalised(src, dst):
                for t in range(TT):
                    last = dve.tensor_scalar(dst[:, t, :], src[:, t, :], mv[:, t, 0:1], rstd[:, t:t + 1],
                                             ALU.subtract, ALU.mult)
                return last

            def layer_norm(it, n, src, dst):
                moments(src).then_inc(var_ready, 1)
                dve.wait_ge(rstd_ready, it * LNS + n)
                return normalised(src, dst)

            def rec_norm(n, k, src, dst):
                moments(src).then_inc(rvar_ready, 1)
                dve.wait_ge(rrstd_ready, n * RNS + k)
                return normalised(src, dst)

            def token_change():
                dve.tensor_tensor(dT[:, :, :], hT[:, :, 1:SEQ + 1], hT[:, :, 0:SEQ], ALU.subtract)
                dve.drain()

            def token_shift(z, r):
                for b in range(GROUP):
                    last = dve.scalar_tensor_tensor(out=z[:, b, :], in0=dT[:, b, :], scalar=col(r),
                                                    in1=hT[:, b, 0:SEQ], op0=ALU.mult, op1=ALU.add)
                last.then_inc(mix_ready, 1)

            dve.memset(hT[:, :, 0:1], 0.0).then_inc(out_stored, 1)
            dve.memset(o_max[:, :, 0:1], -1e38).then_inc(so_ready, 1)
            dve.memset(p_num[:, :, 0:1], 0.0).then_inc(so_ready, 1)
            dve.memset(q_den[:, :, 0:1], 0.0)
            dve.memset(w_bc[:, :], 0.0)
            dve.wait_ge(cols_ready, 1)
            dve.tensor_scalar(decay_w[:, :], decay_e[:, :], -1.0, None, ALU.mult).then_inc(cols_ready, 1)
            dve.tensor_scalar(bq_scaled[:, :], cols[:, R_BQ:R_BQ + PAIRS], float(DK) ** -0.5, None, ALU.mult)\
                .then_inc(cols_ready, 1)
            dve.tensor_scalar(battq_scaled[:, :], col(R_BATT), float(HD) ** -0.5, None, ALU.mult)\
                .then_inc(cols_ready, 1)
            dve.drain()
            dve.tensor_scalar(w_bc[:, :], w_bc[:, :], decay_w[:, 0:1], None, ALU.add).then_inc(cols_ready, 1)
            dve.drain()

            def rec_first_moments(n):
                dve.wait_ge(x_loaded, n * 16 + 16)
                moments(X0).then_inc(rvar_ready, 1)

            def rec_first_normalised(n):
                dve.wait_ge(rrstd_ready, n * RNS + 1)
                normalised(X0, NHAT).then_inc(xhat_ready, 1)

            def rec_key_mix(n):
                dve.wait_ge(hT_ready, n * 2 + 1)
                token_change()
                token_shift(zk, R_MK)

            def rec_value_mix():
                token_shift(zv, R_MV)
                token_shift(zr, R_MR)

            def rec_exponents(n):
                dve.wait_ge(kvr_ready, n * 3 + 1)
                for b in range(GROUP):
                    dve.tensor_tensor_scan(o_max[:, b, 1:SEQ + 1], w_bc[:, :], kS[:, b, :], -1e38, ALU.add, ALU.max)
                dve.drain()
                for b in range(GROUP):
                    last = dve.scalar_tensor_tensor(out=ex[0][:, b, :], in0=o_max[:, b, 0:SEQ], scalar=decay_w[:, 0:1],
                                                    in1=o_max[:, b, 1:SEQ + 1], op0=ALU.add, op1=ALU.subtract)
                last.then_inc(wkv_arg, 1)
                dve.tensor_tensor(ex[1][:, :, :], kS[:, :, :], o_max[:, :, 1:SEQ + 1], ALU.subtract)\
                    .then_inc(wkv_arg, 1)
                for b in range(GROUP):
                    dve.scalar_tensor_tensor(out=o_new[:, b, :], in0=kS[:, b, :], scalar=col(R_FIRST),
                                             in1=o_max[:, b, 0:SEQ], op0=ALU.add, op1=ALU.max)
                dve.drain()
                dve.tensor_tensor(ex[2][:, :, :], o_max[:, :, 0:SEQ], o_new[:, :, :], ALU.subtract)\
                    .then_inc(wkv_arg, 1)
                dve.scalar_tensor_tensor(out=ex[3][:, :, :], in0=kS[:, :, :], scalar=col(R_FIRST), in1=o_new[:, :, :],
                                         op0=ALU.add, op1=ALU.subtract).then_inc(wkv_arg, 1)

            def rec_wkv(n):
                dve.wait_ge(wkv_exp, n * 4 + 2)
                for b in range(GROUP):
                    dve.tensor_tensor_scan(q_den[:, b, 1:SEQ + 1], ex[0][:, b, :], ex[1][:, b, :], 0.0, ALU.mult, ALU.add)
                dve.wait_ge(b2v_ready, n + 1)
                for b in range(GROUP):
                    last = dve.tensor_tensor_scan(p_num[:, b, 1:SEQ + 1], ex[0][:, b, :], b2v[:, b, :], 0.0,
                                                  ALU.mult, ALU.add)
                last.then_inc(p_ready, 1)
                dve.drain()
                dve.wait_ge(wkv_exp, n * 4 + 4)
                dve.tensor_tensor(t_den[:, :, :], ex[2][:, :, :], q_den[:, :, 0:SEQ], ALU.mult)
                dve.drain()
                dve.tensor_tensor(t_den[:, :, :], t_den[:, :, :], ex[3][:, :, :], ALU.add)
                dve.drain()
                dve.reciprocal(rec[:, :, :], t_den[:, :, :])
                dve.drain()
                dve.wait_ge(tnum_ready, n + 1)
                dve.tensor_tensor(rec[:, :, :], rec[:, :, :], t_num[:, :, :], ALU.mult).then_inc(wkv_ready, 1)

            def rec_second_norm(n):
                dve.wait_ge(att_ps, n + 1)
                dve.tensor_tensor(X1[:, :, :], X0[:, :, :], tiles(6), ALU.add)
                dve.drain()
                rec_norm(n, 2, X1, NHAT).then_inc(xhat_ready, 1)

            def rec_feed_mix(n):
                dve.wait_ge(hT_ready, n * 2 + 2)
                token_change()
                token_shift(zk, R_FMK)
                token_shift(zr, R_FMR)

            def rec_feed(n, last_use_of_x=None):
                for h in range(HT):
                    dve.wait_ge(kf_relu, n * HT + h + 1)
                    dve.tensor_tensor(big2[:, h, :], big[:, h, :], big[:, h, :], ALU.mult).then_inc(kf_ready, 1)
                dve.tensor_tensor(X1[:, :, :], X1[:, :, :], X0[:, :, :], ALU.add)
                dve.wait_ge(rf_ready, n + 1)
                dve.wait_ge(ffn_ps, n + 1)
                dve.tensor_tensor(rf[:, :, :], rf[:, :, :], tiles(5), ALU.mult)
                dve.drain()
                dve.tensor_tensor(rf[:, :, :], rf[:, :, :], X1[:, :, :], ALU.add)
                dve.drain()
                moments(rf).then_inc(rvar_ready, 1)
                if last_use_of_x is not None:
                    last_use_of_x()
                dve.wait_ge(rrstd_ready, n * RNS + 3)
                normalised(rf, X).then_inc(layer_done, 1)

            def recurrent(n):
                rec_first_moments(n)
                rec_first_normalised(n)
                rec_key_mix(n)
                rec_value_mix()
                rec_exponents(n)
                rec_wkv(n)
                rec_second_norm(n)
                rec_feed_mix(n)
                rec_feed(n)

            def memory(it):
                dve.wait_ge(rms_ready, it + 1)
                for t in range(TT):
                    last = dve.tensor_scalar(NHAT[:, t, :], X[:, t, :], rms_inv[:, t:t + 1], None, ALU.mult)
                last.then_inc(nhat_ready, 1)
                for t in range(TT):
                    n, lo = CTX + (t % QT + 1) * P, 2 * (t % 2) * 512
                    dve.wait_ge(lg_ps, it * TT + t + 1)
                    dve.tensor_reduce(nmax[:, t:t + 1], psf[:, lo:lo + n], AX.X, ALU.max, negate=True)\
                        .then_inc(lg_max, 1)
                dve.wait_ge(lg_exp, it * TT + TT)
                dve.reciprocal(rinv[:, 0:TT], rsum[:, 0, 0:TT])
                dve.drain()
                dve.wait_ge(av_ps, it + 1)
                dve.wait_ge(out_stored, it * 16 + 1)
                for t in range(TT):
                    dve.scalar_tensor_tensor(out=Y[:, t, :], in0=ps[:, 6, t * D:(t + 1) * D], scalar=rinv[:, t:t + 1],
                                             in1=X[:, t, :], op0=ALU.mult, op1=ALU.subtract)
                dve.drain()
                dve.wait_ge(alpha_ready, it + 1)
                dve.tensor_tensor(Y[:, :, :], Y[:, :, :], alpha[:, :, :], ALU.mult)
                dve.drain()
                dve.scalar_tensor_tensor(out=Y[:, :, :], in0=X[:, :, :], scalar=2.0, in1=Y[:, :, :],
                                         op0=ALU.mult, op1=ALU.add)
                dve.drain()
                layer_norm(it, 1, Y, X).then_inc(layer_done, 1)

            def mixture_top1(it):
                dve.wait_ge(route_ps, it + 1)
                dve.tensor_copy(lg[:, :, :], ps[:, 1, 0:TT * E].rearrange("p (t e) -> p t e", t=TT))
                dve.drain()
                for t in range(TT):
                    dve.max(top[:, t, :], lg[:, t, :])
                dve.drain()
                for t in range(TT):
                    dve.max_index(topi[:, t, :], top[:, t, :], lg[:, t, :])
                dve.drain()
                dve.tensor_copy(topf[:, :, 0:1], topi[:, :, 0:1])
                dve.drain()
                for t in range(TT):
                    last = dve.tensor_scalar(onehot[:, t, :], iota_e[:, :], topf[:, t, 0:1], None, ALU.is_equal)
                last.then_inc(onehot_ready, 1)
                dve.wait_ge(xT_ready, it * 5 + 2)
                for e in range(E):
                    dve.wait_ge(pick_ps, it * E + e + 1)
                    dve.tensor_tensor(XE[:, e % 2, :], XT[:, :], bank(3 + e % 2), ALU.mult).then_inc(xe_ready, 1)
                for t in range(TT):
                    dve.tensor_tensor(NHAT[:, t, :], X[:, t, :], bo_bc[:, :], ALU.add)
                    dve.tensor_tensor(X1[:, t, :], X[:, t, :], beta_bc[:, :], ALU.add)
                dve.drain()
                dve.wait_ge(moe_ps, it + 1)
                dve.tensor_tensor(Y[:, :, :], NHAT[:, :, :], tiles(1), ALU.add)
                dve.drain()
                moments(Y).then_inc(var_ready, 1)
                dve.drain()
                for t in range(TT):
                    dve.scalar_tensor_tensor(out=Y[:, t, :], in0=Y[:, t, :], scalar=mv[:, t, 0:1], in1=gamma_bc[:, :],
                                             op0=ALU.subtract, op1=ALU.mult)
                dve.drain()
                dve.wait_ge(rstd_ready, it * LNS + 2)
                for t in range(TT):
                    dve.scalar_tensor_tensor(out=Y[:, t, :], in0=Y[:, t, :], scalar=rstd[:, t:t + 1], in1=X1[:, t, :],
                                             op0=ALU.mult, op1=ALU.add)
                dve.drain()
                layer_norm(it, 3, Y, X).then_inc(layer_done, 1)

            def sparse_attention(it):
                def mask_head(hh, u):
                    dve.tensor_scalar(qm[:, u, :], qT[:, :], head_mask[:, bass.ds(2 * hh + u, 1)], None, ALU.mult)\
                        .then_inc(qm_ready, 1)

                def row_max(hh, u):
                    dve.wait_ge(s_ps, it * NH + 2 * hh + u + 1)
                    dve.tensor_reduce(snm[:, u, :].rearrange("p (b t) -> p b t", b=GROUP),
                                      ps[:, 2 * u:2 * u + 2, 0:QT * KW].rearrange("p b (t k) -> p b t k", t=QT),
                                      AX.X, ALU.max, negate=True).then_inc(s_max, 1)

                def turned(hh, u):
                    dve.wait_ge(sT_ps, it * NH + 2 * hh + u + 1)
                    dve.reciprocal(sri[:, u, :], srs[:, u, :])
                    dve.tensor_copy(G[:, :, bass.ds(2 * hh + u, 1), :],
                                    SP_[:, u, :, 0:CB].rearrange("p (b t) c -> p b t c", t=QT)[:, :, 1:2, :])
                    dve.drain()
                    dve.tensor_copy(sri_all[:, bass.ds(2 * hh + u, 1), :], sri[:, u, :].unsqueeze(1))

                def normalise(hh, u):
                    dve.wait_ge(so_ps, it * NH + 2 * hh + u + 1)
                    dve.tensor_tensor(O[:, :, bass.ds((2 * hh + u) * HD, HD)],
                                      ps[:, 6 + u, 0:TT * HD].rearrange("p (t d) -> p t d", t=TT),
                                      sri[:, u, :].unsqueeze(2).to_broadcast([P, TT, HD]), ALU.mult)\
                        .then_inc(so_ready, 1)

                def two_heads(hh, more, masks):
                    turned(hh, 0)
                    if more:
                        row_max(hh + 1, 0)
                    if masks:
                        mask_head(hh + 2, 0)
                    turned(hh, 1)
                    normalise(hh, 0)
                    if more:
                        row_max(hh + 1, 1)
                    if masks:
                        mask_head(hh + 2, 1)
                    normalise(hh, 1)

                dve.wait_ge(xT_ready, it * 5 + 3)
                for b in range(GROUP):
                    last = dve.tensor_copy(XTg[:, b, :, :], XT[:, b * SEQ + P - CB:b * SEQ + P].unsqueeze(1)
                                           .to_broadcast([P, NH, CB]))
                last.then_inc(xg_ready, 1)
                dve.wait_ge(qk_ready, it * 2 + 1)
                mask_head(0, 0)
                mask_head(0, 1)
                dve.wait_ge(qkv_ps, it * 4 + 4)
                dve.tensor_tensor(Vg[:, :, :].rearrange("p b (h d) -> p b h d", h=NH),
                                  ps[:, 4, 0:GROUP * D].rearrange("p (b h d) -> p b h d", b=GROUP, h=NH),
                                  head_mask[:, :].unsqueeze(2).unsqueeze(1).to_broadcast([P, GROUP, NH, HD]), ALU.mult)
                for u in range(2):
                    row_max(0, u)
                    mask_head(1, u)
                with dve.Fori(0, NH // 2 - 2) as hh:
                    two_heads(hh, True, True)
                two_heads(NH // 2 - 2, True, False)
                two_heads(NH // 2 - 1, False, False)
                dve.drain().then_inc(g_ready, 1)
                dve.wait_ge(og_ps, it + 1)
                dve.tensor_tensor(Og[:, :, :, :], ps[:, 5, 0:GROUP * D].rearrange("p (b h d) -> p b h d", b=GROUP, h=NH),
                                  sri_all[:, :, :].rearrange("p h (b t) -> p b h t", t=QT)[:, :, :, 1:2]
                                  .to_broadcast([P, GROUP, NH, HD]), ALU.mult)
                dve.drain()
                second = O[:, :, :].rearrange("p (b t) d -> p b t d", t=QT)[:, :, 1:2, :].rearrange(
                    "p b o d -> p b (o d)")
                dve.tensor_tensor(second, second, Og[:, :, :, :].rearrange("p b h d -> p b (h d)"), ALU.add)\
                    .then_inc(so_ready, 1)
                dve.wait_ge(proj_ps, it + 1)
                dve.tensor_tensor(Y[:, :, :], X[:, :, :], tiles(1), ALU.add)
                dve.drain()
                layer_norm(it, 4, Y, X).then_inc(layer_done, 1)

            def cross_attention(it, more_groups=True):
                def context_values(j, u, b, seq):
                    dve.wait_ge(vx_ps, it * (2 * PAIRS) + 2 * j + seq + 1)
                    dve.tensor_copy(Vx[u][:, seq * KT:(seq + 1) * KT, :], tiles(b)).then_inc(vx_ready, 1)

                def row_max(j, s):
                    dve.wait_ge(c_ps, it * (NS * PAIRS) + j * NS + s + 1)
                    dve.tensor_reduce(nmax[:, s:s + 1], bank(s % 2), AX.X, ALU.max, negate=True)\
                        .then_inc(c_max, 1)

                def turned(j, s):
                    dve.wait_ge(cT_ps, it * (NS * PAIRS) + j * NS + s + 1)
                    dve.tensor_copy(cprobT[:, 0, :], bank(2)).then_inc(cT_even, 1)

                def normalise(j, u):
                    dve.wait_ge(o_ps, it * PAIRS + j + 1)
                    for h in range(2):
                        last = dve.tensor_tensor(
                            Cx[:, :, h * DK:(h + 1) * DK], tiles(4 + u)[:, :, h * DK:(h + 1) * DK],
                            rinv[:, h * TT:(h + 1) * TT].unsqueeze(2).to_broadcast([P, TT, DK]), ALU.mult)
                    last.then_inc(o_ready, 1)

                def add_projected(j, b):
                    dve.wait_ge(wo_ps, it * PAIRS + j + 1)
                    dve.tensor_tensor(X1[:, :, :], X1[:, :, :], tiles(b), ALU.add).then_inc(wo_added, 1)

                def pair(j, u, first=False, more=True):
                    for s in range(NS):
                        if s == 0 and not first:
                            normalise(j - 1, 1 - u)
                        if s % 2 == 0:
                            turned(j, s)
                        if s == 4 and not first:
                            add_projected(j - 1, 6)
                        if s == 6 and more:
                            context_values(j + 1, 1 - u, 6, 0)
                        if s == 7 and more:
                            context_values(j + 1, 1 - u, 7, 1)
                        if s + 2 < NS:
                            row_max(j, s + 2)
                        elif more:
                            row_max(j + 1, s + 2 - NS)
                        if more_groups and not more:
                            if s == 0:
                                rec_first_moments(it + 1)
                            if s == 1:
                                rec_first_normalised(it + 1)
                            if s == 4:
                                rec_key_mix(it + 1)
                            if s == 5:
                                rec_value_mix()
                    dve.wait_ge(c_exp, it * (NS * PAIRS) + (j + 1) * NS)
                    dve.reciprocal(rinv[:, :], rsum[:, u, :])
                    dve.drain()

                dve.drain()
                dve.tensor_copy(X1[:, :, :], X[:, :, :]).then_inc(wo_added, 1)
                context_values(0, 0, 4, 0)
                context_values(0, 0, 5, 1)
                row_max(0, 0)
                row_max(0, 1)
                pair(0, 0, first=True)
                with dve.Fori(0, PAIRS // 2 - 1) as jj:
                    pair(2 * jj + 1, 1)
                    pair(2 * jj + 2, 0)
                pair(PAIRS - 1, 1, more=False)
                normalise(PAIRS - 1, 1)
                add_projected(PAIRS - 1, 3)
                dve.drain()
                layer_norm(it, 5, X1, X).then_inc(layer_done, 1)

            def mixture_top2(it, more=True):
                if more:
                    rec_exponents(it + 1)
                dve.wait_ge(r1_ps, it + 1)
                dve.tensor_copy(lg[:, :, :], ps[:, 1, 0:TT * E].rearrange("p (t e) -> p t e", t=TT))
                dve.drain()
                for t in range(TT):
                    dve.max(top[:, t, :], lg[:, t, :])
                dve.drain()
                dve.tensor_tensor(ex1[:, :, :], lg[:, :, :], top[:, :, 0:1].to_broadcast([P, TT, E]), ALU.subtract)\
                    .then_inc(e1_arg, 1)
                for t in range(TT):
                    dve.max_index(topi[:, t, :], top[:, t, :], lg[:, t, :])
                dve.drain()
                dve.tensor_copy(topf[:, :, :], topi[:, :, 0:2])
                dve.drain()
                for t in range(TT):
                    dve.tensor_scalar(A[:, t, :], iota_e[:, :], topf[:, t, 0:1], None, ALU.is_equal)
                    dve.tensor_scalar(onehot[:, t, :], iota_e[:, :], topf[:, t, 1:2], None, ALU.is_equal)
                dve.drain()
                dve.tensor_tensor(A[:, :, :], A[:, :, :], onehot[:, :, :], ALU.add)
                dve.drain()
                dve.tensor_copy(A_bf[:, :, :], A[:, :, :]).then_inc(two_hot, 1)
                dve.wait_ge(e1_exp, it + 1)
                dve.tensor_reduce(esum[:, :], ex1[:, :, :], AX.X, ALU.add)
                dve.drain()
                dve.reciprocal(einv[:, :], esum[:, :])
                dve.drain()
                dve.tensor_tensor(ex1[:, :, :], ex1[:, :, :], einv[:, :].unsqueeze(2).to_broadcast([P, TT, E]), ALU.mult)
                dve.wait_ge(pos_ps, it + 1)
                dve.scalar_tensor_tensor(out=posA[:, :, :], in0=ps[:, 2, 0:TT * E].rearrange("p (t e) -> p t e", t=TT),
                                         scalar=1.0, in1=A[:, :, :], op0=ALU.add, op1=ALU.mult)
                dve.drain()

                def slots(m, t):
                    return m[:, t, :].rearrange("p (e c) -> p e c", e=E)

                def per_expert(m, t):
                    return m[:, t, :].unsqueeze(2).to_broadcast([P, E, CAP])

                for t in range(TT):
                    last = dve.tensor_tensor(slots(disp, t), iota_c[:, :].unsqueeze(1).to_broadcast([P, E, CAP]),
                                             per_expert(posA, t), ALU.is_equal)
                last.then_inc(disp_ready, 1)
                dve.drain()
                for t in range(TT):
                    last = dve.tensor_tensor(slots(comb, t), slots(disp, t), per_expert(ex1, t), ALU.mult)
                last.then_inc(comb_ready, 1)
                def add_mixture():
                    dve.wait_ge(comb_ps, it + 1)
                    dve.tensor_tensor(Y[:, :, :], X[:, :, :], tiles(4), ALU.add)
                    dve.drain()

                if more:
                    rec_wkv(it + 1)
                    rec_second_norm(it + 1)
                    rec_feed_mix(it + 1)
                    rec_feed(it + 1, add_mixture)
                else:
                    add_mixture()
                layer_norm(it, 6, Y, Y).then_inc(out_ready, 1)

            def group(it, more=True):
                memory(it)
                mixture_top1(it)
                sparse_attention(it)
                cross_attention(it, more)
                mixture_top2(it, more)

            recurrent(0)
            with dve.Fori(0, ITERS - 1) as it:
                group(it)
            group(ITERS - 1, more=False)


_INS = [
    'x', 'ctx_1024', 'L0_attn_ln_att_g', 'L0_attn_ln_att_b', 'L0_attn_ln_ffn_g', 'L0_attn_ln_ffn_b',
    'L0_attn_att_time_decay', 'L0_attn_att_time_first', 'L0_attn_att_mix_k', 'L0_attn_att_mix_v',
    'L0_attn_att_mix_r', 'L0_attn_att_wk', 'L0_attn_att_wv', 'L0_attn_att_wr', 'L0_attn_att_wo',
    'L0_attn_ffn_mix_k', 'L0_attn_ffn_mix_r', 'L0_attn_ffn_wk', 'L0_attn_ffn_wv', 'L0_attn_ffn_wr',
    'L0_xattn_q_w', 'L0_xattn_k_w', 'L0_xattn_norm_w', 'L0_xattn_gate_w', 'L0_xattn_gate_b',
    'L0_ffn_Wr', 'L0_ffn_W1', 'L0_ffn_b1', 'L0_ffn_Wo', 'L0_ffn_bo', 'L0_ffn_gamma', 'L0_ffn_beta',
    'L1_attn_W_attn', 'L1_attn_b_attn', 'L1_attn_W_proj', 'L1_attn_b_proj',
    'L1_xattn_Wq', 'L1_xattn_bq', 'L1_xattn_Wk', 'L1_xattn_bk', 'L1_xattn_Wv', 'L1_xattn_bv', 'L1_xattn_Wo',
    'L1_ffn_Wr', 'L1_ffn_br', 'L1_ffn_W1', 'L1_ffn_b1', 'L1_ffn_W2', 'L1_ffn_b2',
]


def kernel(**inputs):
    import numpy as _np
    import concourse.bacc as _bacc
    from concourse import mybir as _mybir
    from concourse.bass_utils import run_bass_kernel_spmd as _run

    nc = _bacc.Bacc("TRN2", target_bir_lowering=False, num_devices=1)
    arrays, args = {}, []
    for name in _INS:
        a = _np.ascontiguousarray(inputs[name])
        arrays[f"in_{name}_dram"] = a
        args.append(nc.dram_tensor(f"in_{name}_dram", a.shape, _mybir.dt.from_np(a.dtype), kind="ExternalInput").ap())
    out = nc.dram_tensor("out_0_dram", (BATCH, SEQ, D), F32, kind="ExternalOutput").ap()
    decoder_kernel(nc, *args, out)
    r = _run(nc, [arrays], core_ids=[0])
    return r.results[0]["out_0_dram"]
```

```python
from contextlib import ExitStack

import concourse.bass as bass
from concourse import mybir

F32 = mybir.dt.float32
BF16 = mybir.dt.bfloat16
U32 = mybir.dt.uint32
ALU = mybir.AluOpType
ACT = mybir.ActivationFunctionType
AX = mybir.AxisListType

P = 128
D = 128
BATCH, SEQ, CTX = 8, 256, 512
GROUP = 2
ITERS = BATCH // GROUP
TOK = GROUP * SEQ
TT = TOK // P
QT = SEQ // P
KT = CTX // P
CT = GROUP * KT
LIN = 512
HT = LIN // P
E = 8
NH, HD = 16, 8
CB = 8
KW = CB + P
XH, DK = 16, 64
PAIRS = XH // 2
CAP = max(1, int(SEQ / E * 1.25))
SLOTS = E * CAP
SB = (SLOTS + P - 1) // P
MASKED = -1.0e30

R_LNG, R_LNB, R_FLNG, R_FLNB, R_DECAY, R_FIRST, R_MK, R_MV, R_MR, R_FMK, R_FMR, R_NORMW = range(12)
R_BATT = 12
R_BQ = 14
R_BK = R_BQ + PAIRS
R_B1 = R_BK + PAIRS
R_B2 = R_B1 + E * HT
N_COL = R_B2 + E

V_GATEB, V_BV, V_BO, V_BPROJ, V_GAMMA, V_BETA, V_NORMW = range(7)
V_BR = 7 * D
V_XBV = V_BR + E
N_ROW = V_XBV + PAIRS * D


def decoder_kernel(
    nc, x, ctx_in,
    ln_att_g, ln_att_b, ln_ffn_g, ln_ffn_b, time_decay, time_first, mix_k, mix_v, mix_r,
    att_wk, att_wv, att_wr, att_wo, ffn_mix_k, ffn_mix_r, ffn_wk, ffn_wv, ffn_wr,
    q_w, k_w, norm_w, gate_w, gate_b,
    m0_wr, m0_w1, m0_b1, m0_wo, m0_bo, m0_gamma, m0_beta,
    a1_w, a1_b, a1_wp, a1_bp,
    x1_wq, x1_bq, x1_wk, x1_bk, x1_wv, x1_bv, x1_wo,
    m1_wr, m1_br, m1_w1, m1_b1, m1_w2, m1_b2,
    out,
):
    with ExitStack() as stack:
        def sb(name, shape, dt=F32):
            return stack.enter_context(nc.sbuf_tensor(name, shape, dt))

        def semaphore(name):
            return stack.enter_context(nc.semaphore(name))

        wk, wv, wr, wo = (sb(n, [P, D]) for n in ("wk", "wv", "wr", "wo"))
        fwk = sb("fwk", [P, LIN])
        fwv = sb("fwv", [P, HT, D])
        fwr = sb("fwr", [P, D])
        qw, kw, gw_raw = (sb(n, [P, D]) for n in ("qw", "kw", "gw_raw"))
        qk_fold = sb("qk_fold", [P, D])
        gwT = sb("gwT", [P, D])
        wr0_raw = sb("wr0_raw", [E, D])
        wr0T = sb("wr0T", [P, E])
        w1a = sb("w1a", [P, E, LIN])
        PARTS = 3
        b1_parts = sb("b1_parts", [PARTS * E, LIN], BF16)
        wo0 = sb("wo0", [P, HT, D])
        wattn = sb("wattn", [P, 3 * D])
        wproj = sb("wproj", [P, D])
        xwT = sb("xwT", [P, 4, PAIRS, D])
        wr1 = sb("wr1", [P, E])
        w1b = sb("w1b", [P, E, LIN])
        w2b = sb("w2b", [P, E, HT, D])
        col_rows = sb("col_rows", [N_COL, D])
        cols = sb("cols", [P, N_COL])
        decay_w = sb("decay_w", [P, 1])
        decay_e = sb("decay_e", [P, 1])
        bq_scaled = sb("bq_scaled", [P, PAIRS])
        battq_scaled = sb("battq_scaled", [P, 1])
        rows = sb("rows", [1, N_ROW])
        gamma_bc, beta_bc, normw_bc, bo_bc, bv_bc, bproj_bc = (
            sb(n, [P, D]) for n in ("gamma_bc", "beta_bc", "normw_bc", "bo_bc", "bv_bc", "bproj_bc"))
        br_bc = sb("br_bc", [P, E])
        xbv_bc = sb("xbv_bc", [P, PAIRS, D])

        ident = sb("ident", [P, P])
        ident_bf = sb("ident_bf", [P, P], BF16)
        causal = sb("causal", [P, P], BF16)
        sparse = sb("sparse", [P, QT * KW], BF16)
        before = sb("before", [P, P], BF16)
        ones_bf = sb("ones_bf", [P, P], BF16)
        ones = sb("ones", [1, P])
        pick = sb("pick", [E, E, P], BF16)
        head_mask = sb("head_mask", [P, NH])
        zeros_bf = sb("zeros_bf", [P, P], BF16)
        pair_mask = sb("pair_mask", [P, NH // 2, NH])
        iota_e = sb("iota_e", [P, PARTS * E])
        iota_ei = sb("iota_ei", [P, PARTS * E], mybir.dt.int32)
        iota_c = sb("iota_c", [P, CAP])
        iota_ci = sb("iota_ci", [P, CAP], mybir.dt.int32)
        neg_half = sb("neg_half", [P, TT])
        eps_ln = sb("eps_ln", [P, TT])
        eps_rms = sb("eps_rms", [P, TT])
        eps_post = sb("eps_post", [P, TT])

        arena = sb("arena", [P, 18 * TOK])

        class Carve:

            def __init__(self):
                self.at = 0

            def __call__(self, *shape, parts=P):
                n = 1
                for k in shape:
                    n *= k
                view = arena[0:parts, self.at:self.at + n]
                self.at += n
                assert self.at <= 18 * TOK
                if len(shape) == 2:
                    return view.rearrange("p (a b) -> p a b", b=shape[1])
                if len(shape) == 3:
                    return view.rearrange("p (a b c) -> p a b c", b=shape[1], c=shape[2])
                return view

        setup, att_c, sparse_c, cross_c, mix_c = (Carve() for _ in range(5))
        xw_raw = setup(4, PAIRS, D)
        causal_f, before_f = setup(P), setup(P)
        sparse_f = setup(QT, KW)
        pick_f = setup(E, P, parts=E)
        b1_rest, b1_part = setup(LIN, parts=E), setup(LIN, parts=E)
        b1_mid, b1_low = (sb(n, [E, LIN], BF16) for n in ("b1_mid", "b1_low"))

        X0 = sb("X0", [P, TT, D])
        X1 = sb("X1", [P, TT, D])
        X = sb("X", [P, TT, D])
        Y = sb("Y", [P, TT, D])
        NHAT = sb("NHAT", [P, TT, D])
        XT = sb("XT", [P, TOK])
        ctx = sb("ctx", [P, CT, D])
        ctxT = sb("ctxT", [P, CT * P])
        bn = sb("bn", [P, TT, 6])
        mv = sb("mv", [P, TT, 2])
        vare = sb("vare", [P, TT])
        rstd = sb("rstd", [P, TT])
        hT = sb("hT", [P, GROUP, SEQ + 1])
        o_max, p_num, q_den = (sb(n, [P, GROUP, SEQ + 1]) for n in ("o_max", "p_num", "q_den"))
        w_bc = sb("w_bc", [P, SEQ])
        big = sb("big", [P, HT, TOK])
        big2 = sb("big2", [P, HT, TOK])
        rf = sb("rf", [P, TT, D])
        ssq, ssq_eps, rms_inv = (sb(n, [P, TT]) for n in ("ssq", "ssq_eps", "rms_inv"))
        nT = sb("nT", [P, TOK])
        nTok = sb("nTok", [P, TT, D])
        qpT = sb("qpT", [P, TOK])
        alpha = sb("alpha", [P, TT, D])
        prob = att_c(2, CTX + SEQ)
        probT = att_c(2, CTX + SEQ)
        nmax = sb("nmax", [P, 8])
        rsum = sb("rsum", [P, 2, 8])
        rinv = sb("rinv", [P, 8])
        lg = sb("lg", [P, TT, E])
        top = sb("top", [P, TT, E])
        topi = sb("topi", [P, TT, E], U32)
        topf = sb("topf", [P, TT, 2])
        onehot = sb("onehot", [P, TT, PARTS * E])
        ohT = sb("ohT", [PARTS * E, TOK], BF16)
        XE = big2[:, 0:2, :]
        qT, kT = sb("qT", [P, TOK]), sb("kT", [P, TOK])
        V = sb("V", [P, TT, D])
        qm = sparse_c(2, TOK)
        SP_ = sparse_c(2, TT, KW)
        spT = sparse_c(2, TOK)
        XTg = sparse_c(GROUP, NH, CB)
        Vg = sparse_c(GROUP, D)
        G = sparse_c(GROUP, NH, CB)
        GT = sparse_c(GROUP, P)
        Vgb = sparse_c(GROUP, NH, HD)
        Vm = sparse_c(TT, D)
        snm = sb("snm", [P, 2, TT])
        srs = sb("srs", [P, 2, TT])
        sri = sb("sri", [P, 2, TT])
        O = sb("O", [P, TT, D])
        OT = sb("OT", [P, TOK])
        wq_s, wk_s = sb("wq_s", [P, D]), sb("wk_s", [P, D])
        cprob, cprobT = cross_c(2, CTX), cross_c(4, CTX)
        QTs = cross_c(2, TOK)
        KTs = cross_c(2, CT * P)
        Vx = [cross_c(CT, P) for _ in range(2)]
        CTs = cross_c(TOK)
        Rs = cross_c(TOK)
        ex1 = sb("ex1", [P, TT, E])
        esum = sb("esum", [P, TT])
        einv = sb("einv", [P, TT])
        A = sb("A", [P, TT, E])
        A_bf = sb("A_bf", [P, TT, E], BF16)
        posA = sb("posA", [P, TT, E])
        disp = mix_c(TT, SLOTS)
        comb = mix_c(TT, SLOTS)
        combT = mix_c(SB, TOK)
        xb = mix_c(GROUP, SLOTS)
        hid = mix_c(2, HT, GROUP * CAP)
        yT = mix_c(GROUP, SLOTS)
        ySl = mix_c(GROUP, SB, D)

        def by_seq(view):
            return view.rearrange("p (b s) -> p b s", b=GROUP)

        def flat(view):
            return view[:, :, :].rearrange("p t d -> p (t d)")

        zk, zv, zr = by_seq(qT[:, :]), by_seq(kT[:, :]), by_seq(qpT[:, :])
        dT, kS, vS = by_seq(OT[:, :]), by_seq(nT[:, :]), by_seq(flat(V))
        rS, o_new, rec = by_seq(flat(O)), by_seq(flat(nTok)), by_seq(flat(alpha))
        ex = [by_seq(big[:, i, :]) for i in range(4)]
        b2v, bv_, t_num, t_den = (by_seq(big2[:, i, :]) for i in range(4))

        ps = stack.enter_context(nc.psum_tensor("ps", [P, 8, 512], F32))

        def bank(i):
            return ps[:, i, :]

        def tiles(i):
            return ps[:, i, :].rearrange("p (t d) -> p t d", t=TT)

        def seqs(i):
            return ps[:, i, :].rearrange("p (b s) -> p b s", b=GROUP)

        psf = ps[:, :, :].rearrange("p b n -> p (b n)")

        rec_loaded, weights_loaded = semaphore("rec_loaded"), semaphore("weights_loaded")
        layers_loaded = semaphore("layers_loaded")
        b1_loaded, b1_split, b1_placed = semaphore("b1_loaded"), semaphore("b1_split"), semaphore("b1_placed")
        consts_ready = semaphore("consts_ready")
        wT_ps = semaphore("wT_ps")
        wT_sb = semaphore("wT_sb")
        cols_ready = semaphore("cols_ready")
        x_loaded, ctx_loaded, out_stored = (semaphore(n) for n in ("x_loaded", "ctx_loaded", "out_stored"))
        RNS, LNS = 3, 6
        rvar_ready, rrstd_ready = semaphore("rvar_ready"), semaphore("rrstd_ready")
        var_ready, rstd_ready = semaphore("var_ready"), semaphore("rstd_ready")
        p_ready, tnum_ready = semaphore("p_ready"), semaphore("tnum_ready")
        xhat_ready, hT_ps, hT_ready = semaphore("xhat_ready"), semaphore("hT_ps"), semaphore("hT_ready")
        mix_ready, kvr_ps, kvr_ready = semaphore("mix_ready"), semaphore("kvr_ps"), semaphore("kvr_ready")
        wkv_arg, wkv_exp = semaphore("wkv_arg"), semaphore("wkv_exp")
        b2v_ready, bv_ready, wkv_ready = semaphore("b2v_ready"), semaphore("bv_ready"), semaphore("wkv_ready")
        att_ps = semaphore("att_ps")
        kf_ps, kf_relu, kf_ready = semaphore("kf_ps"), semaphore("kf_relu"), semaphore("kf_ready")
        rf_ps, rf_ready, ffn_ps = semaphore("rf_ps"), semaphore("rf_ready"), semaphore("ffn_ps")
        LAYERS = 5
        layer_done, out_ready = semaphore("layer_done"), semaphore("out_ready")
        xT_ps, xT_ready = semaphore("xT_ps"), semaphore("xT_ready")
        ctxT_ps, ctxT_ready = semaphore("ctxT_ps"), semaphore("ctxT_ready")
        ssq_ready, rms_ready, nhat_ready = semaphore("ssq_ready"), semaphore("rms_ready"), semaphore("nhat_ready")
        ntok_ready, nT_ps, nT_ready = semaphore("ntok_ready"), semaphore("nT_ps"), semaphore("nT_ready")
        gate_ps, alpha_ready = semaphore("gate_ps"), semaphore("alpha_ready")
        qp_ps, qp_ready = semaphore("qp_ps"), semaphore("qp_ready")
        lg_ps, lg_max, lg_exp = semaphore("lg_ps"), semaphore("lg_max"), semaphore("lg_exp")
        pT_ps, pT_ready, av_ps = semaphore("pT_ps"), semaphore("pT_ready"), semaphore("av_ps")
        route_ps, onehot_ready = semaphore("route_ps"), semaphore("onehot_ready")
        ohT_ps, ohT_ready = semaphore("ohT_ps"), semaphore("ohT_ready")
        pick_ps, xe_ready = semaphore("pick_ps"), semaphore("xe_ready")
        pre_ps, inter_ready, moe_ps = semaphore("pre_ps"), semaphore("inter_ready"), semaphore("moe_ps")
        qkv_ps, qk_ready, v_ready = semaphore("qkv_ps"), semaphore("qk_ready"), semaphore("v_ready")
        qm_ready, s_ps, s_max, s_exp = (semaphore(n) for n in ("qm_ready", "s_ps", "s_max", "s_exp"))
        sT_ps, sT_ready = semaphore("sT_ps"), semaphore("sT_ready")
        xg_ready, g_ready, gT_ps, gT_ready = (semaphore(n) for n in ("xg_ready", "g_ready", "gT_ps", "gT_ready"))
        vm_ready, so_ps = semaphore("vm_ready"), semaphore("so_ps")
        sinv_ps, sinv_ready = semaphore("sinv_ps"), semaphore("sinv_ready")
        oT_ps, oT_ready, proj_ps = semaphore("oT_ps"), semaphore("oT_ready"), semaphore("proj_ps")
        NS = 2 * TT
        staged = semaphore("staged")
        q_ps, k_ps, vx_ps = semaphore("q_ps"), semaphore("k_ps"), semaphore("vx_ps")
        q_ready, k_ready = semaphore("q_ready"), semaphore("k_ready")
        vx_ready = semaphore("vx_ready")
        c_ps, c_max, c_exp = (semaphore(n) for n in ("c_ps", "c_max", "c_exp"))
        cT_ps, cT_even, cT_odd = semaphore("cT_ps"), semaphore("cT_even"), semaphore("cT_odd")
        o_ps, rinv_ready, inv_ps, inv_ready, context_ready = (
            semaphore(n) for n in ("o_ps", "rinv_ready", "inv_ps", "inv_ready", "context_ready"))
        wo_ps, wo_added = semaphore("wo_ps"), semaphore("wo_added")
        r1_ps, e1_arg, e1_exp = semaphore("r1_ps"), semaphore("e1_arg"), semaphore("e1_exp")
        two_hot, pos_ps, disp_ready = semaphore("two_hot"), semaphore("pos_ps"), semaphore("disp_ready")
        comb_ready, combT_ps, combT_ready = semaphore("comb_ready"), semaphore("combT_ps"), semaphore("combT_ready")
        xb_ps, xb_ready = semaphore("xb_ps"), semaphore("xb_ready")
        hid_ps, hid_ready = semaphore("hid_ps"), semaphore("hid_ready")
        y_ps, y_ready = semaphore("y_ps"), semaphore("y_ready")
        ysl_ps, ysl_ready, comb_ps = semaphore("ysl_ps"), semaphore("ysl_ready"), semaphore("comb_ps")

        def one_row(v):
            return v.rearrange("(a n) -> a n", a=1)

        def half(w, n):
            return w.rearrange("(t p) n -> p t n", p=P)

        loads = [
            (qw[:, :], q_w), (kw[:, :], k_w), (gw_raw[:, :], gate_w), (wr0_raw[:, :], m0_wr),
            (xw_raw[:, 0, :, :], half(x1_wq, D)), (xw_raw[:, 1, :, :], half(x1_wk, D)),
            (xw_raw[:, 2, :, :], half(x1_wv, D)),
            (xw_raw[:, 3, :, :], x1_wo.rearrange("p (j f) -> p j f", f=P)),
        ]
        layer_loads = [
            (w1a[:, :, :], m0_w1.rearrange("e c h -> c e h")), (wo0[:, :, :], half(m0_wo, D)),
            (wattn[:, :], a1_w), (wproj[:, :], a1_wp), (wr1[:, :], m1_wr),
            (w1b[:, :, :], m1_w1.rearrange("e c h -> c e h")),
        ] + [(w2b[:, e, :, :], half(m1_w2[e, :, :], D)) for e in range(E)]
        rec_loads = []
        for row, v in ((R_LNG, ln_att_g), (R_LNB, ln_att_b), (R_FLNG, ln_ffn_g), (R_FLNB, ln_ffn_b),
                       (R_DECAY, time_decay), (R_FIRST, time_first), (R_MK, mix_k), (R_MV, mix_v),
                       (R_MR, mix_r), (R_FMK, ffn_mix_k), (R_FMR, ffn_mix_r), (R_NORMW, norm_w)):
            rec_loads.append((col_rows[row:row + 1, :], one_row(v)))
        rec_loads += [
            (col_rows[R_BATT:R_BATT + 2, :], a1_b[0:2 * D].rearrange("(j p) -> j p", p=P)),
            (col_rows[R_BQ:R_BQ + PAIRS, :], x1_bq.rearrange("(j p) -> j p", p=P)),
            (col_rows[R_BK:R_BK + PAIRS, :], x1_bk.rearrange("(j p) -> j p", p=P)),
            (col_rows[R_B1:R_B1 + E * HT, :], m1_b1.rearrange("e (h p) -> (e h) p", p=P)),
            (col_rows[R_B2:R_B2 + E, :], m1_b2),
            (wk[:, :], att_wk), (wv[:, :], att_wv), (wr[:, :], att_wr), (wo[:, :], att_wo),
            (fwk[:, :], ffn_wk), (fwv[:, :, :], half(ffn_wv, D)), (fwr[:, :], ffn_wr),
        ]
        for i, v in enumerate((gate_b, a1_b[2 * D:3 * D], m0_bo, a1_bp, m0_gamma, m0_beta, norm_w)):
            loads.append((rows[0:1, i * D:(i + 1) * D], one_row(v)))
        loads.append((rows[0:1, V_BR:V_BR + E], one_row(m1_br)))
        loads.append((rows[0:1, V_XBV:V_XBV + PAIRS * D], one_row(x1_bv)))

        def col(i):
            return cols[:, i:i + 1]

        weight_turns = [([col_rows[:, :]], cols[:, :])]
        for w in range(4):
            for g in range(0, PAIRS, 4):
                weight_turns.append(([xw_raw[:, w, g + i, :] for i in range(4)], xwT[:, w, g:g + 4, :]))
        weight_turns.append(([gw_raw[:, :]], gwT[:, :]))
        weight_turns.append(([wr0_raw[:, :]], wr0T[:, :]))
        N_TURNS = len(weight_turns)
        def row_of(i):
            return rows[0:1, i * D:(i + 1) * D]

        broadcast_rows = [(row_of(i), dst[:, :]) for i, dst in (
            (V_GAMMA, gamma_bc), (V_BETA, beta_bc), (V_NORMW, normw_bc), (V_BO, bo_bc), (V_BV, bv_bc),
            (V_BPROJ, bproj_bc))] + [(rows[0:1, V_BR:V_BR + E], br_bc[:, :])] + [
            (rows[0:1, V_XBV + j * D:V_XBV + (j + 4) * D], xbv_bc[:, j:j + 4, :].rearrange("p j d -> p (j d)"))
            for j in range(0, PAIRS, 4)]
        N_SETUP = N_TURNS + 1 + len(broadcast_rows)
        SETUP_BANKS = 4

        x_v = x.rearrange("(i b) (t p) d -> i p (b t) d", b=GROUP, p=P)
        out_v = out.rearrange("(i b) (t p) d -> i p (b t) d", b=GROUP, p=P)
        ctx_v = ctx_in.rearrange("(i b) (t p) d -> i p (b t) d", b=GROUP, p=P)

        def at(view, it):
            if isinstance(it, int):
                return view[it, :, :, :]
            return view[bass.ds(it, 1), :, :, :].squeeze(0)

        block = stack.enter_context(nc.Block())

        @block.sync
        def _(sp):
            def load_x(it):
                sp.dma_start(X0[:, :, :], at(x_v, it)).then_inc(x_loaded, 16)

            def load_ctx(it):
                sp.dma_start(ctx[:, :, :], at(ctx_v, it)).then_inc(ctx_loaded, 16)

            def store(it):
                sp.wait_ge(out_ready, it * GROUP + GROUP)
                sp.dma_start(at(out_v, it), Y[:, :, :]).then_inc(out_stored, 16)

            load_x(0)
            for dst, src in rec_loads:
                sp.dma_start(dst, src).then_inc(rec_loaded, 16)
            for dst, src in loads:
                sp.dma_start(dst, src).then_inc(weights_loaded, 16)
            load_ctx(0)
            sp.dma_start(b1_rest, m0_b1).then_inc(b1_loaded, 16)
            for dst, src in layer_loads:
                sp.dma_start(dst, src).then_inc(layers_loaded, 16)
            sp.wait_ge(b1_split, 1)
            sp.dma_start(b1_parts[E:2 * E, :], b1_mid[:, :]).then_inc(b1_placed, 16)
            sp.dma_start(b1_parts[2 * E:3 * E, :], b1_low[:, :]).then_inc(b1_placed, 16)
            with sp.Fori(0, ITERS - 1) as it:
                sp.wait_ge(layer_done, it * (LAYERS * GROUP) + GROUP)
                load_x(it + 1)
                sp.wait_ge(av_ps, it + 1)
                load_ctx(it + 1)
                store(it)
            store(ITERS - 1)
            sp.wait_ge(out_stored, 16 * ITERS + 1)

        @block.tensor
        def _(pe):
            def turn_seq(src, b, seq):
                for t in range(seq * QT, (seq + 1) * QT):
                    last = pe.transpose(ps[:, b, t * P:(t + 1) * P], src[:, t, :], ident[:, :])
                return last

            def turn(src, b):
                for seq in range(GROUP):
                    last = turn_seq(src, b, seq)
                return last

            def turn_x(it, n, layers):
                for seq in range(GROUP):
                    pe.wait_ge(layer_done, it * (LAYERS * GROUP) + (layers - 1) * GROUP + seq + 1)
                    last = turn_seq(X, 0, seq)
                last.then_inc(xT_ps, 1)
                pe.wait_ge(xT_ready, it * 5 + n)

            def token_major(b, lhs, w, row=None):
                for t in range(TT):
                    o = ps[:, b, t * D:(t + 1) * D]
                    if row is not None:
                        pe.matmul(o, ones[0:1, :], row, start=True, stop=False)
                    last = pe.matmul(o, lhs[:, t * P:(t + 1) * P], w, start=row is None, stop=True)
                return last

            def set_up(n):
                if n >= SETUP_BANKS:
                    pe.wait_ge(wT_sb, n - SETUP_BANKS + 1)
                b, i = n % SETUP_BANKS, n - N_TURNS
                if n < N_TURNS:
                    for g, src in enumerate(weight_turns[n][0]):
                        k = src.shape[0]
                        last = pe.transpose(ps[:, b, g * P:g * P + k], src, ident[0:k, 0:k])
                elif i == 0:
                    last = pe.matmul(ps[:, b, 0:D], qw[:, :], kw[:, :], start=True, stop=True)
                else:
                    row = broadcast_rows[i - 1][0]
                    last = pe.matmul(ps[:, b, 0:row.shape[1]], ones[0:1, :], row, start=True, stop=True)
                last.then_inc(wT_ps, 1)

            pe.wait_ge(consts_ready, 1)
            pe.wait_ge(rec_loaded, 16 * len(rec_loads))
            set_up(0)

            def turn_ctx(n, more_y=None):
                pe.wait_ge(ctx_loaded, n * 16 + 16)
                if more_y is not None:
                    pe.wait_ge(y_ready, more_y * E + E)
                for g in range(2):
                    for i in range(4):
                        last = pe.transpose(ps[:, 2 + g, i * P:(i + 1) * P], ctx[:, 4 * g + i, :], ident[:, :])
                    last.then_inc(ctxT_ps, 1)

            def rec_turn(n, k, b):
                for seq in range(GROUP):
                    pe.wait_ge(xhat_ready, n * (2 * GROUP) + (k - 1) * GROUP + seq + 1)
                    last = turn_seq(NHAT, b, seq)
                last.then_inc(hT_ps, 1)

            def rec_project(n, i, b):
                z, w = ((zk, wk), (zv, wv), (zr, wr))[i]
                pe.wait_ge(mix_ready, n * 5 + i + 1)
                pe.matmul(bank(b), w[:, :], z[:, :, :], start=True, stop=True).then_inc(kvr_ps, 1)

            def rec_attend(n):
                pe.wait_ge(wkv_ready, n + 1)
                token_major(6, rec[:, :, :].rearrange("p b s -> p (b s)"), wo[:, :]).then_inc(att_ps, 1)

            def rec_widen(n):
                pe.wait_ge(mix_ready, n * 5 + 4)
                for h, b in enumerate((6, 7, 5, 6)):
                    if h == 3:
                        pe.wait_ge(kf_relu, n * HT + 1)
                    pe.matmul(bank(b), fwk[:, h * P:(h + 1) * P], zk[:, :, :], start=True, stop=True)\
                        .then_inc(kf_ps, 1)
                pe.wait_ge(mix_ready, n * 5 + 5)
                pe.wait_ge(kf_relu, n * HT + 2)
                token_major(7, zr[:, :, :].rearrange("p b s -> p (b s)"), fwr[:, :]).then_inc(rf_ps, 1)

            def rec_narrow(n):
                pe.wait_ge(kf_ready, n * HT + HT)
                for t in range(TT):
                    for h in range(HT):
                        last = pe.matmul(ps[:, 5, t * D:(t + 1) * D], big2[:, h, t * P:(t + 1) * P],
                                         fwv[:, h, :], start=(h == 0), stop=(h == HT - 1))
                last.then_inc(ffn_ps, 1)

            def first_recurrent(n):
                rec_turn(n, 1, 5)
                rec_project(n, 0, 4)
                rec_project(n, 1, 7)
                rec_project(n, 2, 5)
                pe.wait_ge(weights_loaded, 16 * len(loads))
                for i in range(1, N_SETUP):
                    set_up(i)
                pe.wait_ge(wT_sb, N_SETUP)
                rec_attend(n)
                turn_ctx(n)
                rec_turn(n, 2, 5)
                rec_widen(n)
                rec_narrow(n)

            def memory(it):
                turn_x(it, 1, 1)
                for seq in range(GROUP):
                    pe.wait_ge(nhat_ready, it * GROUP + seq + 1)
                    last = turn_seq(NHAT, 1, seq)
                last.then_inc(nT_ps, 1)
                pe.wait_ge(nT_ready, it + 1)
                pe.matmul(bank(3), qk_fold[:, :], nT[:, :], start=True, stop=True).then_inc(qp_ps, 1)
                pe.wait_ge(ctxT_ready, it * 2 + 2)
                pe.wait_ge(qp_ready, it + 1)

                def logits(t):
                    b, tq, base = t // QT, t % QT, 2 * (t % 2)
                    nk = (tq + 1) * P
                    q = qpT[:, t * P:(t + 1) * P]
                    pe.matmul(bank(base), q, ctxT[:, b * CTX:(b + 1) * CTX], start=True, stop=True)
                    k0 = b * SEQ + nk - P
                    if tq:
                        pe.matmul(ps[:, base + 1, 0:nk - P], q, nT[:, b * SEQ:k0], start=True, stop=True)
                    pe.matmul(ps[:, base + 1, nk - P:nk], ident_bf[:, :], causal[:, :], start=True, stop=False)
                    pe.matmul(ps[:, base + 1, nk - P:nk], q, nT[:, k0:k0 + P], start=False, stop=True)\
                        .then_inc(lg_ps, 1)

                def turn_probs(t):
                    pe.wait_ge(lg_exp, it * TT + t + 1)
                    for k in range(KT + t % QT + 1):
                        last = pe.transpose(psf[:, 4 * 512 + k * P:4 * 512 + (k + 1) * P],
                                            prob[:, t % 2, k * P:(k + 1) * P], ident[:, :])
                    last.then_inc(pT_ps, 1)

                def values(t):
                    b, tq = t // QT, t % QT
                    if t == 0:
                        pe.wait_ge(ntok_ready, it + 1)
                    pe.wait_ge(pT_ready, it * TT + t + 1)
                    n = KT + tq + 1
                    for k in range(n):
                        v = ctx[:, b * KT + k, :] if k < KT else nTok[:, b * QT + k - KT, :]
                        last = pe.matmul(ps[:, 6, t * D:(t + 1) * D], probT[:, 0, k * P:(k + 1) * P], v,
                                         start=(k == 0), stop=(k == n - 1))
                    return last

                logits(0)
                logits(1)
                token_major(7, XT, gwT[:, :], row_of(V_GATEB)).then_inc(gate_ps, 1)
                for t in range(TT):
                    turn_probs(t)
                    if t + 2 < TT:
                        logits(t + 2)
                    last = values(t)
                last.then_inc(av_ps, 1)

            def mixture_top1(it):
                turn_x(it, 2, 2)
                for t in range(TT):
                    last = pe.matmul(ps[:, 1, t * E:(t + 1) * E], XT[:, t * P:(t + 1) * P], wr0T[:, :],
                                     start=True, stop=True)
                last.then_inc(route_ps, 1)
                pe.wait_ge(onehot_ready, it + 1)
                for t in range(TT):
                    last = pe.transpose(ps[0:PARTS * E, 2, t * P:(t + 1) * P], onehot[:, t, :], ident[:, :])
                last.then_inc(ohT_ps, 1)

                def pick_rows(e):
                    pe.matmul(bank(3 + e % 2), pick[:, e, :], ohT[0:E, :], start=True, stop=True)\
                        .then_inc(pick_ps, 1)

                acc = (5, 6, 7, 0)
                pe.wait_ge(layers_loaded, 16 * len(layer_loads))
                pe.wait_ge(b1_placed, 32)
                pe.wait_ge(ohT_ready, it + 1)
                pick_rows(0)
                pick_rows(1)
                for e in range(E):
                    pe.wait_ge(xe_ready, it * E + e + 1)
                    for h in range(HT):
                        last = pe.matmul(bank(acc[h]), w1a[:, e, h * P:(h + 1) * P], XE[:, e % 2, :],
                                         start=(e == 0), stop=(e == E - 1))
                        if e == E - 1:
                            last.then_inc(pre_ps, 1)
                    if 1 <= e <= HT:
                        pe.matmul(bank(acc[e - 1]), b1_parts[:, (e - 1) * P:e * P], ohT[:, :], start=False, stop=False)
                    if e + 2 < E:
                        pick_rows(e + 2)
                pe.wait_ge(inter_ready, it * HT + HT)
                for t in range(TT):
                    o = ps[:, 1, t * D:(t + 1) * D]
                    for h in range(HT):
                        last = pe.matmul(o, big[:, h, t * P:(t + 1) * P], wo0[:, h, :], start=(h == 0), stop=(h == HT - 1))
                last.then_inc(moe_ps, 1)

            def project_q(it, j, b):
                pe.wait_ge(staged, it * PAIRS + j + 1)
                pe.matmul(bank(b), wq_s[:, :], XT[:, :], start=True, stop=True).then_inc(q_ps, 1)

            def project_k(b, seq):
                pe.matmul(bank(b), wk_s[:, :], ctxT[:, seq * CTX:(seq + 1) * CTX], start=True, stop=True)\
                    .then_inc(k_ps, 1)

            def project_v(j, b, seq):
                for k in range(KT):
                    c = seq * KT + k
                    last = pe.matmul(ps[:, b, k * P:(k + 1) * P], ctxT[:, c * P:(c + 1) * P],
                                     xwT[:, 2, bass.ds(j, 1), :], start=True, stop=True)
                last.then_inc(vx_ps, 1)

            def sparse_attention(it):
                turn_x(it, 3, 3)
                pe.matmul(bank(1), wattn[:, 0:D], XT[:, :], start=True, stop=True).then_inc(qkv_ps, 1)
                pe.matmul(bank(2), wattn[:, D:2 * D], XT[:, :], start=True, stop=True).then_inc(qkv_ps, 1)
                token_major(3, XT, wattn[:, 2 * D:3 * D]).then_inc(qkv_ps, 1)
                pe.wait_ge(xg_ready, it + 1)
                for b in range(GROUP):
                    last = pe.matmul(ps[:, 4, b * D:(b + 1) * D], XTg[:, b, :, :], wattn[:, 2 * D:3 * D],
                                     start=True, stop=True)
                last.then_inc(qkv_ps, 1)

                def scores(hh, u):
                    pe.wait_ge(qm_ready, it * NH + 2 * hh + u + 1)
                    for b in range(GROUP):
                        o = 2 * u + b
                        for tq in range(QT):
                            c = tq * KW
                            k0 = b * SEQ + tq * (SEQ - KW)
                            pe.matmul(ps[:, o, c:c + KW], ident_bf[:, :], sparse[:, c:c + KW], start=True, stop=False)
                            last = pe.matmul(ps[:, o, c:c + KW], qm[:, u, b * SEQ + tq * P:b * SEQ + (tq + 1) * P],
                                             kT[:, k0:k0 + KW], start=False, stop=True)
                    last.then_inc(s_ps, 1)

                def turn_probs(hh, u):
                    pe.wait_ge(s_exp, it * NH + 2 * hh + u + 1)
                    for t in range(TT):
                        lo = 0 if t % QT == 0 else CB
                        last = pe.transpose(ps[:, 4 + u, t * P:(t + 1) * P], SP_[:, u, t, lo:lo + P], ident[:, :])
                    last.then_inc(sT_ps, 1)

                H = D // 2

                def values(hh):
                    pe.wait_ge(vm_ready, it * (NH // 2) + hh + 1)
                    pe.wait_ge(sT_ready, it * NH + 2 * hh + 2)
                    for t in range(TT):
                        for u in range(2):
                            last = pe.matmul(ps[u * H:(u + 1) * H, 6, t * P:(t + 1) * P], Vm[:, t, u * H:(u + 1) * H],
                                             spT[:, u, t * P:(t + 1) * P], start=False, stop=False)
                    last.then_inc(so_ps, 1)

                def two_heads(hh, more):
                    turn_probs(hh, 0)
                    if more:
                        scores(hh + 1, 0)
                    turn_probs(hh, 1)
                    if more:
                        scores(hh + 1, 1)
                    values(hh)

                def add_zeros(start, stop):
                    return pe.matmul(bank(6), zeros_bf[:, :], ones_bf[:, :].unsqueeze(1).to_broadcast([P, TT, P]),
                                     start=start, stop=stop)

                add_zeros(True, False)
                pe.wait_ge(qk_ready, it * 2 + 2)
                scores(0, 0)
                pe.wait_ge(v_ready, it + 1)
                scores(0, 1)
                with pe.Fori(0, NH // 2 - 1) as hh:
                    two_heads(hh, True)
                two_heads(NH // 2 - 1, False)
                pe.wait_ge(g_ready, it + 1)
                for b in range(GROUP):
                    last = pe.transpose(ps[:, 4, b * P:(b + 1) * P], G[:, b, :, :], ident[:, :])
                last.then_inc(gT_ps, 1)
                for t in range(TT):
                    last = pe.transpose(ps[:, 5, t * P:(t + 1) * P], O[:, t, :], ident[:, :])
                last.then_inc(sinv_ps, 1)
                pe.wait_ge(gT_ready, it + 1)
                for b in range(GROUP):
                    t = b * QT + 1
                    pe.matmul(ps[:, 6, t * P:(t + 1) * P], Vg[:, b, :], GT[:, b, :], start=False, stop=False)
                add_zeros(False, True).then_inc(oT_ps, 1)
                pe.wait_ge(oT_ready, it + 1)
                token_major(1, OT, wproj[:, :]).then_inc(proj_ps, 1)
                pe.wait_ge(staged, it * PAIRS + 1)
                project_k(6, 0)
                project_k(3, 1)
                project_v(0, 4, 0)
                project_v(0, 5, 1)

            def cross_attention(it, more_groups=True):
                turn_x(it, 4, 4)

                def scores(j, u, s):
                    t, h = s // 2, s % 2
                    if s == 0:
                        pe.wait_ge(q_ready, it * PAIRS + j + 1)
                        pe.wait_ge(k_ready, it * (2 * PAIRS) + 2 * j + 1)
                    if s == 2 * QT:
                        pe.wait_ge(k_ready, it * (2 * PAIRS) + 2 * j + 2)
                    r = slice(h * DK, (h + 1) * DK)
                    pe.matmul(bank(s % 2), QTs[r, u, t * P:(t + 1) * P],
                              KTs[r, u, (t // QT) * CTX:(t // QT + 1) * CTX], start=True, stop=True).then_inc(c_ps, 1)

                def turn_probs(j, s):
                    pe.wait_ge(c_exp, it * (NS * PAIRS) + j * NS + s + 1)
                    if s and s % 2 == 0:
                        pe.wait_ge(cT_even, it * (NS * PAIRS // 2) + j * (NS // 2) + s // 2)
                    for k in range(KT):
                        last = pe.transpose(ps[:, 2 + s % 2, k * P:(k + 1) * P], cprob[:, s % 2, k * P:(k + 1) * P],
                                            ident[:, :])
                    last.then_inc(cT_ps, 1)

                def values(j, u, seq):
                    if seq == 0:
                        pe.wait_ge(vx_ready, it * (2 * PAIRS) + 2 * j + 2)
                    for copied in (cT_even, cT_odd):
                        pe.wait_ge(copied, it * (NS * PAIRS // 2) + j * (NS // 2) + (seq + 1) * QT)
                    for k in range(KT):
                        for h in range(2):
                            r = slice(h * DK, (h + 1) * DK)
                            last = pe.matmul(ps[r, 4 + u, seq * SEQ:(seq + 1) * SEQ], Vx[u][:, seq * KT + k, r],
                                             cprobT[:, h:4:2, k * P:(k + 1) * P], start=(k == 0), stop=(k == KT - 1))
                    return last

                def spread_sums(j):
                    pe.wait_ge(rinv_ready, it * PAIRS + j + 1)
                    turn(O, 6).then_inc(inv_ps, 1)

                def project_out(j, b):
                    pe.wait_ge(context_ready, it * PAIRS + j + 1)
                    for t in range(TT):
                        last = pe.matmul(ps[:, b, t * D:(t + 1) * D], CTs[:, t * P:(t + 1) * P],
                                         xwT[:, 3, bass.ds(j, 1), :], start=True, stop=True)
                    last.then_inc(wo_ps, 1)

                def between_steps(j, s, first, more):
                    if s == 0 and more:
                        pe.wait_ge(vx_ready, it * (2 * PAIRS) + 2 * j + 2)
                        project_q(it, j + 1, 7)
                    if s == 1 and not first:
                        spread_sums(j - 1)
                    if s == 2 and more:
                        pe.wait_ge(q_ready, it * PAIRS + j + 2)
                        project_k(7, 0)
                    if s == 3 and not first:
                        project_out(j - 1, 6)
                    if s == 4 and more:
                        pe.wait_ge(k_ready, it * (2 * PAIRS) + 2 * j + 3)
                        project_k(7, 1)
                    if s == 5 and more:
                        pe.wait_ge(wo_added, it * (PAIRS + 1) + j + 1)
                        project_v(j + 1, 6, 0)
                    if s == 6 and more:
                        pe.wait_ge(k_ready, it * (2 * PAIRS) + 2 * j + 4)
                        project_v(j + 1, 7, 1)

                def pair(j, u, first=False, more=True):
                    for s in range(NS):
                        turn_probs(j, s)
                        if s + 2 < NS:
                            scores(j, u, s + 2)
                        elif more:
                            scores(j + 1, 1 - u, s + 2 - NS)
                        between_steps(j, s, first, more)
                        if more_groups and not more:
                            if s == 2:
                                rec_turn(it + 1, 1, 7)
                            if s == 6:
                                rec_project(it + 1, 0, 4)
                        if s == 3:
                            values(j, u, 0)
                    values(j, u, 1).then_inc(o_ps, 1)

                project_q(it, 0, 7)
                scores(0, 0, 0)
                scores(0, 0, 1)
                pair(0, 0, first=True)
                with pe.Fori(0, PAIRS // 2 - 1) as jj:
                    pair(2 * jj + 1, 1)
                    pair(2 * jj + 2, 0)
                pair(PAIRS - 1, 1, more=False)
                if more_groups:
                    rec_project(it + 1, 1, 7)
                spread_sums(PAIRS - 1)
                project_out(PAIRS - 1, 3)
                if more_groups:
                    rec_project(it + 1, 2, 5)

            def mixture_top2(it, more=True):
                turn_x(it, 5, 5)
                for t in range(TT):
                    last = pe.matmul(ps[:, 1, t * E:(t + 1) * E], XT[:, t * P:(t + 1) * P], wr1[:, :],
                                     start=True, stop=True)
                last.then_inc(r1_ps, 1)
                pe.wait_ge(two_hot, it + 1)
                for t in range(TT):
                    o = ps[:, 2, t * E:(t + 1) * E]
                    if t % QT:
                        pe.matmul(o, ones_bf[:, :], A_bf[:, t - 1, :], start=True, stop=False)
                    last = pe.matmul(o, before[:, :], A_bf[:, t, :], start=(t % QT == 0), stop=True)
                last.then_inc(pos_ps, 1)
                pe.wait_ge(disp_ready, it + 1)
                for b in range(GROUP):
                    for tq in range(QT):
                        t = b * QT + tq
                        last = pe.matmul(ps[:, 3 + b, 0:SLOTS], X[:, t, :], disp[:, t, :], start=(tq == 0),
                                         stop=(tq == QT - 1))
                    last.then_inc(xb_ps, 1)
                pe.wait_ge(comb_ready, it + 1)
                if more:
                    pe.wait_ge(kvr_ready, (it + 1) * 3 + 3)
                for t in range(TT):
                    for k in range(SB):
                        n = min(P, SLOTS - k * P)
                        last = pe.transpose(ps[0:n, 5 + k, t * P:(t + 1) * P], comb[:, t, k * P:k * P + n], ident[:, :])
                last.then_inc(combT_ps, 1)
                pe.wait_ge(xb_ready, it * GROUP + GROUP)
                W = GROUP * CAP

                def up(e):
                    for h in range(HT):
                        last = pe.matmul(ps[:, e % 2, h * W:(h + 1) * W], w1b[:, e, h * P:(h + 1) * P],
                                         xb[:, :, e * CAP:(e + 1) * CAP], start=True, stop=True)
                    last.then_inc(hid_ps, 1)

                def down(e):
                    pe.wait_ge(hid_ready, it * E + e + 1)
                    if e >= 2:
                        pe.wait_ge(y_ready, it * E + e - 1)
                    for h in range(HT):
                        last = pe.matmul(ps[:, 2 + e % 2, 0:W], w2b[:, e, h, :], hid[:, e % 2, h, :],
                                         start=(h == 0), stop=(h == HT - 1))
                    last.then_inc(y_ps, 1)

                up(0)
                for e in range(E):
                    if e + 1 < E:
                        up(e + 1)
                    down(e)
                    if more and e == 1:
                        pe.wait_ge(combT_ready, it + 1)
                        rec_attend(it + 1)
                    if more and e == E - 3:
                        rec_turn(it + 1, 2, 5)
                if more:
                    turn_ctx(it + 1, it)
                    rec_widen(it + 1)
                pe.wait_ge(y_ready, it * E + E)
                for b in range(GROUP):
                    for k in range(SB):
                        n = min(P, SLOTS - k * P)
                        last = pe.transpose(ps[0:n, b, k * D:(k + 1) * D], yT[:, b, k * P:k * P + n], ident[:, :])
                    last.then_inc(ysl_ps, 1)
                if more:
                    rec_narrow(it + 1)
                pe.wait_ge(combT_ready, it + 1)
                for t in range(TT):
                    if t % QT == 0:
                        pe.wait_ge(ysl_ready, it * GROUP + t // QT + 1)
                    for k in range(SB):
                        n = min(P, SLOTS - k * P)
                        last = pe.matmul(ps[:, 4, t * D:(t + 1) * D], combT[0:n, k, t * P:(t + 1) * P],
                                         ySl[0:n, t // QT, k, :], start=(k == 0), stop=(k == SB - 1))
                last.then_inc(comb_ps, 1)

            def group(it, more=True):
                memory(it)
                mixture_top1(it)
                sparse_attention(it)
                cross_attention(it, more)
                mixture_top2(it, more)

            first_recurrent(0)
            with pe.Fori(0, ITERS - 1) as it:
                group(it)
            group(ITERS - 1, more=False)

        @block.scalar
        def _(act):
            def copy(dst, src):
                return act.activation(dst, src, ACT.Copy)

            def set_up(n):
                act.wait_ge(wT_ps, n + 1)
                b = n % SETUP_BANKS
                if n >= N_TURNS:
                    dst = qk_fold[:, :] if n == N_TURNS else broadcast_rows[n - N_TURNS - 1][1]
                    src = ps[:, b, 0:dst.shape[1]]
                else:
                    srcs, dst = weight_turns[n]
                    src = tiles(b) if len(srcs) == 4 else ps[:, b, 0:srcs[0].shape[0]]
                copy(dst, src).then_inc(wT_sb, 1)

            set_up(0)
            act.wait_ge(wT_sb, 1)
            act.activation(decay_e[:, :], col(R_DECAY), ACT.Exp).then_inc(cols_ready, 1)
            act.wait_ge(cols_ready, 5)

            def x_turned(it, n):
                act.wait_ge(xT_ps, it * 5 + n)
                copy(XT[:, :], bank(0)).then_inc(xT_ready, 1)

            def ctx_turned(n):
                for g in range(2):
                    act.wait_ge(ctxT_ps, n * 2 + g + 1)
                    copy(ctxT[:, g * 512:(g + 1) * 512], bank(2 + g)).then_inc(ctxT_ready, 1)

            def rec_turned(n, k, b, scale, shift):
                act.wait_ge(hT_ps, n * 2 + k)
                act.activation(hT[:, :, 1:SEQ + 1], seqs(b), ACT.Identity, bias=col(shift), scale=col(scale))\
                    .then_inc(hT_ready, 1)

            def rec_projected(n, i):
                act.wait_ge(kvr_ps, n * 3 + i + 1)
                copy((kS, vS)[i][:, :, :], seqs((4, 7)[i])).then_inc(kvr_ready, 1)

            def rec_exp(n, i):
                act.wait_ge(wkv_arg, n * 4 + i + 1)
                act.activation(ex[i][:, :, :], ex[i][:, :, :], ACT.Exp).then_inc(wkv_exp, 1)

            def rec_receptance(n):
                act.wait_ge(kvr_ps, n * 3 + 3)
                act.activation(rS[:, :, :], seqs(5), ACT.Sigmoid).then_inc(kvr_ready, 1)

            def rec_rectify(n):
                for h, b in enumerate((6, 7, 5, 6)):
                    act.wait_ge(kf_ps, n * HT + h + 1)
                    act.activation(big[:, h, :], bank(b), ACT.Relu).then_inc(kf_relu, 1)
                act.wait_ge(rf_ps, n + 1)
                act.activation(rf[:, :, :], tiles(7), ACT.Sigmoid).then_inc(rf_ready, 1)

            def first_recurrent(n):
                rec_turned(n, 1, 5, R_LNG, R_LNB)
                rec_projected(n, 0)
                rec_projected(n, 1)
                for i in range(4):
                    rec_exp(n, i)
                rec_receptance(n)
                for i in range(1, N_SETUP):
                    set_up(i)
                ctx_turned(n)
                rec_turned(n, 2, 5, R_FLNG, R_FLNB)
                rec_rectify(n)

            def memory(it):
                for seq in range(GROUP):
                    act.wait_ge(layer_done, it * (LAYERS * GROUP) + seq + 1)
                    for t in range(seq * QT, (seq + 1) * QT):
                        last = act.activation(alpha[:, t, :], X[:, t, :], ACT.Square, scale=float(D) ** -0.5,
                                              accum_out=ssq[:, t:t + 1])
                    last.then_inc(ssq_ready, 1)
                x_turned(it, 1)
                act.wait_ge(nT_ps, it + 1)
                act.activation(nT[:, :], bank(1), ACT.Identity, scale=col(R_NORMW)).then_inc(nT_ready, 1)
                act.wait_ge(qp_ps, it + 1)
                act.activation(qpT[:, :], bank(3), ACT.Copy, scale=float(D) ** -0.5).then_inc(qp_ready, 1)

                def exps(t):
                    n = CTX + (t % QT + 1) * P
                    act.wait_ge(lg_max, it * TT + t + 1)
                    lo = 2 * (t % 2) * 512
                    act.activation(prob[:, t % 2, 0:n], psf[:, lo:lo + n], ACT.Exp, bias=nmax[:, t:t + 1],
                                   accum_out=rsum[:, 0, t:t + 1]).then_inc(lg_exp, 1)

                exps(0)
                exps(1)
                for t in range(TT):
                    n = CTX + (t % QT + 1) * P
                    act.wait_ge(pT_ps, it * TT + t + 1)
                    copy(probT[:, 0, 0:n], psf[:, 4 * 512:4 * 512 + n]).then_inc(pT_ready, 1)
                    if t + 2 < TT:
                        exps(t + 2)
                act.wait_ge(gate_ps, it + 1)
                act.activation(alpha[:, :, :], tiles(7), ACT.Sigmoid).then_inc(alpha_ready, 1)

            def mixture_top1(it):
                x_turned(it, 2)
                act.wait_ge(ohT_ps, it + 1)
                copy(ohT[:, :], ps[0:PARTS * E, 2, :]).then_inc(ohT_ready, 1)
                for h, b in enumerate((5, 6, 7, 0)):
                    act.wait_ge(pre_ps, it * HT + h + 1)
                    act.activation(big[:, h, :], bank(b), ACT.Gelu).then_inc(inter_ready, 1)

            def sparse_attention(it):
                x_turned(it, 3)
                act.wait_ge(qkv_ps, it * 4 + 1)
                act.activation(qT[:, :], bank(1), ACT.Identity, bias=battq_scaled[:, 0:1], scale=float(HD) ** -0.5)\
                    .then_inc(qk_ready, 1)
                act.wait_ge(qkv_ps, it * 4 + 2)
                act.activation(kT[:, :], bank(2), ACT.Identity, bias=col(R_BATT + 1)).then_inc(qk_ready, 1)

                def exps(hh, u):
                    act.wait_ge(s_max, it * NH + 2 * hh + u + 1)
                    for t in range(TT):
                        c = (t % QT) * KW
                        last = act.activation(SP_[:, u, t, :], ps[:, 2 * u + t // QT, c:c + KW], ACT.Exp,
                                              bias=snm[:, u, t:t + 1], accum_out=srs[:, u, t:t + 1])
                    last.then_inc(s_exp, 1)

                def turned(hh, u):
                    act.wait_ge(sT_ps, it * NH + 2 * hh + u + 1)
                    copy(spT[:, u, :], bank(4 + u)).then_inc(sT_ready, 1)

                exps(0, 0)
                exps(0, 1)
                with act.Fori(0, NH // 2 - 1) as hh:
                    turned(hh, 0)
                    turned(hh, 1)
                    exps(hh + 1, 0)
                    exps(hh + 1, 1)
                turned(NH // 2 - 1, 0)
                turned(NH // 2 - 1, 1)
                act.wait_ge(gT_ps, it + 1)
                copy(GT[:, :, :], ps[:, 4, 0:GROUP * P].rearrange("p (b q) -> p b q", b=GROUP)).then_inc(gT_ready, 1)
                act.wait_ge(sinv_ps, it + 1)
                copy(qT[:, :], bank(5)).then_inc(sinv_ready, 1)

            def cross_attention(it, more_groups=True):
                def queries(j, u, b):
                    act.wait_ge(q_ps, it * PAIRS + j + 1)
                    act.wait_ge(cols_ready, 5)
                    act.activation(QTs[:, u, :], bank(b), ACT.Identity, bias=bq_scaled[:, bass.ds(j, 1)],
                                   scale=float(DK) ** -0.5).then_inc(q_ready, 1)

                def keys(j, u, b, seq):
                    if seq == 0 or isinstance(j, int):
                        act.wait_ge(k_ps, it * (2 * PAIRS) + 2 * j + seq + 1)
                    act.wait_ge(cols_ready, 5)
                    act.activation(KTs[:, u, seq * CTX:(seq + 1) * CTX], bank(b), ACT.Identity,
                                   bias=cols[:, bass.ds(R_BK + j, 1)]).then_inc(k_ready, 1)

                def exps(j, u, s):
                    act.wait_ge(c_max, it * (NS * PAIRS) + j * NS + s + 1)
                    act.activation(cprob[:, s % 2, :], bank(s % 2), ACT.Exp, bias=nmax[:, s:s + 1],
                                   accum_out=rsum[:, u, s:s + 1]).then_inc(c_exp, 1)

                def spread(j):
                    act.wait_ge(inv_ps, it * PAIRS + j + 1)
                    copy(Rs[:, :], bank(6)).then_inc(inv_ready, 1)

                def pair(j, u, first=False, more=True):
                    for s in range(NS):
                        if s + 1 < NS:
                            exps(j, u, s + 1)
                        elif more:
                            exps(j + 1, 1 - u, 0)
                        if s % 2:
                            act.wait_ge(cT_ps, it * (NS * PAIRS) + j * NS + s + 1)
                            copy(cprobT[:, s % 4, :], bank(3)).then_inc(cT_odd, 1)
                        if s == 1 and more:
                            queries(j + 1, 1 - u, 7)
                        if s == 2 and not first:
                            spread(j - 1)
                        if s == 3 and more:
                            keys(j + 1, 1 - u, 7, 0)
                        if s == 5 and more:
                            keys(j + 1, 1 - u, 7, 1)
                        if more_groups and not more:
                            if s == 3:
                                rec_turned(it + 1, 1, 7, R_LNG, R_LNB)
                            if s == 7:
                                rec_projected(it + 1, 0)

                keys(0, 0, 6, 0)
                keys(0, 0, 3, 1)
                x_turned(it, 4)
                queries(0, 0, 7)
                exps(0, 0, 0)
                pair(0, 0, first=True)
                with act.Fori(0, PAIRS // 2 - 1) as jj:
                    pair(2 * jj + 1, 1)
                    pair(2 * jj + 2, 0)
                pair(PAIRS - 1, 1, more=False)
                if more_groups:
                    rec_projected(it + 1, 1)
                spread(PAIRS - 1)

            def mixture_top2(it, more=True):
                x_turned(it, 5)
                if more:
                    for i in range(4):
                        rec_exp(it + 1, i)
                act.wait_ge(e1_arg, it + 1)
                act.activation(ex1[:, :, :], ex1[:, :, :], ACT.Exp).then_inc(e1_exp, 1)
                if more:
                    rec_receptance(it + 1)
                for b in range(GROUP):
                    act.wait_ge(xb_ps, it * GROUP + b + 1)
                    copy(xb[:, b, :], ps[:, 3 + b, 0:SLOTS]).then_inc(xb_ready, 1)
                act.wait_ge(combT_ps, it + 1)
                for k in range(SB):
                    n = min(P, SLOTS - k * P)
                    last = copy(combT[0:n, k, :], ps[0:n, 5 + k, :])
                last.then_inc(combT_ready, 1)
                W = GROUP * CAP

                def relu(e):
                    act.wait_ge(hid_ps, it * E + e + 1)
                    for h in range(HT):
                        last = act.activation(hid[:, e % 2, h, :], ps[:, e % 2, h * W:(h + 1) * W], ACT.Relu,
                                              bias=col(R_B1 + e * HT + h))
                    last.then_inc(hid_ready, 1)

                relu(0)
                for e in range(E):
                    if e + 1 < E:
                        relu(e + 1)
                    act.wait_ge(y_ps, it * E + e + 1)
                    act.activation(yT[:, :, e * CAP:(e + 1) * CAP],
                                   ps[:, 2 + e % 2, 0:W].rearrange("p (b c) -> p b c", b=GROUP),
                                   ACT.Identity, bias=col(R_B2 + e)).then_inc(y_ready, 1)
                    if more and e == E - 3:
                        rec_turned(it + 1, 2, 5, R_FLNG, R_FLNB)
                if more:
                    ctx_turned(it + 1)
                    rec_rectify(it + 1)
                for b in range(GROUP):
                    act.wait_ge(ysl_ps, it * GROUP + b + 1)
                    for k in range(SB):
                        n = min(P, SLOTS - k * P)
                        last = copy(ySl[0:n, b, k, :], ps[0:n, b, k * D:(k + 1) * D])
                    last.then_inc(ysl_ready, 1)

            def group(it, more=True):
                memory(it)
                mixture_top1(it)
                sparse_attention(it)
                cross_attention(it, more)
                mixture_top2(it, more)

            first_recurrent(0)
            with act.Fori(0, ITERS - 1) as it:
                group(it)
            group(ITERS - 1, more=False)

        @block.gpsimd
        def _(pool):
            pool.memset(ident[:, :], 0.0)
            pool.memset(causal_f[:, :], 0.0)
            pool.memset(sparse_f[:, :, :], 0.0)
            pool.memset(before_f[:, :], 1.0)
            pool.memset(ones_bf[:, :], 1.0)
            pool.memset(ones[:, :], 1.0)
            pool.memset(pick_f[:, :, :], 0.0)
            pool.memset(head_mask[:, :], 1.0)
            pool.memset(zeros_bf[:, :], 0.0)
            pool.memset(pair_mask[:, :, :], 0.0)
            pool.memset(neg_half[:, :], -0.5)
            pool.memset(eps_ln[:, :], 1e-5)
            pool.memset(eps_rms[:, :], 1e-6)
            pool.memset(eps_post[:, :], 1e-12)
            pool.iota(iota_ei[:, :], pattern=[[0, PARTS], [1, E]], base=0, channel_multiplier=0)
            pool.iota(iota_ci[:, :], pattern=[[1, CAP]], base=1, channel_multiplier=0)
            pool.drain()

            def select(m, op, fill, base, pattern, cm):
                pool.affine_select(out=m, in_=m, compare_op=op, fill=fill, base=base, pattern=pattern,
                                   channel_multiplier=cm)

            select(ident[:, :], ALU.not_equal, 1.0, 0, [[-1, P]], 1)
            select(causal_f[:, :], ALU.is_ge, MASKED, 0, [[-1, P]], 1)
            for tq in range(QT):
                select(sparse_f[:, tq, :], ALU.is_ge, MASKED, tq * CB, [[-1, KW]], 1)
            select(before_f[:, :], ALU.is_ge, 0.0, -1, [[1, P]], -1)
            select(pick_f[:, :, :], ALU.not_equal, 1.0, 0, [[-1, E], [0, P]], 1)
            select(head_mask[:, :], ALU.is_ge, 0.0, 0, [[-HD, NH]], 1)
            for half in range(2):
                select(pair_mask[:, :, half * (NH // 2):(half + 1) * (NH // 2)], ALU.not_equal, 1.0, 0,
                       [[1, NH // 2], [-1, NH // 2]], 0)
            pool.drain()
            select(head_mask[:, :], ALU.is_ge, 0.0, HD - 1, [[HD, NH]], -1)
            for dst, src in ((ident_bf, ident), (causal, causal_f), (before, before_f), (iota_e, iota_ei),
                             (iota_c, iota_ci)):
                pool.tensor_copy(dst[:, :], src[:, :])
            pool.tensor_copy(pick[:, :, :], pick_f[:, :, :])
            pool.tensor_copy(sparse[:, :], sparse_f[:, :, :].rearrange("p a b -> p (a b)"))
            pool.drain().then_inc(consts_ready, 1)

            def inverse_root(values, eps, with_eps, result, seq):
                r = slice(seq * QT, (seq + 1) * QT)
                pool.tensor_tensor(with_eps[:, r], values[:, r], eps[:, r], ALU.add)
                pool.drain()
                return pool.tensor_tensor(result[:, r], with_eps[:, r], neg_half[:, r], ALU.pow)

            def rstd_of(it, n, eps):
                for seq in range(GROUP):
                    pool.wait_ge(var_ready, it * (LNS * GROUP) + (n - 1) * GROUP + seq + 1)
                    inverse_root(variance, eps, vare, rstd, seq).then_inc(rstd_ready, 1)

            def rec_rstd(n, k):
                for seq in range(GROUP):
                    pool.wait_ge(rvar_ready, n * (RNS * GROUP) + (k - 1) * GROUP + seq + 1)
                    inverse_root(variance, eps_ln, vare, rstd, seq).then_inc(rrstd_ready, 1)

            def rec_numerator(n):
                pool.wait_ge(wkv_exp, n * 4 + 2)
                pool.tensor_tensor(b2v[:, :, :], ex[1][:, :, :], vS[:, :, :], ALU.mult).then_inc(b2v_ready, 1)
                pool.wait_ge(wkv_exp, n * 4 + 4)
                pool.tensor_tensor(bv_[:, :, :], ex[3][:, :, :], vS[:, :, :], ALU.mult)
                pool.wait_ge(p_ready, n + 1)
                pool.tensor_tensor(t_num[:, :, :], ex[2][:, :, :], p_num[:, :, 0:SEQ], ALU.mult)
                pool.drain()
                pool.tensor_tensor(t_num[:, :, :], t_num[:, :, :], bv_[:, :, :], ALU.add)
                pool.drain()
                pool.wait_ge(kvr_ready, n * 3 + 3)
                pool.tensor_tensor(t_num[:, :, :], t_num[:, :, :], rS[:, :, :], ALU.mult).then_inc(tnum_ready, 1)

            variance = mv[:, :, 1:2].rearrange("p t o -> p (t o)")

            def stage(it, j):
                pool.tensor_copy(wq_s[:, :], xwT[:, 0, bass.ds(j, 1), :])
                pool.tensor_copy(wk_s[:, :], xwT[:, 1, bass.ds(j, 1), :])
                pool.drain().then_inc(staged, 1)

            def group(it, more=True):
                for seq in range(GROUP):
                    pool.wait_ge(ssq_ready, it * GROUP + seq + 1)
                    inverse_root(ssq, eps_rms, ssq_eps, rms_inv, seq).then_inc(rms_ready, 1)
                pool.wait_ge(nhat_ready, it * GROUP + GROUP)
                for t in range(TT):
                    last = pool.tensor_tensor(nTok[:, t, :], NHAT[:, t, :], normw_bc[:, :], ALU.mult)
                last.then_inc(ntok_ready, 1)
                rstd_of(it, 1, eps_ln)
                rstd_of(it, 2, eps_post)
                rstd_of(it, 3, eps_ln)
                stage(it, 0)

                def mask_values(hh):
                    by_head = "p t (h d) -> p t h d"
                    pool.tensor_tensor(Vm[:, :, :].rearrange(by_head, h=NH), V[:, :, :].rearrange(by_head, h=NH),
                                       pair_mask[:, bass.ds(hh, 1), :].unsqueeze(3).to_broadcast([P, TT, NH, HD]),
                                       ALU.mult).then_inc(vm_ready, 1)

                pool.wait_ge(v_ready, it + 1)
                mask_values(0)
                with pool.Fori(0, NH // 2 - 1) as hh:
                    pool.wait_ge(so_ps, it * (NH // 2) + hh + 1)
                    mask_values(hh + 1)
                rstd_of(it, 4, eps_ln)
                with pool.Fori(0, PAIRS - 1) as j:
                    pool.wait_ge(q_ps, it * PAIRS + j + 1)
                    pool.wait_ge(k_ps, it * (2 * PAIRS) + 2 * j + 2)
                    stage(it, j + 1)
                if more:
                    rec_rstd(it + 1, 1)
                rstd_of(it, 5, eps_ln)
                if more:
                    rec_numerator(it + 1)
                    rec_rstd(it + 1, 2)
                if more:
                    rec_rstd(it + 1, 3)
                rstd_of(it, 6, eps_ln)

            rec_rstd(0, 1)
            rec_numerator(0)
            rec_rstd(0, 2)
            pool.wait_ge(b1_loaded, 16)
            for part in (b1_parts[0:E, :], b1_mid[:, :]):
                pool.tensor_copy(part, b1_rest)
                pool.drain()
                pool.tensor_copy(b1_part, part)
                pool.drain()
                pool.tensor_tensor(b1_rest, b1_rest, b1_part, ALU.subtract)
                pool.drain()
            pool.tensor_copy(b1_low[:, :], b1_rest).then_inc(b1_split, 1)
            pool.wait_ge(wT_sb, N_SETUP)
            rec_rstd(0, 3)
            with pool.Fori(0, ITERS - 1) as it:
                group(it)
            group(ITERS - 1, more=False)

        @block.vector
        def _(dve):
            def tiles_of(seq):
                return range(seq * QT, (seq + 1) * QT)

            def half_of(view, seq):
                return view[:, seq * QT:(seq + 1) * QT, :]

            def moments(src, seq):
                for t in tiles_of(seq):
                    dve.bn_stats(bn[:, t, :], src[:, t, :])
                dve.drain()
                for t in tiles_of(seq):
                    last = dve.bn_aggr(mv[:, t, :], bn[:, t, :])
                return last

            def normalised(src, dst, seq):
                for t in tiles_of(seq):
                    last = dve.tensor_scalar(dst[:, t, :], src[:, t, :], mv[:, t, 0:1], rstd[:, t:t + 1],
                                             ALU.subtract, ALU.mult)
                return last

            def layer_norm(it, n, prepare, src, dst, done):
                for seq in range(GROUP):
                    prepare(seq)
                    moments(src, seq).then_inc(var_ready, 1)
                for seq in range(GROUP):
                    dve.wait_ge(rstd_ready, it * (LNS * GROUP) + (n - 1) * GROUP + seq + 1)
                    normalised(src, dst, seq).then_inc(done, 1)

            def rec_normalised(n, k, src, dst, done):
                for seq in range(GROUP):
                    dve.wait_ge(rrstd_ready, n * (RNS * GROUP) + (k - 1) * GROUP + seq + 1)
                    normalised(src, dst, seq).then_inc(done, 1)

            def token_change():
                dve.tensor_tensor(dT[:, :, :], hT[:, :, 1:SEQ + 1], hT[:, :, 0:SEQ], ALU.subtract)
                dve.drain()

            def token_shift(z, r):
                for b in range(GROUP):
                    last = dve.scalar_tensor_tensor(out=z[:, b, :], in0=dT[:, b, :], scalar=col(r),
                                                    in1=hT[:, b, 0:SEQ], op0=ALU.mult, op1=ALU.add)
                last.then_inc(mix_ready, 1)

            dve.memset(hT[:, :, 0:1], 0.0).then_inc(out_stored, 1)
            dve.memset(o_max[:, :, 0:1], -1e38)
            dve.memset(p_num[:, :, 0:1], 0.0)
            dve.memset(q_den[:, :, 0:1], 0.0)
            dve.memset(w_bc[:, :], 0.0)
            dve.wait_ge(cols_ready, 1)
            dve.tensor_scalar(decay_w[:, :], decay_e[:, :], -1.0, None, ALU.mult).then_inc(cols_ready, 1)
            dve.tensor_scalar(bq_scaled[:, :], cols[:, R_BQ:R_BQ + PAIRS], float(DK) ** -0.5, None, ALU.mult)\
                .then_inc(cols_ready, 1)
            dve.tensor_scalar(battq_scaled[:, :], col(R_BATT), float(HD) ** -0.5, None, ALU.mult)\
                .then_inc(cols_ready, 1)
            dve.drain()
            dve.tensor_scalar(w_bc[:, :], w_bc[:, :], decay_w[:, 0:1], None, ALU.add).then_inc(cols_ready, 1)
            dve.drain()

            def rec_first_moments(n):
                dve.wait_ge(x_loaded, n * 16 + 16)
                for seq in range(GROUP):
                    moments(X0, seq).then_inc(rvar_ready, 1)

            def rec_first_normalised(n):
                rec_normalised(n, 1, X0, NHAT, xhat_ready)

            def rec_key_mix(n):
                dve.wait_ge(hT_ready, n * 2 + 1)
                token_change()
                token_shift(zk, R_MK)

            def rec_value_mix():
                token_shift(zv, R_MV)
                token_shift(zr, R_MR)

            def rec_exponents(n):
                dve.wait_ge(kvr_ready, n * 3 + 1)
                for b in range(GROUP):
                    dve.tensor_tensor_scan(o_max[:, b, 1:SEQ + 1], w_bc[:, :], kS[:, b, :], -1e38, ALU.add, ALU.max)
                dve.drain()
                for b in range(GROUP):
                    last = dve.scalar_tensor_tensor(out=ex[0][:, b, :], in0=o_max[:, b, 0:SEQ], scalar=decay_w[:, 0:1],
                                                    in1=o_max[:, b, 1:SEQ + 1], op0=ALU.add, op1=ALU.subtract)
                last.then_inc(wkv_arg, 1)
                dve.tensor_tensor(ex[1][:, :, :], kS[:, :, :], o_max[:, :, 1:SEQ + 1], ALU.subtract)\
                    .then_inc(wkv_arg, 1)
                for b in range(GROUP):
                    dve.scalar_tensor_tensor(out=o_new[:, b, :], in0=kS[:, b, :], scalar=col(R_FIRST),
                                             in1=o_max[:, b, 0:SEQ], op0=ALU.add, op1=ALU.max)
                dve.drain()
                dve.tensor_tensor(ex[2][:, :, :], o_max[:, :, 0:SEQ], o_new[:, :, :], ALU.subtract)\
                    .then_inc(wkv_arg, 1)
                dve.scalar_tensor_tensor(out=ex[3][:, :, :], in0=kS[:, :, :], scalar=col(R_FIRST), in1=o_new[:, :, :],
                                         op0=ALU.add, op1=ALU.subtract).then_inc(wkv_arg, 1)

            def rec_wkv(n):
                dve.wait_ge(wkv_exp, n * 4 + 2)
                for b in range(GROUP):
                    dve.tensor_tensor_scan(q_den[:, b, 1:SEQ + 1], ex[0][:, b, :], ex[1][:, b, :], 0.0, ALU.mult, ALU.add)
                dve.wait_ge(b2v_ready, n + 1)
                for b in range(GROUP):
                    last = dve.tensor_tensor_scan(p_num[:, b, 1:SEQ + 1], ex[0][:, b, :], b2v[:, b, :], 0.0,
                                                  ALU.mult, ALU.add)
                last.then_inc(p_ready, 1)
                dve.drain()
                dve.wait_ge(wkv_exp, n * 4 + 4)
                dve.tensor_tensor(t_den[:, :, :], ex[2][:, :, :], q_den[:, :, 0:SEQ], ALU.mult)
                dve.drain()
                dve.tensor_tensor(t_den[:, :, :], t_den[:, :, :], ex[3][:, :, :], ALU.add)
                dve.drain()
                dve.reciprocal(rec[:, :, :], t_den[:, :, :])
                dve.drain()
                dve.wait_ge(tnum_ready, n + 1)
                dve.tensor_tensor(rec[:, :, :], rec[:, :, :], t_num[:, :, :], ALU.mult).then_inc(wkv_ready, 1)

            def rec_second_norm(n):
                dve.wait_ge(att_ps, n + 1)
                for seq in range(GROUP):
                    dve.tensor_tensor(half_of(X1, seq), half_of(X0, seq), half_of(tiles(6), seq), ALU.add)
                    dve.drain()
                    moments(X1, seq).then_inc(rvar_ready, 1)
                rec_normalised(n, 2, X1, NHAT, xhat_ready)

            def rec_feed_mix(n):
                dve.wait_ge(hT_ready, n * 2 + 2)
                token_change()
                token_shift(zk, R_FMK)
                token_shift(zr, R_FMR)

            def rec_feed(n, last_use_of_x=None):
                for h in range(HT):
                    dve.wait_ge(kf_relu, n * HT + h + 1)
                    dve.tensor_tensor(big2[:, h, :], big[:, h, :], big[:, h, :], ALU.mult).then_inc(kf_ready, 1)
                dve.tensor_tensor(X1[:, :, :], X1[:, :, :], X0[:, :, :], ALU.add)
                dve.wait_ge(rf_ready, n + 1)
                dve.wait_ge(ffn_ps, n + 1)
                for seq in range(GROUP):
                    h = half_of(rf, seq)
                    dve.tensor_tensor(h, h, half_of(tiles(5), seq), ALU.mult)
                    dve.drain()
                    dve.tensor_tensor(h, h, half_of(X1, seq), ALU.add)
                    dve.drain()
                    moments(rf, seq).then_inc(rvar_ready, 1)
                if last_use_of_x is not None:
                    last_use_of_x()
                rec_normalised(n, 3, rf, X, layer_done)

            def recurrent(n):
                rec_first_moments(n)
                rec_first_normalised(n)
                rec_key_mix(n)
                rec_value_mix()
                rec_exponents(n)
                rec_wkv(n)
                rec_second_norm(n)
                rec_feed_mix(n)
                rec_feed(n)

            def memory(it):
                for seq in range(GROUP):
                    dve.wait_ge(rms_ready, it * GROUP + seq + 1)
                    for t in tiles_of(seq):
                        last = dve.tensor_scalar(NHAT[:, t, :], X[:, t, :], rms_inv[:, t:t + 1], None, ALU.mult)
                    last.then_inc(nhat_ready, 1)
                for t in range(TT):
                    n, lo = CTX + (t % QT + 1) * P, 2 * (t % 2) * 512
                    dve.wait_ge(lg_ps, it * TT + t + 1)
                    dve.tensor_reduce(nmax[:, t:t + 1], psf[:, lo:lo + n], AX.X, ALU.max, negate=True)\
                        .then_inc(lg_max, 1)
                dve.wait_ge(lg_exp, it * TT + TT)
                dve.reciprocal(rinv[:, 0:TT], rsum[:, 0, 0:TT])
                dve.drain()
                dve.wait_ge(av_ps, it + 1)
                dve.wait_ge(out_stored, it * 16 + 1)
                for t in range(TT):
                    dve.scalar_tensor_tensor(out=Y[:, t, :], in0=ps[:, 6, t * D:(t + 1) * D], scalar=rinv[:, t:t + 1],
                                             in1=X[:, t, :], op0=ALU.mult, op1=ALU.subtract)
                dve.drain()
                dve.wait_ge(alpha_ready, it + 1)

                def gated(seq):
                    y = half_of(Y, seq)
                    dve.tensor_tensor(y, y, half_of(alpha, seq), ALU.mult)
                    dve.drain()
                    dve.scalar_tensor_tensor(out=y, in0=half_of(X, seq), scalar=2.0, in1=y, op0=ALU.mult, op1=ALU.add)
                    dve.drain()

                layer_norm(it, 1, gated, Y, X, layer_done)

            def mixture_top1(it):
                dve.wait_ge(route_ps, it + 1)
                dve.tensor_copy(lg[:, :, :], ps[:, 1, 0:TT * E].rearrange("p (t e) -> p t e", t=TT))
                dve.drain()
                for t in range(TT):
                    dve.max(top[:, t, :], lg[:, t, :])
                dve.drain()
                for t in range(TT):
                    dve.max_index(topi[:, t, :], top[:, t, :], lg[:, t, :])
                dve.drain()
                dve.tensor_copy(topf[:, :, 0:1], topi[:, :, 0:1])
                dve.drain()
                for t in range(TT):
                    last = dve.tensor_scalar(onehot[:, t, :], iota_e[:, :], topf[:, t, 0:1], None, ALU.is_equal)
                last.then_inc(onehot_ready, 1)
                dve.wait_ge(xT_ready, it * 5 + 2)
                for e in range(E):
                    dve.wait_ge(pick_ps, it * E + e + 1)
                    dve.tensor_tensor(XE[:, e % 2, :], XT[:, :], bank(3 + e % 2), ALU.mult).then_inc(xe_ready, 1)
                for t in range(TT):
                    dve.tensor_tensor(NHAT[:, t, :], X[:, t, :], bo_bc[:, :], ALU.add)
                    dve.tensor_tensor(X1[:, t, :], X[:, t, :], beta_bc[:, :], ALU.add)
                dve.drain()
                dve.wait_ge(moe_ps, it + 1)
                for seq in range(GROUP):
                    dve.tensor_tensor(half_of(Y, seq), half_of(NHAT, seq), half_of(tiles(1), seq), ALU.add)
                    dve.drain()
                    moments(Y, seq).then_inc(var_ready, 1)
                dve.drain()
                for t in range(TT):
                    dve.scalar_tensor_tensor(out=Y[:, t, :], in0=Y[:, t, :], scalar=mv[:, t, 0:1], in1=gamma_bc[:, :],
                                             op0=ALU.subtract, op1=ALU.mult)
                dve.drain()

                def post_normalised(seq):
                    dve.wait_ge(rstd_ready, it * (LNS * GROUP) + GROUP + seq + 1)
                    for t in tiles_of(seq):
                        dve.scalar_tensor_tensor(out=Y[:, t, :], in0=Y[:, t, :], scalar=rstd[:, t:t + 1],
                                                 in1=X1[:, t, :], op0=ALU.mult, op1=ALU.add)
                    dve.drain()

                layer_norm(it, 3, post_normalised, Y, X, layer_done)

            def sparse_attention(it):
                def mask_head(hh, u):
                    dve.tensor_scalar(qm[:, u, :], qT[:, :], head_mask[:, bass.ds(hh + u * (NH // 2), 1)], None, ALU.mult)\
                        .then_inc(qm_ready, 1)

                def row_max(hh, u):
                    dve.wait_ge(s_ps, it * NH + 2 * hh + u + 1)
                    dve.tensor_reduce(snm[:, u, :].rearrange("p (b t) -> p b t", b=GROUP),
                                      ps[:, 2 * u:2 * u + 2, 0:QT * KW].rearrange("p b (t k) -> p b t k", t=QT),
                                      AX.X, ALU.max, negate=True).then_inc(s_max, 1)

                def turned(hh, u):
                    dve.wait_ge(sT_ps, it * NH + 2 * hh + u + 1)
                    dve.reciprocal(sri[:, u, :], srs[:, u, :])
                    dve.tensor_copy(G[:, :, bass.ds(hh + u * (NH // 2), 1), :],
                                    SP_[:, u, :, 0:CB].rearrange("p (b t) c -> p b t c", t=QT)[:, :, 1:2, :])
                    dve.drain()
                    dve.tensor_copy(O[:, :, bass.ds((hh + u * (NH // 2)) * HD, HD)],
                                    sri[:, u, :].unsqueeze(2).to_broadcast([P, TT, HD]))

                def two_heads(hh, more, masks):
                    turned(hh, 0)
                    if more:
                        row_max(hh + 1, 0)
                    if masks:
                        mask_head(hh + 2, 0)
                    turned(hh, 1)
                    if more:
                        row_max(hh + 1, 1)
                    if masks:
                        mask_head(hh + 2, 1)

                dve.wait_ge(xT_ready, it * 5 + 3)
                for b in range(GROUP):
                    last = dve.tensor_copy(XTg[:, b, :, :], XT[:, b * SEQ + P - CB:b * SEQ + P].unsqueeze(1)
                                           .to_broadcast([P, NH, CB]))
                last.then_inc(xg_ready, 1)
                dve.wait_ge(qk_ready, it * 2 + 1)
                mask_head(0, 0)
                mask_head(0, 1)
                dve.wait_ge(qkv_ps, it * 4 + 3)
                dve.tensor_tensor(V[:, :, :], tiles(3), bv_bc[:, :].unsqueeze(1).to_broadcast([P, TT, D]), ALU.add)\
                    .then_inc(v_ready, 1)
                dve.wait_ge(qkv_ps, it * 4 + 4)
                dve.tensor_tensor(Vgb[:, :, :, :].rearrange("p b h d -> p b (h d)"),
                                  ps[:, 4, 0:GROUP * D].rearrange("p (b d) -> p b d", b=GROUP),
                                  bv_bc[:, :].unsqueeze(1).to_broadcast([P, GROUP, D]), ALU.add)
                for u in range(2):
                    row_max(0, u)
                    mask_head(1, u)
                dve.drain()
                dve.tensor_tensor(Vg[:, :, :].rearrange("p b (h d) -> p b h d", h=NH), Vgb[:, :, :, :],
                                  head_mask[:, :].unsqueeze(2).unsqueeze(1).to_broadcast([P, GROUP, NH, HD]), ALU.mult)
                with dve.Fori(0, NH // 2 - 2) as hh:
                    two_heads(hh, True, True)
                two_heads(NH // 2 - 2, True, False)
                two_heads(NH // 2 - 1, False, False)
                dve.drain().then_inc(g_ready, 1)
                dve.tensor_tensor(NHAT[:, :, :], X[:, :, :], bproj_bc[:, :].unsqueeze(1).to_broadcast([P, TT, D]), ALU.add)
                dve.wait_ge(oT_ps, it + 1)
                dve.wait_ge(sinv_ready, it + 1)
                dve.tensor_tensor(OT[:, :], bank(6), qT[:, :], ALU.mult)\
                    .then_inc(oT_ready, 1)
                dve.wait_ge(proj_ps, it + 1)

                def add_attention(seq):
                    dve.tensor_tensor(half_of(Y, seq), half_of(NHAT, seq), half_of(tiles(1), seq), ALU.add)
                    dve.drain()

                layer_norm(it, 4, add_attention, Y, X, layer_done)

            def cross_attention(it, more_groups=True):
                def context_values(j, u, b, seq):
                    dve.wait_ge(vx_ps, it * (2 * PAIRS) + 2 * j + seq + 1)
                    dve.tensor_tensor(Vx[u][:, seq * KT:(seq + 1) * KT, :], tiles(b),
                                      xbv_bc[:, bass.ds(j, 1), :].to_broadcast([P, KT, D]), ALU.add).then_inc(vx_ready, 1)

                def row_max(j, s):
                    dve.wait_ge(c_ps, it * (NS * PAIRS) + j * NS + s + 1)
                    dve.tensor_reduce(nmax[:, s:s + 1], bank(s % 2), AX.X, ALU.max, negate=True)\
                        .then_inc(c_max, 1)

                def turned(j, s):
                    dve.wait_ge(cT_ps, it * (NS * PAIRS) + j * NS + s + 1)
                    dve.tensor_copy(cprobT[:, s % 4, :], bank(2)).then_inc(cT_even, 1)

                def normalise(j, u):
                    dve.wait_ge(o_ps, it * PAIRS + j + 1)
                    dve.wait_ge(inv_ready, it * PAIRS + j + 1)
                    dve.tensor_tensor(CTs[:, :], bank(4 + u), Rs[:, :], ALU.mult).then_inc(context_ready, 1)

                def add_projected(j, b):
                    dve.wait_ge(wo_ps, it * PAIRS + j + 1)
                    dve.tensor_tensor(X1[:, :, :], X1[:, :, :], tiles(b), ALU.add).then_inc(wo_added, 1)

                def pair(j, u, first=False, more=True):
                    for s in range(NS):
                        if s % 2 == 0:
                            turned(j, s)
                        if s == 2 and not first:
                            normalise(j - 1, 1 - u)
                        if s == 4 and not first:
                            add_projected(j - 1, 6)
                        if s == 6 and more:
                            context_values(j + 1, 1 - u, 6, 0)
                        if s == 7 and more:
                            context_values(j + 1, 1 - u, 7, 1)
                        if s + 2 < NS:
                            row_max(j, s + 2)
                        elif more:
                            row_max(j + 1, s + 2 - NS)
                        if more_groups and not more:
                            if s == 0:
                                rec_first_moments(it + 1)
                            if s == 1:
                                rec_first_normalised(it + 1)
                            if s == 4:
                                rec_key_mix(it + 1)
                            if s == 5:
                                rec_value_mix()
                    dve.wait_ge(c_exp, it * (NS * PAIRS) + (j + 1) * NS)
                    dve.reciprocal(rinv[:, :], rsum[:, u, :])
                    dve.drain()
                    dve.tensor_copy(O[:, :, :].rearrange("p t (h d) -> p (t h) d", h=2),
                                    rinv[:, :].unsqueeze(2).to_broadcast([P, NS, DK])).then_inc(rinv_ready, 1)

                dve.drain()
                dve.tensor_copy(X1[:, :, :], X[:, :, :]).then_inc(wo_added, 1)
                context_values(0, 0, 4, 0)
                context_values(0, 0, 5, 1)
                row_max(0, 0)
                row_max(0, 1)
                pair(0, 0, first=True)
                with dve.Fori(0, PAIRS // 2 - 1) as jj:
                    pair(2 * jj + 1, 1)
                    pair(2 * jj + 2, 0)
                pair(PAIRS - 1, 1, more=False)
                normalise(PAIRS - 1, 1)
                dve.wait_ge(wo_ps, it * PAIRS + PAIRS)

                def add_last(seq):
                    last = dve.tensor_tensor(half_of(X1, seq), half_of(X1, seq), half_of(tiles(3), seq), ALU.add)
                    if seq == GROUP - 1:
                        last.then_inc(wo_added, 1)
                    dve.drain()

                layer_norm(it, 5, add_last, X1, X, layer_done)

            def mixture_top2(it, more=True):
                if more:
                    rec_exponents(it + 1)
                dve.wait_ge(r1_ps, it + 1)
                dve.tensor_tensor(lg[:, :, :], ps[:, 1, 0:TT * E].rearrange("p (t e) -> p t e", t=TT),
                                  br_bc[:, :].unsqueeze(1).to_broadcast([P, TT, E]), ALU.add)
                dve.drain()
                for t in range(TT):
                    dve.max(top[:, t, :], lg[:, t, :])
                dve.drain()
                dve.tensor_tensor(ex1[:, :, :], lg[:, :, :], top[:, :, 0:1].to_broadcast([P, TT, E]), ALU.subtract)\
                    .then_inc(e1_arg, 1)
                for t in range(TT):
                    dve.max_index(topi[:, t, :], top[:, t, :], lg[:, t, :])
                dve.drain()
                dve.tensor_copy(topf[:, :, :], topi[:, :, 0:2])
                dve.drain()
                for t in range(TT):
                    dve.tensor_scalar(A[:, t, :], iota_e[:, 0:E], topf[:, t, 0:1], None, ALU.is_equal)
                    dve.tensor_scalar(onehot[:, t, 0:E], iota_e[:, 0:E], topf[:, t, 1:2], None, ALU.is_equal)
                dve.drain()
                dve.tensor_tensor(A[:, :, :], A[:, :, :], onehot[:, :, 0:E], ALU.add)
                dve.drain()
                dve.tensor_copy(A_bf[:, :, :], A[:, :, :]).then_inc(two_hot, 1)
                dve.wait_ge(e1_exp, it + 1)
                dve.tensor_reduce(esum[:, :], ex1[:, :, :], AX.X, ALU.add)
                dve.drain()
                dve.reciprocal(einv[:, :], esum[:, :])
                dve.drain()
                dve.tensor_tensor(ex1[:, :, :], ex1[:, :, :], einv[:, :].unsqueeze(2).to_broadcast([P, TT, E]), ALU.mult)
                dve.wait_ge(pos_ps, it + 1)
                dve.scalar_tensor_tensor(out=posA[:, :, :], in0=ps[:, 2, 0:TT * E].rearrange("p (t e) -> p t e", t=TT),
                                         scalar=1.0, in1=A[:, :, :], op0=ALU.add, op1=ALU.mult)
                dve.drain()

                def slots(m, t):
                    return m[:, t, :].rearrange("p (e c) -> p e c", e=E)

                def per_expert(m, t):
                    return m[:, t, :].unsqueeze(2).to_broadcast([P, E, CAP])

                for t in range(TT):
                    last = dve.tensor_tensor(slots(disp, t), iota_c[:, :].unsqueeze(1).to_broadcast([P, E, CAP]),
                                             per_expert(posA, t), ALU.is_equal)
                last.then_inc(disp_ready, 1)
                dve.drain()
                for t in range(TT):
                    last = dve.tensor_tensor(slots(comb, t), slots(disp, t), per_expert(ex1, t), ALU.mult)
                last.then_inc(comb_ready, 1)
                def add_mixture():
                    dve.wait_ge(comb_ps, it + 1)
                    dve.tensor_tensor(Y[:, :, :], X[:, :, :], tiles(4), ALU.add)
                    dve.drain()

                def added(seq):
                    pass

                if more:
                    rec_wkv(it + 1)
                    rec_second_norm(it + 1)
                    rec_feed_mix(it + 1)
                    rec_feed(it + 1, add_mixture)
                else:
                    add_mixture()
                layer_norm(it, 6, added, Y, Y, out_ready)

            def group(it, more=True):
                memory(it)
                mixture_top1(it)
                sparse_attention(it)
                cross_attention(it, more)
                mixture_top2(it, more)

            recurrent(0)
            with dve.Fori(0, ITERS - 1) as it:
                group(it)
            group(ITERS - 1, more=False)


_INS = [
    'x', 'ctx_1024', 'L0_attn_ln_att_g', 'L0_attn_ln_att_b', 'L0_attn_ln_ffn_g', 'L0_attn_ln_ffn_b',
    'L0_attn_att_time_decay', 'L0_attn_att_time_first', 'L0_attn_att_mix_k', 'L0_attn_att_mix_v',
    'L0_attn_att_mix_r', 'L0_attn_att_wk', 'L0_attn_att_wv', 'L0_attn_att_wr', 'L0_attn_att_wo',
    'L0_attn_ffn_mix_k', 'L0_attn_ffn_mix_r', 'L0_attn_ffn_wk', 'L0_attn_ffn_wv', 'L0_attn_ffn_wr',
    'L0_xattn_q_w', 'L0_xattn_k_w', 'L0_xattn_norm_w', 'L0_xattn_gate_w', 'L0_xattn_gate_b',
    'L0_ffn_Wr', 'L0_ffn_W1', 'L0_ffn_b1', 'L0_ffn_Wo', 'L0_ffn_bo', 'L0_ffn_gamma', 'L0_ffn_beta',
    'L1_attn_W_attn', 'L1_attn_b_attn', 'L1_attn_W_proj', 'L1_attn_b_proj',
    'L1_xattn_Wq', 'L1_xattn_bq', 'L1_xattn_Wk', 'L1_xattn_bk', 'L1_xattn_Wv', 'L1_xattn_bv', 'L1_xattn_Wo',
    'L1_ffn_Wr', 'L1_ffn_br', 'L1_ffn_W1', 'L1_ffn_b1', 'L1_ffn_W2', 'L1_ffn_b2',
]


def kernel(**inputs):
    import numpy as _np
    import concourse.bacc as _bacc
    from concourse import mybir as _mybir
    from concourse.bass_utils import run_bass_kernel_spmd as _run

    nc = _bacc.Bacc("TRN2", target_bir_lowering=False, num_devices=1)
    arrays, args = {}, []
    for name in _INS:
        a = _np.ascontiguousarray(inputs[name])
        arrays[f"in_{name}_dram"] = a
        args.append(nc.dram_tensor(f"in_{name}_dram", a.shape, _mybir.dt.from_np(a.dtype), kind="ExternalInput").ap())
    out = nc.dram_tensor("out_0_dram", (BATCH, SEQ, D), F32, kind="ExternalOutput").ap()
    decoder_kernel(nc, *args, out)
    r = _run(nc, [arrays], core_ids=[0])
    return r.results[0]["out_0_dram"]
```
